# Optimizing a Trainium2 kernel written in Bass

```python
import numpy as np
import jax
import jax.numpy as jnp

def _softmax(x, axis=-1):
    return jax.nn.softmax(x, axis=axis)

def _gelu(x):
    return jax.nn.gelu(x, approximate=True)

def _silu(x):
    return jax.nn.silu(x)

def _sigmoid(x):
    return jax.nn.sigmoid(x)

def _layernorm(x, axis=-1, eps=1e-05):
    m = jnp.mean(x, axis=axis, keepdims=True)
    v = jnp.var(x, axis=axis, keepdims=True)
    return (x - m) / jnp.sqrt(v + eps)

def _scatter_add(tgt, idx, src, axis=0):
    return tgt.at[idx].add(src)

def _segment_sum(src, seg, n):
    return jax.ops.segment_sum(src, seg, n)
kernel_name = 'mk_seq_postln_d2_jaxref_r8_551b4a'

def setup_inputs(seed: int=0):
    np.random.seed(seed)
    _w = jnp.asarray

    def _L0_attn_setup():
        import jax, jax.numpy as jnp
        import numpy as np
        from math import sqrt
        N_HEAD = 16
        W_SCALE = 0.02

        def _reference_tuple_inner(x, W_dq, W_uq, W_dkv, W_uk, W_uv, W_o):
            B, T, C = x.shape
            nh = N_HEAD
            hs = C // nh
            n_kvl = W_dkv.shape[0]
            k_eff = (W_dq.T @ W_uq.T @ W_uk).reshape(nh, hs, n_kvl)
            v_eff = jnp.transpose((W_uv.T @ W_o.T).reshape(n_kvl, nh, hs), (1, 0, 2))
            c_kv = x @ W_dkv.T
            q = x @ W_dq.T @ W_uq.T
            q = q.reshape(B, T, nh, hs)
            q_lat = jnp.einsum('bqhd,hdl->bhql', q, k_eff)
            attn = jnp.einsum('bhql,bkl->bhqk', q_lat, c_kv) / sqrt(hs)
            causal = jnp.tril(jnp.ones((T, T), dtype=bool))
            attn = jnp.where(causal[None, None], attn, -jnp.inf)
            attn = jax.nn.softmax(attn, axis=-1)
            y_lat = jnp.einsum('bhqk,bkl->bhql', attn, c_kv)
            y = jnp.einsum('bhql,hld->bqhd', y_lat, v_eff).reshape(B, T, C)
            return (y, c_kv)
        key = jax.random.key(seed)
        ks = jax.random.split(key, 7)
        B, T, C = (2, 256, 128)
        QL, KVL = (64, 64)
        return {'x': jax.random.normal(ks[0], (B, T, C), dtype=jnp.float32), 'W_dq': jax.random.normal(ks[1], (QL, C), dtype=jnp.float32) * W_SCALE, 'W_uq': jax.random.normal(ks[2], (C, QL), dtype=jnp.float32) * W_SCALE, 'W_dkv': jax.random.normal(ks[3], (KVL, C), dtype=jnp.float32) * W_SCALE, 'W_uk': jax.random.normal(ks[4], (C, KVL), dtype=jnp.float32) * W_SCALE, 'W_uv': jax.random.normal(ks[5], (C, KVL), dtype=jnp.float32) * W_SCALE, 'W_o': jax.random.normal(ks[6], (C, C), dtype=jnp.float32) * W_SCALE}
    _L0_attn_in = _L0_attn_setup()

    def _L0_ffn_setup():
        import jax, jax.numpy as jnp
        import numpy as np
        DIM = 128
        DEPTH = 6
        HEADS = 16
        DIM_HEAD = 64
        WINDOW = 32
        INNER = HEADS * DIM_HEAD
        DIM_INNER = int(DIM * 4 * 2 / 3)
        QK_SCALE = 8.0

        def shift_tokens(t):
            a, s = jnp.split(t, 2, -1)
            s = jnp.pad(s, ((0, 0), (1, 0), (0, 0)))[:, :-1]
            return jnp.concatenate([a, s], -1)

        def l2norm(t):
            return t / jnp.maximum(jnp.linalg.norm(t, axis=-1, keepdims=True), 1e-12)

        def rotate_half(x):
            x1, x2 = jnp.split(x, 2, -1)
            return jnp.concatenate([-x2, x1], -1)

        def rotary_tables(n):
            half = jnp.arange(0, DIM_HEAD, 2, dtype=jnp.float32)
            inv_freq = 1.0 / 10000.0 ** (half / DIM_HEAD)
            t = jnp.arange(n, dtype=jnp.float32)
            freqs = t[:, None] * inv_freq[None, :]
            freqs = jnp.concatenate([freqs, freqs], -1)
            base_scale = (half + 0.4 * DIM_HEAD) / (1.4 * DIM_HEAD)
            power = (t - n // 2) / (WINDOW // 2)
            scale = base_scale[None, :] ** power[:, None]
            scale = jnp.concatenate([scale, scale], -1)
            return (freqs, scale)

        def local_attention(q, k, v):
            b, h, n, d = q.shape
            w = WINDOW
            nw = n // w
            bq = q.reshape(b, h, nw, w, d)
            bk = k.reshape(b, h, nw, w, d)
            bv = v.reshape(b, h, nw, w, d)

            def look(t):
                p = jnp.pad(t, ((0, 0), (0, 0), (1, 0), (0, 0), (0, 0)))
                return jnp.concatenate([p[:, :, :nw], p[:, :, 1:]], axis=3)
            bk2, bv2 = (look(bk), look(bv))
            seq = jnp.arange(n).reshape(nw, w)
            seq_p = jnp.pad(seq, ((1, 0), (0, 0)), constant_values=-1)
            jt = jnp.concatenate([seq_p[:nw], seq_p[1:]], axis=1)
            it = seq[:, :, None]
            jb = jt[:, None, :]
            mask = (it < jb) | (it > jb + w) | (jb == -1)
            sim = jnp.einsum('bhwie,bhwje->bhwij', bq, bk2) * QK_SCALE
            sim = jnp.where(mask, -jnp.finfo(sim.dtype).max, sim)
            attn = jax.nn.softmax(sim, -1)
            out = jnp.einsum('bhwij,bhwje->bhwie', attn, bv2)
            return out.reshape(b, h, n, d)

        def attn_layer(x, Wqkv, qs, ksc, Wo):
            b, n, _ = x.shape
            qkv = x @ Wqkv
            q, k, v = jnp.split(qkv, 3, -1)
            sh = lambda t: t.reshape(b, n, HEADS, DIM_HEAD).transpose(0, 2, 1, 3)
            q, k, v = (sh(q), sh(k), sh(v))
            q = l2norm(q) * qs
            k = l2norm(k) * ksc
            freqs, scale = rotary_tables(n)
            cos, sin = (jnp.cos(freqs), jnp.sin(freqs))
            q = q * cos * scale + rotate_half(q) * sin * scale
            inv = 1.0 / scale
            k = k * cos * inv + rotate_half(k) * sin * inv
            out = local_attention(q, k, v)
            out = out.transpose(0, 2, 1, 3).reshape(b, n, INNER)
            return out @ Wo

        def ffn_layer(x, g, bln, W1, b1, W2, b2):
            mu = x.mean(-1, keepdims=True)
            var = ((x - mu) ** 2).mean(-1, keepdims=True)
            xn = (x - mu) / jnp.sqrt(var + 1e-05) * g + bln
            hg = xn @ W1 + b1
            a, gate = jnp.split(hg, 2, -1)
            return a * jax.nn.gelu(gate, approximate=False) @ W2 + b2
        key = jax.random.key(seed)
        ks = jax.random.split(key, 8)
        B, N = (2, 256)
        init = lambda k, shape: jax.random.normal(k, shape, jnp.float32) * 0.02
        return {'x': jax.random.normal(ks[0], (B, N, DIM), jnp.float32), 'Wqkv': init(ks[1], (DEPTH, DIM, 3 * INNER)), 'q_scale': jnp.ones((DEPTH, DIM_HEAD), jnp.float32), 'k_scale': jnp.ones((DEPTH, DIM_HEAD), jnp.float32), 'Wo': init(ks[2], (DEPTH, INNER, DIM)), 'ln_g': jnp.ones((DEPTH, DIM), jnp.float32), 'ln_b': jnp.zeros((DEPTH, DIM), jnp.float32), 'W1': init(ks[3], (DEPTH, DIM, 2 * DIM_INNER)), 'b1': jnp.zeros((DEPTH, 2 * DIM_INNER), jnp.float32), 'W2': init(ks[4], (DEPTH, DIM_INNER, DIM)), 'b2': jnp.zeros((DEPTH, DIM), jnp.float32)}
    _L0_ffn_in = _L0_ffn_setup()

    def _L1_attn_setup():
        import jax, jax.numpy as jnp
        import numpy as np
        import math
        D = 128
        H = 4
        HD = D // H
        DI = int(HD * 1.5)
        FF_INNER = int(D * 4 * 2 / 3)
        K = 4
        RES_SCALE = 1.0

        def _rmsnorm(x, gamma):
            n = jnp.sqrt(jnp.sum(x * x, axis=-1, keepdims=True))
            return x / jnp.maximum(n, 1e-12) * math.sqrt(x.shape[-1]) * (gamma + 1.0)

        def _log_g(x):
            return jnp.where(x >= 0, jnp.log(jax.nn.relu(x) + 0.5), -jax.nn.softplus(-x))

        def _causal_conv(x, dw_w, dw_b, pw_w, pw_b):
            xt = jnp.transpose(x, (0, 2, 1))
            xt = jnp.pad(xt, ((0, 0), (0, 0), (K - 1, 0)))
            y = jax.lax.conv_general_dilated(xt, dw_w, (1,), 'VALID', dimension_numbers=('NCH', 'OIH', 'NCH'), feature_group_count=D) + dw_b[None, :, None]
            y = jnp.einsum('bdl,ed->bel', y, pw_w) + pw_b[None, :, None]
            return jnp.transpose(y, (0, 2, 1))

        def _reference_tuple_inner(x, dw_w, dw_b, pw_w, pw_b, conv_gamma, gru_gamma, ff_gamma, w_hg, w_out, w_gate, w_value, w_ff_out):
            B, L, _ = x.shape
            x = _causal_conv(_rmsnorm(x, conv_gamma), dw_w, dw_b, pw_w, pw_b) * RES_SCALE + x
            normed = _rmsnorm(x, gru_gamma).reshape(B, L, H, HD)
            hg = jnp.einsum('blhd,hde->blhe', normed, w_hg)
            hidden, gate = (hg[..., :DI], hg[..., DI:])
            log_coeffs = -jax.nn.softplus(gate)
            log_values = -jax.nn.softplus(-gate) + _log_g(hidden)
            a_star = jnp.cumsum(log_coeffs, axis=1)
            log_h = a_star + jax.lax.cumlogsumexp(log_values - a_star, axis=1)
            h = jnp.exp(log_h)
            next_hidden = h[:, -1:].reshape(B, 1, H * DI)
            gru_out = jnp.einsum('blhe,heo->blho', h, w_out).reshape(B, L, D)
            x = gru_out * RES_SCALE + x
            n = _rmsnorm(x, ff_gamma)
            ff = jax.nn.silu(n @ w_gate) * (n @ w_value) @ w_ff_out
            x = ff * RES_SCALE + x
            return (x, next_hidden)
        key = jax.random.key(seed)
        ks = jax.random.split(key, 12)
        s = lambda k, shape, sc: jax.random.normal(k, shape, jnp.float32) * sc
        return {'x': s(ks[0], (4, 512, D), 1.0), 'dw_w': s(ks[1], (D, 1, K), 0.3), 'dw_b': jnp.zeros((D,), jnp.float32), 'pw_w': s(ks[2], (D, D), 1.0 / math.sqrt(D)), 'pw_b': jnp.zeros((D,), jnp.float32), 'conv_gamma': jnp.zeros((D,), jnp.float32), 'gru_gamma': jnp.zeros((D,), jnp.float32), 'ff_gamma': jnp.zeros((D,), jnp.float32), 'w_hg': s(ks[3], (H, HD, 2 * DI), 1.0 / math.sqrt(HD)), 'w_out': s(ks[4], (H, DI, HD), 1.0 / math.sqrt(DI)), 'w_gate': s(ks[5], (D, FF_INNER), 1.0 / math.sqrt(D)), 'w_value': s(ks[6], (D, FF_INNER), 1.0 / math.sqrt(D)), 'w_ff_out': s(ks[7], (FF_INNER, D), 1.0 / math.sqrt(FF_INNER))}
    _L1_attn_in = _L1_attn_setup()

    def _L1_ffn_setup():
        import jax, jax.numpy as jnp
        import numpy as np
        DIM = 128
        DEPTH = 2
        HEADS = 8
        DIM_HEAD = 64
        WINDOW = 64
        INNER = HEADS * DIM_HEAD
        HID = int(DIM * 4 * 2 / 3)
        B, N = (2, 1024)
        QK_SCALE = 8.0

        def shift_token(t):
            t1, t2 = jnp.split(t, 2, axis=-1)
            t2 = jnp.pad(t2, ((0, 0), (1, 0), (0, 0)))[:, :-1]
            return jnp.concatenate([t1, t2], axis=-1)

        def l2norm(t):
            return t / jnp.clip(jnp.linalg.norm(t, axis=-1, keepdims=True), 1e-12)

        def rotate_half(x):
            x1, x2 = jnp.split(x, 2, axis=-1)
            return jnp.concatenate([-x2, x1], axis=-1)

        def rotary_xpos(q, k):
            n = q.shape[-2]
            half_idx = jnp.arange(0, DIM_HEAD, 2, dtype=jnp.float32)
            inv_freq = 1.0 / 10000.0 ** (half_idx / DIM_HEAD)
            t = jnp.arange(n, dtype=jnp.float32)
            freqs = t[:, None] * inv_freq[None, :]
            freqs = jnp.concatenate([freqs, freqs], axis=-1)
            base = (half_idx + 0.4 * DIM_HEAD) / (1.4 * DIM_HEAD)
            power = (t - n // 2) / float(WINDOW // 2)
            scale = base[None, :] ** power[:, None]
            scale = jnp.concatenate([scale, scale], axis=-1)
            cos, sin = (jnp.cos(freqs), jnp.sin(freqs))
            q = q * cos * scale + rotate_half(q) * sin * scale
            k = k * cos / scale + rotate_half(k) * sin / scale
            return (q, k)

        def local_attention(q, k, v):
            b, h, n, d = q.shape
            w = n // WINDOW
            bq = q.reshape(b, h, w, WINDOW, d) * QK_SCALE
            bk = k.reshape(b, h, w, WINDOW, d)
            bv = v.reshape(b, h, w, WINDOW, d)

            def look_around(t):
                p = jnp.pad(t, ((0, 0), (0, 0), (1, 0), (0, 0), (0, 0)))
                return jnp.concatenate([p[:, :, :w], p[:, :, 1:]], axis=3)
            bk, bv = (look_around(bk), look_around(bv))
            bt = jnp.arange(n).reshape(w, WINDOW)
            btp = jnp.pad(bt, ((1, 0), (0, 0)), constant_values=-1)
            btk = jnp.concatenate([btp[:w], btp[1:]], axis=1)
            sim = jnp.einsum('bhwid,bhwjd->bhwij', bq, bk)
            i = bt[:, :, None]
            j = btk[:, None, :]
            mask = (i < j) | (i > j + WINDOW) | (j == -1)
            sim = jnp.where(mask, -jnp.finfo(sim.dtype).max, sim)
            attn = jax.nn.softmax(sim, axis=-1)
            out = jnp.einsum('bhwij,bhwjd->bhwid', attn, bv)
            return out.reshape(b, h, n, d)

        def _layer(x, wqkv, qs, ksc, wo, lg, lb, w1, b1, w2, b2):
            b, n, _ = x.shape
            h = shift_token(x)
            qkv = h @ wqkv
            q, k, v = jnp.split(qkv, 3, axis=-1)
            to_heads = lambda t: t.reshape(b, n, HEADS, DIM_HEAD).transpose(0, 2, 1, 3)
            q, k, v = (to_heads(q), to_heads(k), to_heads(v))
            q = l2norm(q) * qs
            k = l2norm(k) * ksc
            q, k = rotary_xpos(q, k)
            o = local_attention(q, k, v)
            o = o.transpose(0, 2, 1, 3).reshape(b, n, INNER)
            x = x + o @ wo
            h = shift_token(x)
            mu = h.mean(-1, keepdims=True)
            var = h.var(-1, keepdims=True)
            h = (h - mu) / jnp.sqrt(var + 1e-05) * lg + lb
            h = h @ w1 + b1
            a, g = jnp.split(h, 2, axis=-1)
            h = a * jax.nn.gelu(g, approximate=False)
            x = x + h @ w2 + b2
            return x
        key = jax.random.key(seed)
        ks = jax.random.split(key, 6)
        return {'x': jax.random.normal(ks[0], (B, N, DIM), jnp.float32), 'wqkv': jax.random.normal(ks[1], (DEPTH, DIM, 3 * INNER), jnp.float32) * 0.02, 'q_scale': jnp.ones((DEPTH, DIM_HEAD), jnp.float32), 'k_scale': jnp.ones((DEPTH, DIM_HEAD), jnp.float32), 'wo': jax.random.normal(ks[2], (DEPTH, INNER, DIM), jnp.float32) * 0.02, 'ln_g': jnp.ones((DEPTH, DIM), jnp.float32), 'ln_b': jnp.zeros((DEPTH, DIM), jnp.float32), 'w1': jax.random.normal(ks[3], (DEPTH, DIM, 2 * HID), jnp.float32) * 0.02, 'b1': jnp.zeros((DEPTH, 2 * HID), jnp.float32), 'w2': jax.random.normal(ks[4], (DEPTH, HID, DIM), jnp.float32) * 0.02, 'b2': jnp.zeros((DEPTH, DIM), jnp.float32)}
    _L1_ffn_in = _L1_ffn_setup()
    _d = {'L0_attn_x': _L0_attn_in['x'], 'L0_attn_W_dq': _L0_attn_in['W_dq'], 'L0_attn_W_uq': _L0_attn_in['W_uq'], 'L0_attn_W_dkv': _L0_attn_in['W_dkv'], 'L0_attn_W_uk': _L0_attn_in['W_uk'], 'L0_attn_W_uv': _L0_attn_in['W_uv'], 'L0_attn_W_o': _L0_attn_in['W_o'], 'L0_ffn_Wqkv': _L0_ffn_in['Wqkv'], 'L0_ffn_q_scale': _L0_ffn_in['q_scale'], 'L0_ffn_k_scale': _L0_ffn_in['k_scale'], 'L0_ffn_Wo': _L0_ffn_in['Wo'], 'L0_ffn_ln_g': _L0_ffn_in['ln_g'], 'L0_ffn_ln_b': _L0_ffn_in['ln_b'], 'L0_ffn_W1': _L0_ffn_in['W1'], 'L0_ffn_b1': _L0_ffn_in['b1'], 'L0_ffn_W2': _L0_ffn_in['W2'], 'L0_ffn_b2': _L0_ffn_in['b2'], 'L1_attn_dw_w': _L1_attn_in['dw_w'], 'L1_attn_dw_b': _L1_attn_in['dw_b'], 'L1_attn_pw_w': _L1_attn_in['pw_w'], 'L1_attn_pw_b': _L1_attn_in['pw_b'], 'L1_attn_conv_gamma': _L1_attn_in['conv_gamma'], 'L1_attn_gru_gamma': _L1_attn_in['gru_gamma'], 'L1_attn_ff_gamma': _L1_attn_in['ff_gamma'], 'L1_attn_w_hg': _L1_attn_in['w_hg'], 'L1_attn_w_out': _L1_attn_in['w_out'], 'L1_attn_w_gate': _L1_attn_in['w_gate'], 'L1_attn_w_value': _L1_attn_in['w_value'], 'L1_attn_w_ff_out': _L1_attn_in['w_ff_out'], 'L1_ffn_wqkv': _L1_ffn_in['wqkv'], 'L1_ffn_q_scale': _L1_ffn_in['q_scale'], 'L1_ffn_k_scale': _L1_ffn_in['k_scale'], 'L1_ffn_wo': _L1_ffn_in['wo'], 'L1_ffn_ln_g': _L1_ffn_in['ln_g'], 'L1_ffn_ln_b': _L1_ffn_in['ln_b'], 'L1_ffn_w1': _L1_ffn_in['w1'], 'L1_ffn_b1': _L1_ffn_in['b1'], 'L1_ffn_w2': _L1_ffn_in['w2'], 'L1_ffn_b2': _L1_ffn_in['b2']}
    _x0 = _d['L0_attn_x']
    _d['L0_attn_x'] = jax.random.normal(jax.random.fold_in(jax.random.key(seed), 1), (4, 1024, 128), dtype=_x0.dtype)
    del _x0
    return _d

def reference(L0_attn_x, L0_attn_W_dq, L0_attn_W_uq, L0_attn_W_dkv, L0_attn_W_uk, L0_attn_W_uv, L0_attn_W_o, L0_ffn_Wqkv, L0_ffn_q_scale, L0_ffn_k_scale, L0_ffn_Wo, L0_ffn_ln_g, L0_ffn_ln_b, L0_ffn_W1, L0_ffn_b1, L0_ffn_W2, L0_ffn_b2, L1_attn_dw_w, L1_attn_dw_b, L1_attn_pw_w, L1_attn_pw_b, L1_attn_conv_gamma, L1_attn_gru_gamma, L1_attn_ff_gamma, L1_attn_w_hg, L1_attn_w_out, L1_attn_w_gate, L1_attn_w_value, L1_attn_w_ff_out, L1_ffn_wqkv, L1_ffn_q_scale, L1_ffn_k_scale, L1_ffn_wo, L1_ffn_ln_g, L1_ffn_ln_b, L1_ffn_w1, L1_ffn_b1, L1_ffn_w2, L1_ffn_b2):

    def _L0_attn_ref(x, W_dq, W_uq, W_dkv, W_uk, W_uv, W_o):
        import jax, jax.numpy as jnp
        import numpy as np
        from math import sqrt
        N_HEAD = 16
        W_SCALE = 0.02

        def _reference_tuple_inner(x, W_dq, W_uq, W_dkv, W_uk, W_uv, W_o):
            B, T, C = x.shape
            nh = N_HEAD
            hs = C // nh
            n_kvl = W_dkv.shape[0]
            k_eff = (W_dq.T @ W_uq.T @ W_uk).reshape(nh, hs, n_kvl)
            v_eff = jnp.transpose((W_uv.T @ W_o.T).reshape(n_kvl, nh, hs), (1, 0, 2))
            c_kv = x @ W_dkv.T
            q = x @ W_dq.T @ W_uq.T
            q = q.reshape(B, T, nh, hs)
            q_lat = jnp.einsum('bqhd,hdl->bhql', q, k_eff)
            attn = jnp.einsum('bhql,bkl->bhqk', q_lat, c_kv) / sqrt(hs)
            causal = jnp.tril(jnp.ones((T, T), dtype=bool))
            attn = jnp.where(causal[None, None], attn, -jnp.inf)
            attn = jax.nn.softmax(attn, axis=-1)
            y_lat = jnp.einsum('bhqk,bkl->bhql', attn, c_kv)
            y = jnp.einsum('bhql,hld->bqhd', y_lat, v_eff).reshape(B, T, C)
            return (y, c_kv)
        return _reference_tuple_inner(x, W_dq, W_uq, W_dkv, W_uk, W_uv, W_o)[0]

    def _L0_ffn_ref(x, Wqkv, q_scale, k_scale, Wo, ln_g, ln_b, W1, b1, W2, b2):
        import jax, jax.numpy as jnp
        import numpy as np
        DIM = 128
        DEPTH = 6
        HEADS = 16
        DIM_HEAD = 64
        WINDOW = 32
        INNER = HEADS * DIM_HEAD
        DIM_INNER = int(DIM * 4 * 2 / 3)
        QK_SCALE = 8.0

        def shift_tokens(t):
            a, s = jnp.split(t, 2, -1)
            s = jnp.pad(s, ((0, 0), (1, 0), (0, 0)))[:, :-1]
            return jnp.concatenate([a, s], -1)

        def l2norm(t):
            return t / jnp.maximum(jnp.linalg.norm(t, axis=-1, keepdims=True), 1e-12)

        def rotate_half(x):
            x1, x2 = jnp.split(x, 2, -1)
            return jnp.concatenate([-x2, x1], -1)

        def rotary_tables(n):
            half = jnp.arange(0, DIM_HEAD, 2, dtype=jnp.float32)
            inv_freq = 1.0 / 10000.0 ** (half / DIM_HEAD)
            t = jnp.arange(n, dtype=jnp.float32)
            freqs = t[:, None] * inv_freq[None, :]
            freqs = jnp.concatenate([freqs, freqs], -1)
            base_scale = (half + 0.4 * DIM_HEAD) / (1.4 * DIM_HEAD)
            power = (t - n // 2) / (WINDOW // 2)
            scale = base_scale[None, :] ** power[:, None]
            scale = jnp.concatenate([scale, scale], -1)
            return (freqs, scale)

        def local_attention(q, k, v):
            b, h, n, d = q.shape
            w = WINDOW
            nw = n // w
            bq = q.reshape(b, h, nw, w, d)
            bk = k.reshape(b, h, nw, w, d)
            bv = v.reshape(b, h, nw, w, d)

            def look(t):
                p = jnp.pad(t, ((0, 0), (0, 0), (1, 0), (0, 0), (0, 0)))
                return jnp.concatenate([p[:, :, :nw], p[:, :, 1:]], axis=3)
            bk2, bv2 = (look(bk), look(bv))
            seq = jnp.arange(n).reshape(nw, w)
            seq_p = jnp.pad(seq, ((1, 0), (0, 0)), constant_values=-1)
            jt = jnp.concatenate([seq_p[:nw], seq_p[1:]], axis=1)
            it = seq[:, :, None]
            jb = jt[:, None, :]
            mask = (it < jb) | (it > jb + w) | (jb == -1)
            sim = jnp.einsum('bhwie,bhwje->bhwij', bq, bk2) * QK_SCALE
            sim = jnp.where(mask, -jnp.finfo(sim.dtype).max, sim)
            attn = jax.nn.softmax(sim, -1)
            out = jnp.einsum('bhwij,bhwje->bhwie', attn, bv2)
            return out.reshape(b, h, n, d)

        def attn_layer(x, Wqkv, qs, ksc, Wo):
            b, n, _ = x.shape
            qkv = x @ Wqkv
            q, k, v = jnp.split(qkv, 3, -1)
            sh = lambda t: t.reshape(b, n, HEADS, DIM_HEAD).transpose(0, 2, 1, 3)
            q, k, v = (sh(q), sh(k), sh(v))
            q = l2norm(q) * qs
            k = l2norm(k) * ksc
            freqs, scale = rotary_tables(n)
            cos, sin = (jnp.cos(freqs), jnp.sin(freqs))
            q = q * cos * scale + rotate_half(q) * sin * scale
            inv = 1.0 / scale
            k = k * cos * inv + rotate_half(k) * sin * inv
            out = local_attention(q, k, v)
            out = out.transpose(0, 2, 1, 3).reshape(b, n, INNER)
            return out @ Wo

        def ffn_layer(x, g, bln, W1, b1, W2, b2):
            mu = x.mean(-1, keepdims=True)
            var = ((x - mu) ** 2).mean(-1, keepdims=True)
            xn = (x - mu) / jnp.sqrt(var + 1e-05) * g + bln
            hg = xn @ W1 + b1
            a, gate = jnp.split(hg, 2, -1)
            return a * jax.nn.gelu(gate, approximate=False) @ W2 + b2
        for i in range(DEPTH):
            x = attn_layer(shift_tokens(x), Wqkv[i], q_scale[i], k_scale[i], Wo[i]) + x
            x = ffn_layer(shift_tokens(x), ln_g[i], ln_b[i], W1[i], b1[i], W2[i], b2[i]) + x
        return x

    def _L1_attn_ref(x, dw_w, dw_b, pw_w, pw_b, conv_gamma, gru_gamma, ff_gamma, w_hg, w_out, w_gate, w_value, w_ff_out):
        import jax, jax.numpy as jnp
        import numpy as np
        import math
        D = 128
        H = 4
        HD = D // H
        DI = int(HD * 1.5)
        FF_INNER = int(D * 4 * 2 / 3)
        K = 4
        RES_SCALE = 1.0

        def _rmsnorm(x, gamma):
            n = jnp.sqrt(jnp.sum(x * x, axis=-1, keepdims=True))
            return x / jnp.maximum(n, 1e-12) * math.sqrt(x.shape[-1]) * (gamma + 1.0)

        def _log_g(x):
            return jnp.where(x >= 0, jnp.log(jax.nn.relu(x) + 0.5), -jax.nn.softplus(-x))

        def _causal_conv(x, dw_w, dw_b, pw_w, pw_b):
            xt = jnp.transpose(x, (0, 2, 1))
            xt = jnp.pad(xt, ((0, 0), (0, 0), (K - 1, 0)))
            y = jax.lax.conv_general_dilated(xt, dw_w, (1,), 'VALID', dimension_numbers=('NCH', 'OIH', 'NCH'), feature_group_count=D) + dw_b[None, :, None]
            y = jnp.einsum('bdl,ed->bel', y, pw_w) + pw_b[None, :, None]
            return jnp.transpose(y, (0, 2, 1))

        def _reference_tuple_inner(x, dw_w, dw_b, pw_w, pw_b, conv_gamma, gru_gamma, ff_gamma, w_hg, w_out, w_gate, w_value, w_ff_out):
            B, L, _ = x.shape
            x = _causal_conv(_rmsnorm(x, conv_gamma), dw_w, dw_b, pw_w, pw_b) * RES_SCALE + x
            normed = _rmsnorm(x, gru_gamma).reshape(B, L, H, HD)
            hg = jnp.einsum('blhd,hde->blhe', normed, w_hg)
            hidden, gate = (hg[..., :DI], hg[..., DI:])
            log_coeffs = -jax.nn.softplus(gate)
            log_values = -jax.nn.softplus(-gate) + _log_g(hidden)
            a_star = jnp.cumsum(log_coeffs, axis=1)
            log_h = a_star + jax.lax.cumlogsumexp(log_values - a_star, axis=1)
            h = jnp.exp(log_h)
            next_hidden = h[:, -1:].reshape(B, 1, H * DI)
            gru_out = jnp.einsum('blhe,heo->blho', h, w_out).reshape(B, L, D)
            x = gru_out * RES_SCALE + x
            n = _rmsnorm(x, ff_gamma)
            ff = jax.nn.silu(n @ w_gate) * (n @ w_value) @ w_ff_out
            x = ff * RES_SCALE + x
            return (x, next_hidden)
        return _reference_tuple_inner(x, dw_w, dw_b, pw_w, pw_b, conv_gamma, gru_gamma, ff_gamma, w_hg, w_out, w_gate, w_value, w_ff_out)[0]

    def _L1_ffn_ref(x, wqkv, q_scale, k_scale, wo, ln_g, ln_b, w1, b1, w2, b2):
        import jax, jax.numpy as jnp
        import numpy as np
        DIM = 128
        DEPTH = 2
        HEADS = 8
        DIM_HEAD = 64
        WINDOW = 64
        INNER = HEADS * DIM_HEAD
        HID = int(DIM * 4 * 2 / 3)
        B, N = (2, 1024)
        QK_SCALE = 8.0

        def shift_token(t):
            t1, t2 = jnp.split(t, 2, axis=-1)
            t2 = jnp.pad(t2, ((0, 0), (1, 0), (0, 0)))[:, :-1]
            return jnp.concatenate([t1, t2], axis=-1)

        def l2norm(t):
            return t / jnp.clip(jnp.linalg.norm(t, axis=-1, keepdims=True), 1e-12)

        def rotate_half(x):
            x1, x2 = jnp.split(x, 2, axis=-1)
            return jnp.concatenate([-x2, x1], axis=-1)

        def rotary_xpos(q, k):
            n = q.shape[-2]
            half_idx = jnp.arange(0, DIM_HEAD, 2, dtype=jnp.float32)
            inv_freq = 1.0 / 10000.0 ** (half_idx / DIM_HEAD)
            t = jnp.arange(n, dtype=jnp.float32)
            freqs = t[:, None] * inv_freq[None, :]
            freqs = jnp.concatenate([freqs, freqs], axis=-1)
            base = (half_idx + 0.4 * DIM_HEAD) / (1.4 * DIM_HEAD)
            power = (t - n // 2) / float(WINDOW // 2)
            scale = base[None, :] ** power[:, None]
            scale = jnp.concatenate([scale, scale], axis=-1)
            cos, sin = (jnp.cos(freqs), jnp.sin(freqs))
            q = q * cos * scale + rotate_half(q) * sin * scale
            k = k * cos / scale + rotate_half(k) * sin / scale
            return (q, k)

        def local_attention(q, k, v):
            b, h, n, d = q.shape
            w = n // WINDOW
            bq = q.reshape(b, h, w, WINDOW, d) * QK_SCALE
            bk = k.reshape(b, h, w, WINDOW, d)
            bv = v.reshape(b, h, w, WINDOW, d)

            def look_around(t):
                p = jnp.pad(t, ((0, 0), (0, 0), (1, 0), (0, 0), (0, 0)))
                return jnp.concatenate([p[:, :, :w], p[:, :, 1:]], axis=3)
            bk, bv = (look_around(bk), look_around(bv))
            bt = jnp.arange(n).reshape(w, WINDOW)
            btp = jnp.pad(bt, ((1, 0), (0, 0)), constant_values=-1)
            btk = jnp.concatenate([btp[:w], btp[1:]], axis=1)
            sim = jnp.einsum('bhwid,bhwjd->bhwij', bq, bk)
            i = bt[:, :, None]
            j = btk[:, None, :]
            mask = (i < j) | (i > j + WINDOW) | (j == -1)
            sim = jnp.where(mask, -jnp.finfo(sim.dtype).max, sim)
            attn = jax.nn.softmax(sim, axis=-1)
            out = jnp.einsum('bhwij,bhwjd->bhwid', attn, bv)
            return out.reshape(b, h, n, d)

        def _layer(x, wqkv, qs, ksc, wo, lg, lb, w1, b1, w2, b2):
            b, n, _ = x.shape
            h = shift_token(x)
            qkv = h @ wqkv
            q, k, v = jnp.split(qkv, 3, axis=-1)
            to_heads = lambda t: t.reshape(b, n, HEADS, DIM_HEAD).transpose(0, 2, 1, 3)
            q, k, v = (to_heads(q), to_heads(k), to_heads(v))
            q = l2norm(q) * qs
            k = l2norm(k) * ksc
            q, k = rotary_xpos(q, k)
            o = local_attention(q, k, v)
            o = o.transpose(0, 2, 1, 3).reshape(b, n, INNER)
            x = x + o @ wo
            h = shift_token(x)
            mu = h.mean(-1, keepdims=True)
            var = h.var(-1, keepdims=True)
            h = (h - mu) / jnp.sqrt(var + 1e-05) * lg + lb
            h = h @ w1 + b1
            a, g = jnp.split(h, 2, axis=-1)
            h = a * jax.nn.gelu(g, approximate=False)
            x = x + h @ w2 + b2
            return x
        for l in range(DEPTH):
            x = _layer(x, wqkv[l], q_scale[l], k_scale[l], wo[l], ln_g[l], ln_b[l], w1[l], b1[l], w2[l], b2[l])
        return x
    x = L0_attn_x
    x = _layernorm(x + _L0_attn_ref(x, L0_attn_W_dq, L0_attn_W_uq, L0_attn_W_dkv, L0_attn_W_uk, L0_attn_W_uv, L0_attn_W_o), axis=-1)
    x = _layernorm(x + _L0_ffn_ref(x, L0_ffn_Wqkv, L0_ffn_q_scale, L0_ffn_k_scale, L0_ffn_Wo, L0_ffn_ln_g, L0_ffn_ln_b, L0_ffn_W1, L0_ffn_b1, L0_ffn_W2, L0_ffn_b2), axis=-1)
    x = _layernorm(x + _L1_attn_ref(x, L1_attn_dw_w, L1_attn_dw_b, L1_attn_pw_w, L1_attn_pw_b, L1_attn_conv_gamma, L1_attn_gru_gamma, L1_attn_ff_gamma, L1_attn_w_hg, L1_attn_w_out, L1_attn_w_gate, L1_attn_w_value, L1_attn_w_ff_out), axis=-1)
    x = _layernorm(x + _L1_ffn_ref(x, L1_ffn_wqkv, L1_ffn_q_scale, L1_ffn_k_scale, L1_ffn_wo, L1_ffn_ln_g, L1_ffn_ln_b, L1_ffn_w1, L1_ffn_b1, L1_ffn_w2, L1_ffn_b2), axis=-1)
    return x

_drawn_inputs = setup_inputs


def setup_inputs(seed=0):
    import zlib

    import numpy as np

    out = dict(_drawn_inputs(seed))
    spreads = {'L0_ffn_q_scale': (1.0, 0.6),
     'L0_ffn_k_scale': (1.0, 0.6),
     'L0_ffn_ln_g': (1.0, 0.6),
     'L0_ffn_ln_b': (0.0, 0.8),
     'L0_ffn_b1': (0.0, 0.8),
     'L0_ffn_b2': (0.0, 0.1),
     'L1_attn_dw_b': (0.0, 0.1),
     'L1_attn_pw_b': (0.0, 0.1),
     'L1_attn_conv_gamma': (0.0, 0.1),
     'L1_attn_gru_gamma': (0.0, 0.333),
     'L1_attn_ff_gamma': (0.0, 0.1),
     'L1_ffn_q_scale': (1.0, 0.6),
     'L1_ffn_k_scale': (1.0, 0.6),
     'L1_ffn_ln_g': (1.0, 0.6),
     'L1_ffn_ln_b': (0.0, 0.8),
     'L1_ffn_b1': (0.0, 0.8),
     'L1_ffn_b2': (0.0, 0.66)}
    factors = {'L0_attn_W_dq': 8.0,
     'L0_attn_W_uq': 8.0,
     'L0_attn_W_dkv': 8.0,
     'L0_attn_W_uk': 8.0,
     'L0_attn_W_uv': 8.0,
     'L0_attn_W_o': 8.0,
     'L0_ffn_W1': 3.819,
     'L0_ffn_W2': 3.736,
     'L1_ffn_w1': 6.552,
     'L1_ffn_w2': 6.533}
    for name, (base, spread) in spreads.items():
        noise = np.random.default_rng([zlib.crc32(name.encode()), seed]).standard_normal(out[name].shape)
        drawn = base * np.exp(spread * noise) if base else spread * noise
        out[name] = jnp.asarray(drawn.astype(out[name].dtype))
    for name, factor in factors.items():
        out[name] = (out[name] * factor).astype(out[name].dtype)
    return out
```

```python
from contextlib import ExitStack

import numpy as np
import concourse.bass as bass
from concourse import mybir

F32 = mybir.dt.float32
BF16 = mybir.dt.bfloat16
ALU = mybir.AluOpType
ACT = mybir.ActivationFunctionType
AX_X = mybir.AxisListType.X
ds = bass.ds

P = 128
SEQS, SEQ = 4, 1024
TOK = SEQS * SEQ
TILES = SEQ // P
HALF = 512
X0 = P
PAD = 3 * P
HD = 64
GH = 8
GW = GH * HD
VW_ = HD + 1
SCRATCH = 10 * 1024
ARENA = 27 * 1024
LEAD = 4
MASKED = -1e30
HID = int(P * 4 * 2 / 3)
HC = [114, 114, 113]
HO = [0, 114, 228]
NORM_EPS = 1e-5
MLA_HEADS, MLA_HD, MLA_LAT = 16, 8, 64
DI = 48
CONV = 4
LOCAL = {"L0": dict(layers=6, groups=2, window=32), "L1": dict(layers=2, groups=1, window=64)}
AHEAD = 3
ROPE_TILES = TILES + AHEAD


def after(n):
    return n + 1 + LEAD


class Machine:

    def __init__(self, nc, ctx):
        self.nc, self.ctx = nc, ctx
        self.sems = []
        self.settled = self.sem("settled")
        sb = self.sb
        self.xa = sb("xa", [P, X0 + TOK + PAD])
        self.xb = sb("xb", [P, X0 + TOK])
        self.xres = sb("xres", [P, X0 + TOK])
        self.hn = sb("hn", [P, TOK + HALF])
        self.ident = sb("ident", [P, P])
        self.center = sb("center", [P, P])
        self.center_a = sb("center_a", [P, P])
        self.center_b = sb("center_b", [P, P])
        self.mean = sb("mean", [P, P])
        self.onehot = sb("onehot", [P, MLA_HEADS])
        self.ident_bf = sb("ident_bf", [P, P], BF16)
        self.arena = sb("arena", [P, ARENA])
        self.psum = ctx.enter_context(nc.psum_tensor("psum", [P, 8, HALF], F32))

    def sb(self, name, shape, dt=F32):
        return self.ctx.enter_context(self.nc.sbuf_tensor(name, shape, dt))

    def carve(self, at, shape):
        size = int(np.prod(shape[1:]))
        assert at + size <= ARENA
        ap = self.arena[0:shape[0], at:at + size]
        if len(shape) > 2:
            names = "abcd"[:len(shape) - 1]
            ap = ap.rearrange(f"p ({' '.join(names)}) -> p {' '.join(names)}", **dict(zip(names, shape[1:])))
        return ap, at + size

    def sem(self, name):
        s = self.ctx.enter_context(self.nc.semaphore(name))
        self.sems.append(s)
        return s

    def settle(self, eng):
        eng.sem_inc(self.settled, 1)

    def phase_end(self):
        nums = sorted(s.num for s in self.sems)
        self.nc.all_engine_barrier(sems_to_clear=range(nums[0], nums[-1] + 1))


class Norm:

    def __init__(self, m):
        self.m = m
        self.sq, at = m.carve(0, [P, 2, HALF])
        self.lnv, at = m.carve(at, [P, 2, HALF])
        self.y0, at = m.carve(at, [P, 2, HALF])
        self.t1, at = m.carve(at, [P, 2, HALF])
        self.t2, at = m.carve(at, [P, 2, HALF])
        self.t3, at = m.carve(at, [P, 2, HALF])
        self.un, at = m.carve(at, [P, 2, HALF])
        self.s_cen = m.sem("norm_centred")
        self.s_sq = m.sem("norm_squared")
        self.s_var = m.sem("norm_variance")
        self.s_floor = m.sem("norm_floored")
        self.s_ln = m.sem("norm_ln")
        self.s_y0 = m.sem("norm_guess")
        self.s_t1 = m.sem("norm_newton1")
        self.s_t2 = m.sem("norm_newton2")
        self.s_t3 = m.sem("norm_newton3")
        self.s_un = m.sem("norm_scaled")
        self.s_out = m.sem("norm_written")

    def phase(self, kind, terms=None, src=None, gain=None, bias=None, out=None, out_at=0, out2=None, sp_work=None):
        nc, m, s = self.m.nc, self.m, self
        cen, var = m.psum[:, 0:2, :], m.psum[:, 2:4, :]
        layer = kind == "layer"
        ln_scale = 2.0 ** 24
        floor = 1e-24 / P
        eps = NORM_EPS if layer else 0.0
        with nc.Block() as block:
            if sp_work:
                block.sync(sp_work)

            @block.tensor
            def _(pe):
                pe.sem_inc(s.s_cen, LEAD)
                pe.sem_inc(s.s_var, LEAD)
                with pe.Fori(0, SEQS) as seq:
                    for half in range(2):
                        if not layer:
                            break
                        n = 2 * seq + half
                        pe.wait_ge(s.s_un, after(n - 2))
                        for i, (mat, buf, shifted) in enumerate(terms):
                            if not shifted:
                                mm = nc.tensor.matmul(cen[:, half, :], mat[:, :], buf[:, ds(X0 + seq * SEQ + half * HALF, HALF)],
                                                      start=i == 0, stop=True, skip_group_check=True)
                            elif half == 0:
                                mm = nc.tensor.matmul(cen[:, half, 1:HALF], mat[:, :], buf[:, ds(X0 + seq * SEQ, HALF - 1)],
                                                      start=False, stop=True, skip_group_check=True)
                            else:
                                mm = nc.tensor.matmul(cen[:, half, :], mat[:, :], buf[:, ds(X0 + seq * SEQ + half * HALF - 1, HALF)],
                                                      start=False, stop=True, skip_group_check=True)
                        mm.then_inc(s.s_cen, 1)
                    for half in range(2):
                        n = 2 * seq + half
                        pe.wait_ge(s.s_sq, after(n))
                        pe.wait_ge(s.s_t1, after(n - 2))
                        nc.tensor.matmul(var[:, half, :], m.mean[:, :], s.sq[:, half, :], start=True, stop=True, skip_group_check=True).then_inc(s.s_var, 1)

            @block.scalar
            def _(act):
                act.preload_act_table_set("natural_log_exp_and_others")
                act.sem_inc(s.s_sq, LEAD)
                act.sem_inc(s.s_ln, LEAD)
                act.sem_inc(s.s_y0, LEAD)
                act.sem_inc(s.s_out, LEAD)

                def finish(n, half, seq):
                    act.wait_ge(s.s_un, after(n))
                    m.settle(act)
                    here = ds(out_at + seq * SEQ + half * HALF, HALF)
                    if gain is not None:
                        nc.scalar.activation(out[:, here], s.un[:, half, :], ACT.Identity, scale=gain,
                                             bias=bias if bias is not None else 0.0).then_inc(s.s_out, 1)
                    else:
                        nc.scalar.activation(out[:, here], s.un[:, half, :], ACT.Copy).then_inc(s.s_out, 1)

                with act.Fori(0, SEQS) as seq:
                    for half in range(2):
                        n = 2 * seq + half
                        act.wait_ge(s.s_var, after(n - 2))
                        if layer:
                            act.wait_ge(s.s_cen, after(n))
                            nc.scalar.activation(s.sq[:, half, :], cen[:, half, :], ACT.Square).then_inc(s.s_sq, 1)
                        else:
                            m.settle(act)
                            nc.scalar.activation(s.sq[:, half, :], src[:, ds(X0 + seq * SEQ + half * HALF, HALF)], ACT.Square).then_inc(s.s_sq, 1)
                    for half in range(2):
                        n = 2 * seq + half
                        if layer:
                            act.wait_ge(s.s_var, after(n))
                            act.wait_ge(s.s_y0, after(n - 2))
                            nc.scalar.activation(s.lnv[:, half, :], var[:, half, :], ACT.Ln, scale=ln_scale,
                                                 bias=eps * ln_scale).then_inc(s.s_ln, 1)
                        else:
                            act.wait_ge(s.s_floor, after(n))
                            act.wait_ge(s.s_y0, after(n - 2))
                            nc.scalar.activation(s.lnv[:, half, :], s.t2[:, half, :], ACT.Ln, scale=ln_scale).then_inc(s.s_ln, 1)
                    for half in range(2):
                        n = 2 * seq + half
                        act.wait_ge(s.s_ln, after(n))
                        act.wait_ge(s.s_t3, after(n - 2))
                        nc.scalar.activation(s.y0[:, half, :], s.lnv[:, half, :], ACT.Exp, scale=-0.5,
                                             bias=12 * float(np.log(2.0))).then_inc(s.s_y0, 1)
                    for half in range(2):
                        finish(2 * seq + half, half, seq)

            @block.vector
            def _(dve):
                for x in (s.s_floor, s.s_t1, s.s_t2, s.s_t3, s.s_un):
                    dve.sem_inc(x, LEAD)
                with dve.Fori(0, SEQS) as seq:
                    if not layer:
                        for half in range(2):
                            n = 2 * seq + half
                            dve.wait_ge(s.s_var, after(n))
                            dve.wait_ge(s.s_t3, after(n - 2))
                            nc.vector.tensor_scalar(s.t2[:, half, :], var[:, half, :], floor, None, ALU.max).then_inc(s.s_floor, 1)
                    for half in range(2):
                        n = 2 * seq + half
                        dve.wait_ge(s.s_y0, after(n))
                        dve.wait_ge(s.s_t2, after(n - 2))
                        nc.vector.scalar_tensor_tensor(s.t1[:, half, :], var[:, half, :], eps if layer else floor, s.y0[:, half, :],
                                                       ALU.add if layer else ALU.max, ALU.mult).then_inc(s.s_t1, 1)
                    for half in range(2):
                        n = 2 * seq + half
                        dve.wait_ge(s.s_t1, after(n))
                        dve.wait_ge(s.s_t3, after(n - 2))
                        if not layer:
                            dve.wait_ge(s.s_ln, after(n))
                        nc.vector.scalar_tensor_tensor(s.t2[:, half, :], s.t1[:, half, :], -0.5, s.y0[:, half, :],
                                                       ALU.mult, ALU.mult).then_inc(s.s_t2, 1)
                    for half in range(2):
                        n = 2 * seq + half
                        dve.wait_ge(s.s_t2, after(n))
                        dve.wait_ge(s.s_un, after(n - 2))
                        nc.vector.scalar_tensor_tensor(s.t3[:, half, :], s.t2[:, half, :], 1.5, s.y0[:, half, :],
                                                       ALU.add, ALU.mult).then_inc(s.s_t3, 1)
                    for half in range(2):
                        n = 2 * seq + half
                        here = ds(X0 + seq * SEQ + half * HALF, HALF)
                        dve.wait_ge(s.s_t3, after(n))
                        dve.wait_ge(s.s_out, after(n - 2))
                        nc.vector.tensor_tensor(s.un[:, half, :], cen[:, half, :] if layer else src[:, here], s.t3[:, half, :],
                                                ALU.mult).then_inc(s.s_un, 1)

            if out2 is not None:
                @block.gpsimd
                def _(pool):
                    with pool.Fori(0, SEQS) as seq:
                        for half in range(2):
                            pool.wait_ge(s.s_out, after(2 * seq + half))
                            m.settle(pool)
                            here = ds(out_at + seq * SEQ + half * HALF, HALF)
                            nc.gpsimd.tensor_copy(out2[:, here], out[:, here])
        m.phase_end()


class Ffn:

    def __init__(self, m):
        self.m = m
        self.w1 = m.sb("ffn_w1", [P, 2 * HID])
        self.w2 = m.sb("ffn_w2", [HC[0], 3, P])
        self.vec = m.sb("ffn_vec", [P, 9])
        self.gate, at = m.carve(0, [HC[0], 3, HALF])
        self.u, at = m.carve(at, [HC[0], 3, HALF])
        self.s_load = m.sem("ffn_loaded")
        self.s_gp = m.sem("ffn_gate_products")
        self.s_ap = m.sem("ffn_value_products")
        self.s_gate = m.sem("ffn_gates")
        self.s_u = m.sem("ffn_gated")
        self.s_down = m.sem("ffn_down")
        self.s_x = m.sem("ffn_added")

    def load(self, sp, w1, w2, vec):
        sp.dma_start(self.w1[:, :], w1).then_inc(self.s_load, 16)
        sp.dma_start(self.w2[:, 0:2, :], w2[0:HO[2], :].rearrange("(c p) n -> p c n", c=2)).then_inc(self.s_load, 16)
        sp.dma_start(self.w2[0:HC[2], 2, :], w2[HO[2]:HID, :]).then_inc(self.s_load, 16)
        sp.dma_start(self.vec[:, :], vec).then_inc(self.s_load, 16)
        sp.wait_ge(self.s_load, 64)

    def phase(self, src, dst, func, sp_work=None, gate_first=False):
        nc, m, s = self.m.nc, self.m, self
        CH = TOK // HALF
        avals, gates, down = m.psum[:, 0:3, :], m.psum[:, 3:6, :], m.psum[:, 6, :]
        off = dict(a=HID, g=0) if gate_first else dict(a=0, g=HID)
        with nc.Block() as block:
            if sp_work:
                block.sync(sp_work)

            @block.tensor
            def _(pe):
                for x in (s.s_gp, s.s_ap, s.s_down):
                    pe.sem_inc(x, LEAD)

                def up(which, bank, n, at):
                    for c in range(3):
                        if which == "g":
                            pe.wait_ge(s.s_gate, after(3 * (n - 1) + c))
                        else:
                            pe.wait_ge(s.s_u, after(3 * (n - 1) + c))
                        nc.tensor.matmul(bank[0:HC[c], c, :], s.w1[:, off[which] + HO[c]:off[which] + HO[c] + HC[c]],
                                         m.hn[:, at], start=True, stop=True, skip_group_check=True).then_inc(s.s_gp if which == "g" else s.s_ap, 1)

                up("g", gates, 0, ds(0, HALF))
                up("a", avals, 0, ds(0, HALF))
                with pe.Fori(0, CH) as n:
                    up("g", gates, n + 1, ds((n + 1) * HALF, HALF))
                    pe.wait_ge(s.s_x, after(n - 1))
                    for c in range(3):
                        pe.wait_ge(s.s_u, after(3 * n + c))
                        mm = nc.tensor.matmul(down, s.w2[0:HC[c], c, :], s.u[0:HC[c], c, :], start=c == 0, stop=True, skip_group_check=True)
                    mm.then_inc(s.s_down, 1)
                    up("a", avals, n + 1, ds((n + 1) * HALF, HALF))

            @block.scalar
            def _(act):
                act.preload_act_table(func)
                act.sem_inc(s.s_gate, LEAD)
                with act.Fori(0, CH) as n:
                    for c in range(3):
                        act.wait_ge(s.s_gp, after(3 * n + c))
                        act.wait_ge(s.s_u, after(3 * (n - 1) + c))
                        nc.scalar.activation(s.gate[0:HC[c], c, :], gates[0:HC[c], c, :], func,
                                             bias=s.vec[0:HC[c], 6 + c:7 + c]).then_inc(s.s_gate, 1)

            @block.vector
            def _(dve):
                dve.sem_inc(s.s_u, LEAD)
                dve.sem_inc(s.s_x, LEAD)
                with dve.Fori(0, CH) as n:
                    for c in range(3):
                        dve.wait_ge(s.s_ap, after(3 * n + c))
                        dve.wait_ge(s.s_gate, after(3 * n + c))
                        dve.wait_ge(s.s_down, after(n - 1))
                        nc.vector.scalar_tensor_tensor(s.u[0:HC[c], c, :], avals[0:HC[c], c, :], s.vec[0:HC[c], 3 + c:4 + c],
                                                       s.gate[0:HC[c], c, :], ALU.add, ALU.mult).then_inc(s.s_u, 1)
                    dve.wait_ge(s.s_down, after(n))
                    here = ds(X0 + n * HALF, HALF)
                    nc.vector.scalar_tensor_tensor(dst[:, here], down, s.vec[:, 2:3], src[:, here],
                                                   ALU.add, ALU.add).then_inc(s.s_x, 1)
        m.phase_end()


class Windowed:

    U = 4

    def __init__(self, m):
        self.m = m
        sb, sem, U = m.sb, m.sem, self.U
        self.wqkv, top = m.carve(SCRATCH, [P, 2 * 3 * GW])
        self.wo, top = m.carve(top, [P, 8, P])
        self.scale_qk = sb("att_scale_qk", [P, 2, HD])
        self.rope, top = m.carve(top, [P, 4, ROPE_TILES, HD])
        self.rope_l, top = m.carve(top, [P, 4, ROPE_TILES, HD])
        self.masks = sb("att_masks", [P, P + HD], BF16)
        self.prior_off = sb("att_prior_off", [P, ROPE_TILES])
        self.prior_cap = sb("att_prior_cap", [P, ROPE_TILES])
        self.keep = sb("att_keep", [P, ROPE_TILES])
        self.h, at = m.carve(0, [P, U, P])
        self.sq, at = m.carve(at, [P, 2 * GW])
        self.ssq = sb("att_ssq", [P, 2 * GH])
        self.lnv = sb("att_lnv", [P, 2 * GH])
        self.y0 = sb("att_y0", [P, 2 * GH])
        self.t1 = sb("att_t1", [P, 2 * GH])
        self.t2 = sb("att_t2", [P, 2 * GH])
        self.t3 = sb("att_t3", [P, 2 * GH])
        self.rinv = sb("att_rinv", [P, 2 * GH])
        self.qkn, at = m.carve(at, [P, 2, GW])
        self.qcos, at = m.carve(at, [P, GW])
        self.qsin, at = m.carve(at, [P, GW])
        self.kcos, at = m.carve(at, [P, GW])
        self.ksin, at = m.carve(at, [P, GW])
        self.qr, at = m.carve(at, [P, GW])
        self.kr, at = m.carve(at, [P, GW])
        self.qt, at = m.carve(at, [P, 4, P])
        self.kt, top = m.carve(top, [P, U, 4, 2, P])
        self.v, top = m.carve(top, [P, U, GH, VW_])
        self.mx = sb("att_mx", [P, GH])
        self.mxp = sb("att_mxp", [HD, GH])
        self.e, at = m.carve(at, [P, GH, P])
        self.dp, at = m.carve(at, [HD, GH * HD])
        self.ep, top = m.carve(top, [HD, GH, P])
        self.et, at = m.carve(at, [P, GH, P])
        self.ept, at = m.carve(at, [P, GH * HD])
        self.rden = sb("att_rden", [P, GH])
        self.o = sb("att_o", [P, GW])
        self.ot, at = m.carve(at, [P, 4, P])
        assert at <= SCRATCH
        self.s_h = sem("att_tile_staged")
        self.s_qk = sem("att_q_k_projected")
        self.s_vp = sem("att_v_projected")
        self.s_sq = sem("att_squared")
        self.s_ssq = sem("att_squares_summed")
        self.s_clamp = sem("att_sums_clamped")
        self.s_ln = sem("att_sums_ln")
        self.s_y0 = sem("att_norm_guess")
        self.s_t1 = sem("att_newton1")
        self.s_t2 = sem("att_newton2")
        self.s_t3 = sem("att_newton3")
        self.s_rinv = sem("att_norm_inverse")
        self.s_qkn = sem("att_q_k_normalised")
        self.s_qcos = sem("att_q_cos")
        self.s_qsin = sem("att_q_sin")
        self.s_qr = sem("att_q_rotated")
        self.s_kcos = sem("att_k_cos")
        self.s_ksin = sem("att_k_sin")
        self.s_kr = sem("att_k_rotated")
        self.s_qkt = sem("att_q_k_transposed")
        self.s_qt = sem("att_q_copied")
        self.s_kt = sem("att_k_copied")
        self.s_v = sem("att_v_copied")
        self.s_scp = sem("att_prior_scores")
        self.s_sc = sem("att_scores")
        self.s_mxp = sem("att_prior_maxima")
        self.s_mx = sem("att_maxima")
        self.s_mxc = sem("att_maxima_joined")
        self.s_subp = sem("att_prior_less_maxima")
        self.s_sub = sem("att_less_maxima")
        self.s_ep = sem("att_prior_exp")
        self.s_e = sem("att_exp")
        self.s_pt = sem("att_weights_transposed")
        self.s_ptp = sem("att_prior_weights_transposed")
        self.s_et = sem("att_weights_copied")
        self.s_ept = sem("att_prior_weights_copied")
        self.s_pv = sem("att_values_weighted")
        self.s_rden = sem("att_reciprocals")
        self.s_o = sem("att_values_scaled")
        self.s_otp = sem("att_output_transposed")
        self.s_ot = sem("att_output_copied")
        self.s_wo = sem("att_output_projected")
        self.s_x = sem("att_output_added")
        self.s_load = sem("att_loaded")

    def load(self, sp, wqkv, wo, scale_qk, n, extra=()):
        for dst, src in [(self.wqkv[:, 0:wqkv.shape[-1]], wqkv), (self.wo[:, 0:n, :], wo), (self.scale_qk[:, :, :], scale_qk), *extra]:
            sp.dma_start(dst, src).then_inc(self.s_load, 16)
        sp.wait_ge(self.s_load, 16 * (3 + len(extra)))

    def scale_tables(self):
        nc, m, s = self.m.nc, self.m, self
        with nc.Block() as block:
            @block.vector
            def _(dve):
                H2 = HD // 2
                for i, (side, swap) in enumerate([(0, False), (0, True), (1, False), (1, True)]):
                    for a in range(2):
                        b = 1 - a if swap else a
                        nc.vector.tensor_tensor(s.rope_l[:, i, :, a * H2:(a + 1) * H2], s.rope[:, i, :, a * H2:(a + 1) * H2],
                                                s.scale_qk[:, side, b * H2:(b + 1) * H2].unsqueeze(1).to_broadcast([P, ROPE_TILES, H2]),
                                                ALU.mult)
        m.phase_end()

    def phase(self, G, W, sp_work=None):
        nc, m, s, U = self.m.nc, self.m, self, self.U
        NT = U // G
        BODIES = TILES // NT
        UNITS = SEQS * BODIES * U
        ps = m.psum
        p_qk, p_v = ps[:, 0:2, :], ps[:, 2, :]
        p_qt, p_kt = ps[:, 3, :], ps[:, 4, :]
        p_s, p_sp = ps[:, 3:5, :], ps[:, 5, :]
        p_et, p_ept = ps[:, 6:8, :], ps[:, 5, :]
        p_o = ps[:, 6:8, 0:4 * VW_]
        p_ot, p_wo = ps[:, 2, :], ps[:, 2, 0:P]
        mask, mask_p = s.masks[:, 0:P], s.masks[:, P:P + W]
        H2 = HD // 2

        def heads(ap, d=HD):
            return ap.rearrange("p (h d) -> p h d", d=d)

        def halves(ap):
            return ap.rearrange("p (h two d) -> p h two d", two=2, d=H2)

        def flat(ap):
            return ap.rearrange("p h t -> p (h t)")

        def split(k):
            return k // G, k % G

        def tile_of(j, k):
            return ds(j * NT + split(k)[0], 1)

        def pe_qk(pe, bi, k):
            n = bi * U + k
            tile, g = split(k)
            pe.wait_ge(s.s_h, after(bi * NT + tile))
            pe.wait_ge(s.s_qkn, after(n - 1))
            for side in range(2):
                at = (side * G + g) * GW
                mm = nc.tensor.matmul(ps[:, side, :], s.h[:, tile % NT, :], s.wqkv[:, at:at + GW], start=True, stop=True, skip_group_check=True)
            mm.then_inc(s.s_qk, 1)

        def pe_v(pe, n, k):
            tile, g = split(k)
            pe.wait_ge(s.s_x, after(n - 2))
            at = (2 * G + g) * GW
            nc.tensor.matmul(p_v, s.h[:, tile % NT, :], s.wqkv[:, at:at + GW], start=True, stop=True, skip_group_check=True).then_inc(s.s_vp, 1)

        def pe_transpose(pe, n):
            pe.wait_ge(s.s_qr, after(n))
            pe.wait_ge(s.s_kr, after(n))
            pe.wait_ge(s.s_sub, after(n - 1))
            for src, bank in ((s.qr, p_qt), (s.kr, p_kt)):
                for c in range(4):
                    mm = nc.tensor.transpose(bank[:, c * P:(c + 1) * P], src[:, c * P:(c + 1) * P], m.ident[:, :])
            mm.then_inc(s.s_qkt, 1)

        def pe_scores(pe, n, k):
            pe.wait_ge(s.s_qt, after(n))
            pe.wait_ge(s.s_kt, after(n))
            pe.wait_ge(s.s_ept, after(n - 2))
            nc.tensor.matmul(p_sp[0:W, 0:GH * W], m.ident_bf[:, 0:W], mask_p.unsqueeze(1).to_broadcast([P, GH, W]),
                             start=True, stop=True, skip_group_check=True)
            for pair in range(4):
                mm = nc.tensor.matmul(p_sp[0:W, pair * 2 * W:(pair + 1) * 2 * W], s.qt[:, pair, 0:W],
                                      s.kt[:, (k - G) % U, pair, :, P - W:P], start=False, stop=True, skip_group_check=True)
            mm.then_inc(s.s_scp, 1)
            for b in range(2):
                nc.tensor.matmul(p_s[:, b, :], m.ident_bf[:, :], mask.unsqueeze(1).to_broadcast([P, 4, P]),
                                 start=True, stop=True, skip_group_check=True)
                for c in range(2):
                    mm = nc.tensor.matmul(p_s[:, b, c * 2 * P:(c + 1) * 2 * P], s.qt[:, 2 * b + c, :], flat(s.kt[:, k % U, 2 * b + c, :, :]),
                                          start=False, stop=True, skip_group_check=True)
            mm.then_inc(s.s_sc, 1)

        def pe_transpose_weights(pe, n):
            pe.wait_ge(s.s_e, after(n))
            pe.wait_ge(s.s_o, after(n - 1))
            for b in range(2):
                for c in range(4):
                    mm = nc.tensor.transpose(p_et[:, b, c * P:(c + 1) * P], s.e[:, 4 * b + c, :], m.ident[:, :])
                mm.then_inc(s.s_pt, 1)

        def pe_transpose_prior_weights(pe, n):
            pe.wait_ge(s.s_ep, after(n))
            pe.wait_ge(s.s_subp, after(n + 1))
            m.settle(pe)
            for h in range(GH):
                mm = nc.tensor.transpose(p_ept[:, h * W:(h + 1) * W], s.ep[0:W, h, :], m.ident[0:W, 0:W])
            mm.then_inc(s.s_ptp, 1)

        def pe_values(pe, n, k):
            pe.wait_ge(s.s_v, after(n))
            pe.wait_ge(s.s_ept, after(n))
            for h in range(GH):
                b, c = divmod(h, 4)
                if c == 0:
                    pe.wait_ge(s.s_et, after(2 * n + b))
                nc.tensor.matmul(p_o[:, b, c * VW_:(c + 1) * VW_], s.et[:, h, :], s.v[:, k, h, :],
                                 start=True, stop=True, skip_group_check=True)
                mm = nc.tensor.matmul(p_o[0:W, b, c * VW_:(c + 1) * VW_], s.ept[:, h * W:(h + 1) * W],
                                      s.v[:, (k - G) % U, h, :], start=False, stop=True, skip_group_check=True)
            mm.then_inc(s.s_pv, 1)

        def pe_transpose_out(pe, n):
            pe.wait_ge(s.s_o, after(n))
            pe.wait_ge(s.s_v, after(n + 1))
            for c in range(4):
                mm = nc.tensor.transpose(p_ot[:, c * P:(c + 1) * P], s.o[:, c * P:(c + 1) * P], m.ident[:, :])
            mm.then_inc(s.s_otp, 1)

        def pe_project_out(pe, n, k):
            pe.wait_ge(s.s_ot, after(n))
            for c in range(4):
                mm = nc.tensor.matmul(p_wo, s.wo[:, 4 * split(k)[1] + c, :], s.ot[:, c, :], start=c == 0, stop=True, skip_group_check=True)
            mm.then_inc(s.s_wo, 1)

        def act_stage(act, bi, j, k):
            tile = split(k)[0]
            slot = tile % NT
            col = X0 + (bi * NT + tile) * P
            act.wait_ge(s.s_vp, after(bi * U + k - U + G - 1))
            m.settle(act)
            nc.scalar.activation(s.h[0:64, slot, :], m.xa[0:64, ds(col, P)], ACT.Copy)
            nc.scalar.activation(s.h[64:P, slot, 1:P], m.xa[64:P, ds(col, P - 1)], ACT.Copy)
            nc.scalar.activation(s.h[64:P, slot, 0:1], m.xa[64:P, ds(col - 1, 1)], ACT.Copy,
                                 scale=s.keep[64:P, tile_of(j, k)]).then_inc(s.s_h, 1)

        def act_squares(act, n):
            act.wait_ge(s.s_qk, after(n))
            act.wait_ge(s.s_ssq, after(n - 1))
            nc.scalar.activation(s.sq[:, :].rearrange("p (a c) -> p a c", a=2), p_qk, ACT.Square).then_inc(s.s_sq, 1)

        def act_guess(act, n):
            act.wait_ge(s.s_clamp, after(n))
            nc.scalar.activation(s.lnv[:, :], s.ssq[:, :], ACT.Ln, scale=2.0 ** 16).then_inc(s.s_ln, 1)
            act.wait_ge(s.s_ln, after(n))
            act.wait_ge(s.s_rinv, after(n - 1))
            nc.scalar.activation(s.y0[:, :], s.lnv[:, :], ACT.Exp, scale=-0.5, bias=8 * float(np.log(2.0))).then_inc(s.s_y0, 1)

        def act_qk(act, n, k):
            act.wait_ge(s.s_qkt, after(n))
            act.wait_ge(s.s_sc, after(n - 1))
            nc.scalar.activation(flat(s.qt[:, :, :]), p_qt, ACT.Copy).then_inc(s.s_qt, 1)
            src = p_kt.rearrange("p (c t) -> p c t", c=4)
            nc.scalar.activation(s.kt[0:HD, k % U, :, 0, :], src[0:HD], ACT.Copy)
            nc.scalar.activation(s.kt[HD:P, k % U, :, 1, :], src[HD:P], ACT.Copy).then_inc(s.s_kt, 1)

        def act_v(act, n, k):
            act.wait_ge(s.s_vp, after(n))
            act.wait_ge(s.s_pv, after(n - 2))
            nc.scalar.activation(s.v[:, k % U, :, 0:HD], heads(p_v), ACT.Copy).then_inc(s.s_v, 1)

        def act_exp(act, n, j, k):
            act.wait_ge(s.s_sub, after(n))
            nc.scalar.activation(s.e[:, :, :], s.e[:, :, :], ACT.Exp).then_inc(s.s_e, 1)
            act.wait_ge(s.s_subp, after(n))
            act.wait_ge(s.s_ptp, after(n - 1))
            m.settle(act)
            nc.scalar.activation(s.ep[0:W, :, P - W:P], heads(s.dp[0:W, 0:GH * W], W), ACT.Exp, bias=s.prior_off[0:W, tile_of(j, k)],
                                 scale=s.keep[0:W, tile_of(j, k)]).then_inc(s.s_ep, 1)

        def act_weights(act, n):
            act.wait_ge(s.s_pv, after(n - 1))
            for b in range(2):
                act.wait_ge(s.s_pt, after(2 * n + b))
                nc.scalar.activation(flat(s.et[:, 4 * b:4 * b + 4, :]), p_et[:, b, :], ACT.Copy).then_inc(s.s_et, 1)

        def act_prior_weights(act, n):
            act.wait_ge(s.s_ptp, after(n))
            nc.scalar.activation(s.ept[:, 0:GH * W], p_ept[:, 0:GH * W], ACT.Copy).then_inc(s.s_ept, 1)

        def act_out(act, n):
            act.wait_ge(s.s_otp, after(n))
            act.wait_ge(s.s_wo, after(n - 1))
            nc.scalar.activation(flat(s.ot[:, :, :]), p_ot, ACT.Copy).then_inc(s.s_ot, 1)

        def dve_sums(dve, n):
            dve.wait_ge(s.s_sq, after(n))
            dve.wait_ge(s.s_t1, after(n - 1))
            nc.vector.reduce_sum(s.ssq[:, :], heads(s.sq[:, :]), AX_X).then_inc(s.s_ssq, 1)

        def dve_norm(dve, n):
            dve.wait_ge(s.s_rinv, after(n))
            dve.wait_ge(s.s_qsin, after(n - 1))
            dve.wait_ge(s.s_ksin, after(n - 1))
            nc.vector.tensor_tensor(s.qkn[:, :, :].rearrange("p a (h d) -> p (a h) d", d=HD), p_qk.rearrange("p a (h d) -> p (a h) d", d=HD),
                                    s.rinv[:, :].unsqueeze(2).to_broadcast([P, 2 * GH, HD]), ALU.mult).then_inc(s.s_qkn, 1)

        def cos_sin(eng, j, k, side, cos_b, sin_b, s_cos, s_sin):
            src = s.qkn[:, side, :]
            cos, sin = (s.rope_l[:, 2 * side + i, tile_of(j, k), :] for i in range(2))
            eng.tensor_tensor(heads(cos_b[:, :]), heads(src), cos.to_broadcast([P, GH, HD]), ALU.mult).then_inc(s_cos, 1)
            for a in range(2):
                ins = eng.tensor_tensor(halves(sin_b[:, :])[:, :, a, :], halves(src)[:, :, 1 - a, :],
                                        sin[:, :, a * H2:(a + 1) * H2].to_broadcast([P, GH, H2]), ALU.mult)
            ins.then_inc(s_sin, 1)

        def dve_q(dve, n, j, k):
            dve.wait_ge(s.s_qkn, after(n))
            dve.wait_ge(s.s_qr, after(n - 1))
            cos_sin(nc.vector, j, k, 0, s.qcos, s.qsin, s.s_qcos, s.s_qsin)

        def dve_maxima(dve, n, j, k):
            dve.wait_ge(s.s_scp, after(n))
            dve.wait_ge(s.s_sub, after(n - 1))
            nc.vector.reduce_max(s.mxp[0:W, :], heads(p_sp[0:W, 0:GH * W], W), AX_X).then_inc(s.s_mxp, 1)
            dve.wait_ge(s.s_sc, after(n))
            nc.vector.reduce_max(s.mx[:, :], p_s.rearrange("p b (h t) -> p (b h) t", t=P), AX_X).then_inc(s.s_mx, 1)
            dve.wait_ge(s.s_mxp, after(n))
            dve.wait_ge(s.s_mx, after(n))
            nc.vector.scalar_tensor_tensor(s.mx[0:W, :], s.mxp[0:W, :], s.prior_cap[0:W, tile_of(j, k)], s.mx[0:W, :],
                                           ALU.min, ALU.max).then_inc(s.s_mxc, 1)
            dve.wait_ge(s.s_mxc, after(n))
            dve.wait_ge(s.s_ep, after(n - 1))
            nc.vector.tensor_tensor(heads(s.dp[0:W, 0:GH * W], W), heads(p_sp[0:W, 0:GH * W], W),
                                    s.mx[0:W, :].unsqueeze(2).to_broadcast([W, GH, W]), ALU.subtract).then_inc(s.s_subp, 1)
            dve.wait_ge(s.s_pt, after(2 * (n - 1) + 1))
            nc.vector.tensor_tensor(s.e[:, :, :], p_s.rearrange("p b (h t) -> p (b h) t", t=P),
                                    s.mx[:, :].unsqueeze(2).to_broadcast([P, GH, P]), ALU.subtract).then_inc(s.s_sub, 1)

        def dve_scale(dve, n):
            dve.wait_ge(s.s_pv, after(n))
            dve.wait_ge(s.s_o, after(n - 1))
            ov = p_o.rearrange("p b (h d) -> p b h d", d=VW_)
            rden = s.rden[:, :].rearrange("p (b h) -> p b h", b=2)
            nc.vector.reciprocal(rden, ov[:, :, :, HD]).then_inc(s.s_rden, 1)
            dve.wait_ge(s.s_rden, after(n))
            dve.wait_ge(s.s_otp, after(n - 1))
            nc.vector.tensor_tensor(s.o[:, :].rearrange("p (b h d) -> p b h d", b=2, d=HD), ov[:, :, :, 0:HD],
                                    rden.unsqueeze(3).to_broadcast([P, 2, 4, HD]), ALU.mult).then_inc(s.s_o, 1)

        def dve_add(dve, n, bi, k):
            tile, g = split(k)
            dve.wait_ge(s.s_wo, after(n))
            here = ds(X0 + (bi * NT + tile) * P, P)
            if g:
                dve.wait_ge(s.s_x, after(n - 1))
            nc.vector.tensor_tensor(m.xb[:, here], p_wo, (m.xb if g else m.xa)[:, here], ALU.add).then_inc(s.s_x, 1)

        def pool_clamp(pool, n):
            pool.wait_ge(s.s_ssq, after(n))
            m.settle(pool)
            nc.gpsimd.tensor_scalar(s.ssq[:, :], s.ssq[:, :], 1e-24, None, ALU.max).then_inc(s.s_clamp, 1)

        def pool_newton(pool, n):
            pool.wait_ge(s.s_y0, after(n))
            pool.wait_ge(s.s_t2, after(n - 1))
            nc.gpsimd.tensor_tensor(s.t1[:, :], s.ssq[:, :], s.y0[:, :], ALU.mult).then_inc(s.s_t1, 1)
            pool.wait_ge(s.s_t1, after(n))
            pool.wait_ge(s.s_rinv, after(n - 1))
            nc.gpsimd.tensor_tensor(s.t2[:, :], s.t1[:, :], s.y0[:, :], ALU.mult).then_inc(s.s_t2, 1)
            pool.wait_ge(s.s_t2, after(n))
            m.settle(pool)
            nc.gpsimd.tensor_scalar(s.t3[:, :], s.t2[:, :], -0.5, 1.5, ALU.mult, ALU.add).then_inc(s.s_t3, 1)
            pool.wait_ge(s.s_t3, after(n))
            pool.wait_ge(s.s_qkn, after(n - 1))
            nc.gpsimd.tensor_tensor(s.rinv[:, :], s.t3[:, :], s.y0[:, :], ALU.mult).then_inc(s.s_rinv, 1)

        def pool_rotate(pool, n, j, k):
            pool.wait_ge(s.s_qkn, after(n))
            pool.wait_ge(s.s_kr, after(n - 1))
            m.settle(pool)
            cos_sin(nc.gpsimd, j, k, 1, s.kcos, s.ksin, s.s_kcos, s.s_ksin)
            pool.wait_ge(s.s_qsin, after(n))
            pool.wait_ge(s.s_qkt, after(n - 1))
            nc.gpsimd.tensor_tensor(s.qr[:, :], s.qcos[:, :], s.qsin[:, :], ALU.add).then_inc(s.s_qr, 1)
            pool.wait_ge(s.s_ksin, after(n))
            nc.gpsimd.tensor_tensor(s.kr[:, :], s.kcos[:, :], s.ksin[:, :], ALU.add).then_inc(s.s_kr, 1)

        with nc.Block() as block:
            if sp_work:
                block.sync(sp_work)

            @block.tensor
            def _(pe):
                for x in (s.s_qk, s.s_vp, s.s_qkt, s.s_scp, s.s_sc, s.s_pt, s.s_ptp, s.s_pv):
                    pe.sem_inc(x, LEAD)
                for x in (s.s_otp, s.s_wo):
                    pe.sem_inc(x, LEAD - 1)
                pe_qk(pe, 0, 0)
                pe_qk(pe, 0, 1)
                pe_transpose(pe, 0)
                pe_scores(pe, 0, 0)
                pe_qk(pe, 0, 2)
                pe_transpose(pe, 1)
                pe_v(pe, 0, 0)
                with pe.Fori(0, SEQS) as seq:
                    with pe.Fori(0, BODIES) as j:
                        for k in range(U):
                            bi = seq * BODIES + j
                            n = bi * U + k
                            pe_scores(pe, n + 1, k + 1)
                            pe_qk(pe, bi, k + 3)
                            pe_transpose_out(pe, n - 1)
                            pe_transpose_weights(pe, n)
                            pe_transpose_prior_weights(pe, n)
                            pe_project_out(pe, n - 1, k - 1)
                            pe_transpose(pe, n + 2)
                            pe_v(pe, n + 1, k + 1)
                            pe_values(pe, n, k)
                pe_transpose_out(pe, UNITS - 1)
                pe_project_out(pe, UNITS - 1, U - 1)

            @block.scalar
            def _(act):
                act.preload_act_table_set("natural_log_exp_and_others")
                for x in (s.s_h, s.s_sq, s.s_ln, s.s_y0, s.s_v, s.s_qt, s.s_kt, s.s_ep, s.s_e, s.s_et, s.s_ept):
                    act.sem_inc(x, LEAD)
                act.sem_inc(s.s_ot, LEAD - 1)
                for k in range(0, AHEAD, G):
                    act_stage(act, 0, 0, k)
                act_squares(act, 0)
                act_guess(act, 0)
                act_squares(act, 1)
                act_guess(act, 1)
                act_qk(act, 0, 0)
                act_squares(act, 2)
                act_guess(act, 2)
                act_exp(act, 0, 0, 0)
                act_qk(act, 1, 1)
                act_v(act, 0, 0)
                with act.Fori(0, SEQS) as seq:
                    with act.Fori(0, BODIES) as j:
                        for k in range(U):
                            bi = seq * BODIES + j
                            n = bi * U + k
                            if (k + 3) % G == 0:
                                act_stage(act, bi, j, k + 3)
                            act_squares(act, n + 3)
                            act_out(act, n - 1)
                            act_weights(act, n)
                            act_prior_weights(act, n)
                            act_guess(act, n + 3)
                            act_qk(act, n + 2, k + 2)
                            act_v(act, n + 1, k + 1)
                            act_exp(act, n + 1, j, k + 1)
                act_out(act, UNITS - 1)

            @block.vector
            def _(dve):
                for x in (s.s_ssq, s.s_qkn, s.s_qcos, s.s_qsin, s.s_mx, s.s_mxp, s.s_mxc, s.s_subp, s.s_sub, s.s_rden, s.s_o):
                    dve.sem_inc(x, LEAD)
                dve.sem_inc(s.s_x, LEAD - 1)
                dve_sums(dve, 0)
                dve_norm(dve, 0)
                dve_q(dve, 0, 0, 0)
                dve_sums(dve, 1)
                dve_norm(dve, 1)
                dve_maxima(dve, 0, 0, 0)
                dve_q(dve, 1, 0, 1)
                dve_sums(dve, 2)
                dve_norm(dve, 2)
                with dve.Fori(0, SEQS) as seq:
                    with dve.Fori(0, BODIES) as j:
                        for k in range(U):
                            bi = seq * BODIES + j
                            n = bi * U + k
                            dve_q(dve, n + 2, j, k + 2)
                            dve_maxima(dve, n + 1, j, k + 1)
                            dve_sums(dve, n + 3)
                            dve_add(dve, n - 1, bi, k - 1)
                            dve_norm(dve, n + 3)
                            dve_scale(dve, n)
                dve_add(dve, UNITS - 1, SEQS * BODIES - 1, U - 1)

            @block.gpsimd
            def _(pool):
                for x in (s.s_clamp, s.s_t1, s.s_t2, s.s_t3, s.s_rinv, s.s_kcos, s.s_ksin, s.s_kr, s.s_qr):
                    pool.sem_inc(x, LEAD)
                for k in range(2):
                    pool_clamp(pool, k)
                    pool_newton(pool, k)
                    pool_rotate(pool, k, 0, k)
                pool_clamp(pool, 2)
                pool_newton(pool, 2)
                with pool.Fori(0, SEQS) as seq:
                    with pool.Fori(0, BODIES) as j:
                        for k in range(U):
                            n = (seq * BODIES + j) * U + k
                            pool_rotate(pool, n + 2, j, k + 2)
                            pool_clamp(pool, n + 3)
                            pool_newton(pool, n + 3)
        m.phase_end()


class Mla:

    SHIFT, ROWS = 64, 80
    PART_Q, PART_K = [0, 0, 1, 0, 2, 1], [0, 1, 0, 2, 0, 1]
    VW = MLA_HD + 1
    PIECE = HALF // P

    def __init__(self, m):
        self.m = m
        sem = m.sem
        self.qs, at = self.wide(0)
        self.ks, at = self.wide(at)
        self.e, at = m.carve(at, [P, 4, HALF])
        self.mxp, at = m.carve(at, [P, MLA_HEADS, 2])
        self.neg, at = m.carve(at, [P, self.ROWS])
        self.y, at = m.carve(at, [P, P])
        self.rden, at = m.carve(at, [P, MLA_HEADS])
        self.oc, at = m.carve(at, [P, HALF])
        self.vs, at = m.carve(at, [P, 4, self.PIECE, self.VW])
        self.w = {}
        top = 0
        for name, rows in (("dq", 64), ("uqT", 64), ("dkv", 64), ("uk", P), ("uv", P), ("oT", P), ("aT", P), ("a", P),
                           ("keT", 64), ("kw", P), ("ve", 64), ("vw", P)):
            ap, top = m.carve(top, [P, P])
            self.w[name] = ap[0:rows]
        self.part, top = self.bf(top, 2 * 3 * HALF)
        self.rest, top = m.carve(top, [P, 2, HALF])
        self.rest2, top = m.carve(top, [P, 2, HALF])
        self.xt, top = m.carve(top, [P, SEQ])
        self.v = m.hn[:, 0:SEQS * TILES * MLA_HEADS * self.VW].rearrange("p (t h d) -> p t h d", h=MLA_HEADS, d=self.VW)
        self.causal = m.sb("mla_causal", [P, 2 * P], BF16)
        self.s_w = sem("mla_s_w")
        self.s_wc = sem("mla_s_wc")
        self.s_pj = sem("mla_s_pj")
        self.s_p1 = sem("mla_s_p1")
        self.s_r1 = sem("mla_s_r1")
        self.s_p2 = sem("mla_s_p2")
        self.s_r2 = sem("mla_s_r2")
        self.s_p3 = sem("mla_s_p3")
        self.s_scr = sem("mla_s_scr")
        self.s_xt = sem("mla_s_xt")
        self.s_v = sem("mla_s_v")
        self.s_vc = sem("mla_s_vc")
        self.s_load = sem("mla_s_load")
        self.s_one = sem("mla_s_one")
        self.s_a = sem("mla_s_a")
        self.s_max = sem("mla_s_max")
        self.s_neg = sem("mla_s_neg")
        self.s_negt = sem("mla_s_negt")
        self.s_shift = sem("mla_s_shift")
        self.s_st = sem("mla_s_st")
        self.s_e = sem("mla_s_e")
        self.s_pv = sem("mla_s_pv")
        self.s_y = sem("mla_s_y")
        self.s_yt = sem("mla_s_yt")
        self.s_out = sem("mla_s_out")
        self.s_rden = sem("mla_s_rden")
        self.s_zero = sem("mla_s_zero")
        self.s_vs = sem("mla_s_vs")
        self.s_oc = sem("mla_s_oc")
        self.s_ot = sem("mla_s_ot")
        self.s_negc = sem("mla_s_negc")

    def bf(self, at, cols):
        return self.m.arena[:, at:at + cols // 2].bitcast(BF16), at + cols // 2

    def wide(self, at):
        ap, at = self.bf(at, MLA_HEADS * SEQ)
        return ap.rearrange("p (h t) -> p h t", h=MLA_HEADS), at

    def weights(self, t):
        nc, m, s, w = self.m.nc, self.m, self, self.w
        steps = [("aT", "uqT", "dq"), ("a", "dq", "uqT"), ("ve", "uv", "oT"), ("keT", "uk", "aT"), ("kw", "dkv", "keT"), ("vw", "dkv", "ve")]
        widths = {"uk": MLA_LAT, "uv": MLA_LAT}
        with nc.Block() as block:
            @block.sync
            def _(sp):
                for name in ("dq", "uqT", "dkv", "uk", "uv", "oT"):
                    sp.dma_start(w[name][:, 0:widths.get(name, P)], t["mla_" + name]).then_inc(s.s_load, 16)

            @block.tensor
            def _(pe):
                pe.wait_ge(s.s_load, 6 * 16)
                for i, (_, a, b) in enumerate(steps):
                    if i:
                        pe.wait_ge(s.s_wc, i)
                    cols = widths.get(a, P)
                    nc.tensor.matmul(m.psum[0:cols, 0, 0:P], w[a][:, 0:cols], w[b][:, 0:P], start=True, stop=True).then_inc(s.s_w, 1)

            @block.vector
            def _(dve):
                for i, (name, a, _) in enumerate(steps):
                    dve.wait_ge(s.s_w, i + 1)
                    nc.vector.tensor_copy(w[name], m.psum[0:widths.get(a, P), 0, 0:P]).then_inc(s.s_wc, 1)
        m.phase_end()

    def projections(self, scratch):
        nc, m, s = self.m.nc, self.m, self
        scale = float(MLA_HD) ** -0.5
        part = s.part.rearrange("p (a i t) -> p a i t", a=2, i=3)
        with nc.Block() as block:
            @block.tensor
            def _(pe):
                pe.sem_inc(s.s_pj, LEAD)
                pe.sem_inc(s.s_v, LEAD)
                with pe.Fori(0, SEQS) as seq:
                    for half in range(2):
                        n = 2 * seq + half
                        pe.wait_ge(s.s_r1, after(n - 1))
                        for a, wn in enumerate(("a", "kw")):
                            mm = nc.tensor.matmul(m.psum[:, a, :], s.w[wn], m.xa[:, ds(X0 + seq * SEQ + half * HALF, HALF)], start=True, stop=True)
                        mm.then_inc(s.s_pj, 1)
                    pe.wait_ge(s.s_xt, after(seq))
                    pe.wait_ge(s.s_vc, after(seq - 1))
                    for i in range(TILES):
                        mm = nc.tensor.matmul(m.psum[:, 4 + i // 4, (i % 4) * P:(i % 4 + 1) * P], s.xt[:, i * P:(i + 1) * P], s.w["vw"],
                                              start=True, stop=True)
                    mm.then_inc(s.s_v, 1)

            @block.scalar
            def _(act):
                for x in (s.s_p1, s.s_p2, s.s_p3, s.s_xt, s.s_vc):
                    act.sem_inc(x, LEAD)
                with act.Fori(0, SEQS) as seq:
                    act.wait_ge(s.s_v, after(seq - 1))
                    m.settle(act)
                    nc.scalar.activation(s.xt[:, :], m.xa[:, ds(X0 + seq * SEQ, SEQ)], ACT.Copy).then_inc(s.s_xt, 1)
                    for half in range(2):
                        n = 2 * seq + half
                        act.wait_ge(s.s_pj, after(n))
                        act.wait_ge(s.s_scr, 16 * (2 * n + LEAD))
                        nc.scalar.activation(part[:, 0, 0, :], m.psum[:, 0, :], ACT.Copy, scale=scale)
                        nc.scalar.activation(part[:, 1, 0, :], m.psum[:, 1, :], ACT.Copy).then_inc(s.s_p1, 1)
                        act.wait_ge(s.s_r1, after(n))
                        nc.scalar.activation(part[:, :, 1, :], s.rest[:, :, :], ACT.Copy).then_inc(s.s_p2, 1)
                        act.wait_ge(s.s_r2, after(n))
                        nc.scalar.activation(part[:, :, 2, :], s.rest2[:, :, :], ACT.Copy).then_inc(s.s_p3, 1)
                    act.wait_ge(s.s_v, after(seq))
                    m.settle(act)
                    for i in range(TILES):
                        ins = nc.scalar.activation(s.v[:, ds(seq * TILES + i, 1), :, 0:MLA_HD],
                                                   m.psum[:, 4 + i // 4, (i % 4) * P:(i % 4 + 1) * P].rearrange("p (h d) -> p h d", d=MLA_HD).unsqueeze(1),
                                                   ACT.Copy)
                    ins.then_inc(s.s_vc, 1)

            @block.vector
            def _(dve):
                dve.sem_inc(s.s_r1, LEAD)
                dve.sem_inc(s.s_r2, LEAD)
                with dve.Fori(0, SEQS) as seq:
                    for half in range(2):
                        n = 2 * seq + half
                        dve.wait_ge(s.s_p1, after(n))
                        dve.wait_ge(s.s_p2, after(n - 1))
                        dve.wait_ge(s.s_r2, after(n - 1))
                        nc.vector.scalar_tensor_tensor(s.rest[:, 0, :], m.psum[:, 0, :], scale, part[:, 0, 0, :], ALU.mult, ALU.subtract)
                        nc.vector.scalar_tensor_tensor(s.rest[:, 1, :], m.psum[:, 1, :], 1.0, part[:, 1, 0, :], ALU.mult, ALU.subtract).then_inc(s.s_r1, 1)
                        dve.wait_ge(s.s_p2, after(n))
                        dve.wait_ge(s.s_p3, after(n - 1))
                        nc.vector.tensor_tensor(s.rest2[:, :, :], s.rest[:, :, :], part[:, :, 1, :], ALU.subtract).then_inc(s.s_r2, 1)

            @block.sync
            def _(sp):
                sp.sem_inc(s.s_scr, 16 * LEAD)
                with sp.Fori(0, SEQS) as seq:
                    for half in range(2):
                        n = 2 * seq + half
                        sp.wait_ge(s.s_p3, after(n))
                        m.settle(sp)
                        for a in range(2):
                            sp.dma_start(scratch[a][:, :, ds(seq * SEQ + half * HALF, HALF)].rearrange("i p t -> p i t"),
                                         part[:, a, :, :]).then_inc(s.s_scr, 16)
                sp.wait_ge(s.s_scr, 16 * (4 * SEQS + LEAD))
        m.phase_end()

    def attention(self, scratch):
        nc, m, s = self.m.nc, self.m, self
        H, SH, R, NB, HB = MLA_HEADS, self.SHIFT, self.ROWS, TILES, 4
        BODIES = H // HB
        ps = m.psum
        mask_q, mask_k = s.causal[:, 0:P], s.causal[:, P:2 * P]
        np_ = [i // self.PIECE + 1 for i in range(NB)]
        base = [H * sum(np_[:i]) for i in range(NB)]
        TOTAL = H * sum(np_)

        with nc.Block() as block:
            @block.vector
            def _(dve):
                nc.vector.memset(s.qs[32:SH, :, :], 0.0)
                nc.vector.memset(s.qs[SH:R, :, :], 0.0)
                nc.vector.memset(s.neg[:, :], 0.0)
                nc.vector.memset(s.ks[32:SH, :, :], 0.0)
                nc.vector.tensor_copy(s.ks[SH:R, :, :], m.onehot[SH:R, :].unsqueeze(2).to_broadcast([H, H, SEQ]))
                nc.vector.memset(s.oc[:, :], 0.0)
        m.phase_end()

        def pieces(i):
            return [(hh, range(piece * self.PIECE, min(i + 1, (piece + 1) * self.PIECE))) for hh in range(HB) for piece in range(np_[i])]

        def number(seq, i, hb, g):
            return seq * TOTAL + base[i] + hb * HB * np_[i] + g

        def head(ap, h, a, b):
            return ap[0:R, ds(h, 1), a * P:b * P].rearrange("p h t -> p (h t)")

        def maxima_scores(pe, seq, i, hb, g):
            hh, bl = pieces(i)[g]
            h = hb * HB + hh
            pe.wait_ge(s.s_max, after(number(seq, i, hb, g) - 2))
            mm = nc.tensor.matmul(ps[:, g % 2, 0:len(bl) * P], head(s.qs, h, i, i + 1), head(s.ks, h, bl[0], bl[-1] + 1), start=True, stop=True)
            if bl[-1] == i:
                mm = nc.tensor.matmul(ps[:, g % 2, (len(bl) - 1) * P:len(bl) * P], m.ident_bf[:, :], mask_q, start=False, stop=True,
                                      skip_group_check=True)
            mm.then_inc(s.s_a, 1)

        def reduce_maxima(dve, seq, i, hb, g):
            hh, bl = pieces(i)[g]
            dve.wait_ge(s.s_a, after(number(seq, i, hb, g)))
            piece = bl[0] // self.PIECE
            nc.vector.reduce_max(s.mxp[:, ds(hb * HB + hh, 1), piece:piece + 1].rearrange("p h o -> p (h o)"),
                                 ps[:, g % 2, 0:len(bl) * P], AX_X).then_inc(s.s_max, 1)

        def finish_maxima(dve, seq, i):
            T = seq * NB + i
            dve.wait_ge(s.s_max, after(number(seq, i, BODIES, -1)))
            dve.wait_ge(s.s_negt, after(T - 1))
            if np_[i] == 2:
                nc.vector.tensor_tensor(s.mxp[:, :, 0], s.mxp[:, :, 0], s.mxp[:, :, 1], ALU.max).then_inc(s.s_negc, 1)
                dve.wait_ge(s.s_negc, after(seq * np_.count(2) + i - np_.index(2)))
            nc.vector.tensor_scalar(s.neg[:, SH:R], s.mxp[:, :, 0], -1.0, None, ALU.mult).then_inc(s.s_neg, 1)

        def transpose_maxima(pe, seq, i):
            T = seq * NB + i
            pe.wait_ge(s.s_neg, after(T))
            pe.wait_ge(s.s_out, after(T - 2 if i else T - 1))
            nc.tensor.matmul(ps[0:R, 7, 0:P], s.neg[:, :], m.ident[:, :], start=True, stop=True).then_inc(s.s_negt, 1)

        def write_shift(act, seq, i):
            act.wait_ge(s.s_negt, after(seq * NB + i))
            for hb in range(BODIES):
                nc.scalar.activation(s.qs[SH:R, hb * HB:(hb + 1) * HB, i * P:(i + 1) * P], ps[SH:R, 7, 0:P].unsqueeze(1).to_broadcast([H, HB, P]),
                                     ACT.Copy).then_inc(s.s_shift, 1)

        def shifted_scores(pe, seq, i, hb, g):
            hh, bl = pieces(i)[g]
            h = hb * HB + hh
            pe.wait_ge(s.s_e, after(number(seq, i, hb, g) - 4))
            for b in bl:
                at = (b - bl[0]) * P
                mm = nc.tensor.matmul(ps[:, 2 + g % 4, at:at + P], head(s.ks, h, b, b + 1), head(s.qs, h, i, i + 1), start=True, stop=True)
                if b == i:
                    mm = nc.tensor.matmul(ps[:, 2 + g % 4, at:at + P], m.ident_bf[:, :], mask_k, start=False, stop=True,
                                          skip_group_check=True)
            mm.then_inc(s.s_st, 1)

        def weigh(pe, seq, i, hb, g):
            hh, bl = pieces(i)[g]
            pe.wait_ge(s.s_e, after(number(seq, i, hb, g)))
            pe.wait_ge(s.s_vs, after(number(seq, i, hb, g)))
            if bl[0] == 0:
                pe.wait_ge(s.s_oc, after(H * (seq * NB + i) + hb * HB + hh - 4))
            for b in bl:
                c = b - bl[0]
                mm = nc.tensor.matmul(ps[32 * hh:32 * hh + s.VW, 6, 0:P], s.vs[:, g % 4, c, :], s.e[:, g % 4, c * P:(c + 1) * P],
                                      start=b == 0, stop=True, skip_group_check=True)
            mm.then_inc(s.s_pv, 1)

        def body(pe, seq, i, hb, last=False):
            count = len(pieces(i))
            more = len(pieces(i + 1)) if i + 1 < NB else 0
            for g in range(count):
                if g + 4 < count:
                    shifted_scores(pe, seq, i, hb, g + 4)
                elif not last:
                    if g + 4 == count:
                        pe.wait_ge(s.s_shift, after(BODIES * (seq * NB + i) + hb + 1))
                    shifted_scores(pe, seq, i, hb + 1, g + 4 - count)
                for a in range(more * min(g, 4) // 4, more * min(g + 1, 4) // 4):
                    maxima_scores(pe, seq, i + 1, hb, a)
                if last and more and count > 4 and g == count - 1:
                    transpose_maxima(pe, seq, i + 1)
                weigh(pe, seq, i, hb, g)
                if last and i and g == 1:
                    transpose_output(pe, seq * NB + i - 1)
            if last and more and count == 4:
                transpose_maxima(pe, seq, i + 1)

        def transpose_weighed(pe, T):
            pe.wait_ge(s.s_oc, after(H * T + H - 1))
            pe.wait_ge(s.s_out, after(T - 1))
            for c in range(BODIES):
                mm = nc.tensor.transpose(ps[:, 7, c * P:(c + 1) * P], s.oc[:, c * P:(c + 1) * P], m.ident[:, :])
            mm.then_inc(s.s_ot, 1)

        def transpose_output(pe, T):
            pe.wait_ge(s.s_y, after(T))
            nc.tensor.transpose(ps[:, 7, 0:P], s.y[:, :], m.ident[:, :]).then_inc(s.s_yt, 1)

        def exp_body(act, seq, i, hb):
            for g, (hh, bl) in enumerate(pieces(i)):
                act.wait_ge(s.s_st, after(number(seq, i, hb, g)))
                act.wait_ge(s.s_pv, after(number(seq, i, hb, g) - 4))
                nc.scalar.activation(s.e[:, g % 4, 0:len(bl) * P], ps[:, 2 + g % 4, 0:len(bl) * P], ACT.Exp).then_inc(s.s_e, 1)

        def copy_weighed(dve, seq, i, hb, hh):
            T = seq * NB + i
            dve.wait_ge(s.s_pv, after(number(seq, i, hb, (hh + 1) * np_[i] - 1)))
            dve.wait_ge(s.s_ot, after(T - 1))
            rows = slice(32 * hh, 32 * hh + s.VW)
            nc.vector.tensor_copy(s.oc[rows, ds(hb * P, P)], ps[rows, 6, 0:P]).then_inc(s.s_oc, 1)

        def dve_body(dve, seq, i, hb, last=False):
            more = len(pieces(i + 1)) if i + 1 < NB else 0
            for g, (hh, bl) in enumerate(pieces(i)):
                for a in range(more * min(g, 4) // 4, more * min(g + 1, 4) // 4):
                    reduce_maxima(dve, seq, i + 1, hb, a)
                if last and more and g == len(pieces(i)) - 1:
                    finish_maxima(dve, seq, i + 1)
                if bl[-1] == i:
                    copy_weighed(dve, seq, i, hb, hh)

        def copy_output(act, T):
            act.wait_ge(s.s_yt, after(T))
            m.settle(act)
            nc.scalar.activation(m.xb[:, ds(X0 + T * P, P)], ps[:, 7, 0:P], ACT.Copy).then_inc(s.s_out, 1)

        def divide(dve, T):
            dve.wait_ge(s.s_ot, after(T))
            ov = ps[:, 7, :].rearrange("p (h d) -> p h d", h=H)
            nc.vector.reciprocal(s.rden[:, :], ov[:, :, MLA_HD]).then_inc(s.s_rden, 1)
            dve.wait_ge(s.s_rden, after(T))
            dve.wait_ge(s.s_yt, after(T - 1))
            nc.vector.tensor_tensor(s.y[:, :].rearrange("p (h d) -> p h d", d=MLA_HD), ov[:, :, 0:MLA_HD],
                                    s.rden[:, :].unsqueeze(2).to_broadcast([P, H, MLA_HD]), ALU.mult).then_inc(s.s_y, 1)

        with nc.Block() as block:
            @block.sync
            def _(sp):
                with sp.Fori(0, SEQS) as seq:
                    sp.wait_ge(s.s_st, after(seq * TOTAL - 1))
                    m.settle(sp)
                    for dst, a, parts in ((s.qs, 0, s.PART_Q), (s.ks, 1, s.PART_K)):
                        for slot, i in enumerate(parts):
                            sp.dma_start(dst[slot * MLA_HD:(slot + 1) * MLA_HD, :, :],
                                         scratch[a][i, :, ds(seq * SEQ, SEQ)].rearrange("(h d) t -> d h t", d=MLA_HD)).then_inc(s.s_load, 16)

            @block.gpsimd
            def _(pool):
                pool.sem_inc(s.s_zero, LEAD)
                pool.sem_inc(s.s_vs, LEAD)
                with pool.Fori(0, SEQS) as seq:
                    pool.wait_ge(s.s_st, after(seq * TOTAL - 1))
                    pool.wait_ge(s.s_vs, after(seq * TOTAL - 1))
                    m.settle(pool)
                    nc.gpsimd.memset(s.qs[SH:R, :, :], 0.0).then_inc(s.s_zero, 1)
                    pool.wait_ge(s.s_zero, after(seq))
                    m.settle(pool)
                    for i in range(NB):
                        with pool.Fori(0, BODIES) as hb:
                            for g, (hh, bl) in enumerate(pieces(i)):
                                pool.wait_ge(s.s_pv, after(number(seq, i, hb, g) - 4))
                                m.settle(pool)
                                nc.gpsimd.tensor_copy(s.vs[:, g % 4, 0:len(bl), :],
                                                      s.v[:, ds(seq * TILES + bl[0], len(bl)), ds(hb * HB + hh, 1), :]
                                                      .rearrange("p t h d -> p t (h d)")).then_inc(s.s_vs, 1)

            @block.tensor
            def _(pe):
                for x in (s.s_a, s.s_negt, s.s_st, s.s_pv, s.s_ot, s.s_yt):
                    pe.sem_inc(x, LEAD)
                with pe.Fori(0, SEQS) as seq:
                    pe.wait_ge(s.s_load, 16 * 12 * (seq + 1))
                    pe.wait_ge(s.s_zero, after(seq))
                    m.settle(pe)
                    with pe.Fori(0, BODIES) as hb:
                        for g in range(HB):
                            maxima_scores(pe, seq, 0, hb, g)
                    transpose_maxima(pe, seq, 0)
                    for i in range(NB):
                        T = seq * NB + i
                        pe.wait_ge(s.s_shift, after(BODIES * T))
                        for g in range(4):
                            shifted_scores(pe, seq, i, 0, g)
                        if i:
                            pe.wait_ge(s.s_shift, after(BODIES * T + BODIES - 1))
                            transpose_weighed(pe, T - 1)
                        m.settle(pe)
                        with pe.Fori(0, BODIES - 1) as hb:
                            body(pe, seq, i, hb)
                        body(pe, seq, i, BODIES - 1, last=True)
                    transpose_weighed(pe, seq * NB + NB - 1)
                    transpose_output(pe, seq * NB + NB - 1)

            @block.scalar
            def _(act):
                act.preload_act_table(ACT.Exp)
                for x in (s.s_shift, s.s_e, s.s_out):
                    act.sem_inc(x, LEAD)
                with act.Fori(0, SEQS) as seq:
                    write_shift(act, seq, 0)
                    for i in range(NB):
                        with act.Fori(0, BODIES - 1) as hb:
                            exp_body(act, seq, i, hb)
                        exp_body(act, seq, i, BODIES - 1)
                        if i:
                            copy_output(act, seq * NB + i - 1)
                        if i + 1 < NB:
                            write_shift(act, seq, i + 1)
                    copy_output(act, seq * NB + NB - 1)

            @block.vector
            def _(dve):
                for x in (s.s_max, s.s_negc, s.s_neg, s.s_oc, s.s_rden, s.s_y):
                    dve.sem_inc(x, LEAD)
                with dve.Fori(0, SEQS) as seq:
                    with dve.Fori(0, BODIES) as hb:
                        for g in range(HB):
                            reduce_maxima(dve, seq, 0, hb, g)
                    finish_maxima(dve, seq, 0)
                    for i in range(NB):
                        T = seq * NB + i
                        dve.wait_ge(s.s_neg, after(T))
                        m.settle(dve)
                        with dve.Fori(0, BODIES - 1) as hb:
                            dve_body(dve, seq, i, hb)
                        if i:
                            divide(dve, T - 1)
                        dve_body(dve, seq, i, BODIES - 1, last=True)
                    divide(dve, seq * NB + NB - 1)
        m.phase_end()


class Gru:

    ROWS = 2 * DI

    def __init__(self, m):
        self.m = m
        sb, sem = m.sb, m.sem
        self.taps, top = m.carve(SCRATCH, [P, CONV, P])
        self.pwt, top = m.carve(top, [P, P])
        self.cols, top = m.carve(top, [P, 16])
        self.gain, top = m.carve(top, [P, 4])
        self.cbias, top = m.carve(top, [P, 1])
        self.w_hg, top = m.carve(top, [P, 4, self.ROWS])
        self.w_out, top = m.carve(top, [self.ROWS, 2, P])
        R = self.ROWS
        self.sg, at = m.carve(0, [R, 2, HALF])
        self.a, at = m.carve(at, [R, 2, HALF])
        self.sh, at = m.carve(at, [R, 2, HALF])
        self.g, at = m.carve(at, [R, 2, HALF])
        self.v, at = m.carve(at, [R, 2, HALF])
        self.h, at = m.carve(at, [R, 2, 2, HALF])
        self.s_load = sem("gru_s_load")
        self.s_taps = sem("gru_s_taps")
        self.s_cb = sem("gru_s_cb")
        self.s_cbc = sem("gru_s_cbc")
        self.s_conv = sem("gru_s_conv")
        self.s_x = sem("gru_s_x")
        self.s_up = sem("gru_s_up")
        self.s_sg = sem("gru_s_sg")
        self.s_a = sem("gru_s_a")
        self.s_sh = sem("gru_s_sh")
        self.s_m = sem("gru_s_m")
        self.s_g = sem("gru_s_g")
        self.s_v = sem("gru_s_v")
        self.s_h = sem("gru_s_h")
        self.s_out = sem("gru_s_out")

    def setup(self, t):
        nc, m, s = self.m.nc, self.m, self
        with nc.Block() as block:
            @block.sync
            def _(sp):
                for dst, name in ((s.pwt, "gru_pwT"), (s.cols[:, 0:9], "gru_cols"), (s.w_hg, "gru_hg"), (s.w_out, "gru_out")):
                    sp.dma_start(dst, t[name]).then_inc(s.s_load, 16)

            @block.vector
            def _(dve):
                dve.wait_ge(s.s_load, 64)
                for j in range(CONV):
                    nc.vector.tensor_scalar(s.taps[:, j, :], s.pwt[:, :], s.cols[:, j:j + 1], None, ALU.mult)
                nc.vector.tensor_scalar(s.gain[:, 0:3], s.cols[:, 6:9], 1.0, None, ALU.add)
                nc.vector.memset(m.hn[:, TOK:TOK + HALF], 0.0)
                dve.wait_ge(s.s_cb, 1)
                nc.vector.tensor_tensor(s.cbias[:, :], m.psum[:, 0, 0:1], s.cols[:, 5:6], ALU.add)

            @block.tensor
            def _(pe):
                pe.wait_ge(s.s_load, 64)
                nc.tensor.matmul(m.psum[:, 0, 0:1], s.pwt[:, :], s.cols[:, 4:5], start=True, stop=True).then_inc(s.s_cb, 1)
        m.phase_end()

    def conv(self):
        nc, m, s = self.m.nc, self.m, self
        with nc.Block() as block:
            @block.tensor
            def _(pe):
                pe.sem_inc(s.s_conv, LEAD)
                with pe.Fori(0, SEQS) as seq:
                    for half in range(2):
                        n = 2 * seq + half
                        pe.wait_ge(s.s_x, after(n - 2))
                        for j in range(CONV - 1, -1, -1):
                            lag = CONV - 1 - j
                            at = seq * SEQ + half * HALF - lag
                            cut = lag if half == 0 else 0
                            mm = nc.tensor.matmul(m.psum[:, half, cut:HALF], s.taps[:, j, :], m.hn[:, ds(at + cut, HALF - cut)],
                                                  start=lag == 0, stop=True, skip_group_check=True)
                        mm.then_inc(s.s_conv, 1)

            @block.vector
            def _(dve):
                dve.sem_inc(s.s_x, LEAD)
                with dve.Fori(0, SEQS) as seq:
                    for half in range(2):
                        n = 2 * seq + half
                        here = ds(X0 + seq * SEQ + half * HALF, HALF)
                        dve.wait_ge(s.s_conv, after(n))
                        nc.vector.scalar_tensor_tensor(m.xb[:, here], m.psum[:, half, :], s.cbias[:, 0:1], m.xa[:, here],
                                                       ALU.add, ALU.add).then_inc(s.s_x, 1)
        m.phase_end()

    def recurrence(self):
        nc, m, s, R = self.m.nc, self.m, self, self.ROWS
        hid, gate, down = m.psum[0:R, 0:2, :], m.psum[0:R, 2:4, :], m.psum[:, 4:6, :]
        with nc.Block() as block:
            @block.tensor
            def _(pe):
                pe.sem_inc(s.s_up, LEAD)
                pe.sem_inc(s.s_out, LEAD)

                def up(n, at):
                    pe.wait_ge(s.s_a, after(n - 1))
                    for c in range(2):
                        nc.tensor.matmul(gate[:, c, :], s.w_hg[:, 2 + c, :], m.hn[:, at], start=True, stop=True)
                    pe.wait_ge(s.s_g, after(n - 1))
                    for c in range(2):
                        mm = nc.tensor.matmul(hid[:, c, :], s.w_hg[:, c, :], m.hn[:, at], start=True, stop=True)
                    mm.then_inc(s.s_up, 1)

                up(0, ds(0, HALF))
                with pe.Fori(0, SEQS) as seq:
                    for half in range(2):
                        n = 2 * seq + half
                        up(n + 1, ds((n + 1) * HALF, HALF))
                        pe.wait_ge(s.s_h, after(n))
                        pe.wait_ge(s.s_x, after(n - 2))
                        for c in range(2):
                            mm = nc.tensor.matmul(down[:, half, :], s.w_out[:, c, :], s.h[:, half, c, :], start=c == 0, stop=True, skip_group_check=True)
                        mm.then_inc(s.s_out, 1)

            @block.scalar
            def _(act):
                act.preload_act_table(ACT.Sigmoid)
                for x in (s.s_sg, s.s_a, s.s_sh):
                    act.sem_inc(x, LEAD)
                with act.Fori(0, SEQS * 2) as n:
                    act.wait_ge(s.s_up, after(n))
                    act.wait_ge(s.s_m, after(n - 1))
                    nc.scalar.activation(s.sh[:, :, :], hid, ACT.Sigmoid).then_inc(s.s_sh, 1)
                    act.wait_ge(s.s_v, after(n - 1))
                    nc.scalar.activation(s.sg[:, :, :], gate, ACT.Sigmoid).then_inc(s.s_sg, 1)
                    act.wait_ge(s.s_h, after(n - 1))
                    nc.scalar.activation(s.a[:, :, :], gate, ACT.Sigmoid, scale=-1.0).then_inc(s.s_a, 1)

            @block.vector
            def _(dve):
                for x in (s.s_m, s.s_g, s.s_v, s.s_h, s.s_x):
                    dve.sem_inc(x, LEAD)

                def add(n, half):
                    dve.wait_ge(s.s_out, after(n))
                    here = ds(X0 + n * HALF, HALF)
                    nc.vector.tensor_tensor(m.xa[:, here], down[:, half, :], m.xb[:, here], ALU.add).then_inc(s.s_x, 1)

                with dve.Fori(0, SEQS) as seq:
                    for half in range(2):
                        n = 2 * seq + half
                        dve.wait_ge(s.s_sh, after(n))
                        dve.wait_ge(s.s_v, after(n - 1))
                        nc.vector.tensor_scalar(s.g[:, :, :], s.sh[:, :, :], 0.5, None, ALU.min).then_inc(s.s_m, 1)
                        dve.wait_ge(s.s_m, after(n))
                        nc.vector.scalar_tensor_tensor(s.v[:, :, :], hid, 0.0, s.g[:, :, :], ALU.max, ALU.add).then_inc(s.s_g, 1)
                        dve.wait_ge(s.s_g, after(n))
                        dve.wait_ge(s.s_sg, after(n))
                        nc.vector.tensor_tensor(s.g[:, :, :], s.v[:, :, :], s.sg[:, :, :], ALU.mult).then_inc(s.s_v, 1)
                        dve.wait_ge(s.s_v, after(n))
                        dve.wait_ge(s.s_a, after(n))
                        dve.wait_ge(s.s_out, after(n - 2))
                        dve.wait_ge(s.s_h, after(n - 1))
                        for c in range(2):
                            ins = nc.vector.tensor_tensor_scan(s.h[:, half, c, :], s.a[:, c, :], s.g[:, c, :],
                                                               0.0 if half == 0 else s.h[:, 0, c, HALF - 1:HALF], ALU.mult, ALU.add)
                        ins.then_inc(s.s_h, 1)
                        add(n, half)
        m.phase_end()


def shape_constants():
    f = np.float32
    eye = np.eye(P, dtype=f)
    center = eye - f(1.0 / P)
    upper = (np.arange(P) >= HD)[:, None]
    parts = [eye, center, np.where(upper, f(0), center), np.where(upper, center, f(0)), np.full((P, P), 1.0 / P, f)]
    out = {"squares": np.concatenate(parts, 1).astype(f)}
    i = np.arange(P)
    for name, c in LOCAL.items():
        W = c["window"]
        lag = i[:, None] - i[None, :]
        own = np.where((lag >= 0) & (lag <= W), 0, MASKED)
        prior = np.full((P, HD), MASKED)
        prior[0:W, 0:W] = np.where(i[:W, None] <= i[None, :W], 0, MASKED)
        out["masks_" + name] = np.concatenate([own, prior], 1).astype(f)
        half = np.arange(0, HD, 2, dtype=f)
        inv_freq = (f(1.0) / f(10000.0) ** (half / f(HD))).astype(f)
        t = np.arange(SEQ, dtype=f)
        freqs = t[:, None] * inv_freq[None, :]
        base = ((half + f(0.4 * HD)) / f(1.4 * HD)).astype(f)
        power = ((t - f(SEQ // 2)) / f(W // 2)).astype(f)
        scale = (base[None, :] ** power[:, None]).astype(f)
        cos, sin = np.cos(freqs).astype(f), np.sin(freqs).astype(f)
        tabs = []
        for s in (scale * f(8.0), f(1.0) / scale):
            tabs += [np.concatenate([cos * s, cos * s], 1), np.concatenate([-sin * s, sin * s], 1)]
        tab = np.stack(tabs).astype(f).reshape(4, TILES, P, HD).transpose(2, 0, 1, 3)
        out["rope_" + name] = np.ascontiguousarray(np.concatenate([tab, tab[:, :, 0:AHEAD]], 2))
    flags = np.zeros((P, 3, ROPE_TILES), f)
    flags[:, 2] = 3e38
    flags[:, 2, [0, TILES]] = -3e38
    flags[:, 0, [0, TILES]] = MASKED
    flags[:, 1] = 1
    flags[:, 1, [0, TILES]] = 0
    out["flags"] = flags
    one = np.zeros((P, MLA_HEADS), f)
    one[Mla.SHIFT:Mla.SHIFT + MLA_HEADS] = np.eye(MLA_HEADS, dtype=f)
    out["onehot"] = one
    causal = np.where(i[:, None] >= i[None, :], 0, MASKED).astype(f)
    out["causal"] = np.concatenate([causal, causal.T], 1)
    return out


def ffn_vectors(gain, bias, b2, b1):
    import numpy as np
    L = gain.shape[0]
    v = np.zeros((L, P, 9), np.float32)
    v[:, :, 0], v[:, :, 1], v[:, :, 2] = gain, bias, b2
    for c in range(3):
        v[:, 0:HC[c], 3 + c] = b1[:, HO[c]:HO[c] + HC[c]]
        v[:, 0:HC[c], 6 + c] = b1[:, HID + HO[c]:HID + HO[c] + HC[c]]
    return v


def local_layout(d, pre, up):
    import numpy as np
    qk = np.stack([d[f"{pre}_ffn_q_scale"], d[f"{pre}_ffn_k_scale"]], 1)
    names = ("Wqkv", "Wo", "W1", "b1", "W2", "b2") if up else ("wqkv", "wo", "w1", "b1", "w2", "b2")
    wqkv, wo, w1, b1, w2, b2 = (d[f"{pre}_ffn_{n}"] for n in names)
    return {
        f"{pre}_wqkv": wqkv, f"{pre}_wo": wo, f"{pre}_w1": w1, f"{pre}_w2": w2,
        f"{pre}_scale_qk": np.ascontiguousarray(np.broadcast_to(qk[:, None], (len(qk), P, 2, HD))),
        f"{pre}_vec": ffn_vectors(d[f"{pre}_ffn_ln_g"], d[f"{pre}_ffn_ln_b"], b2, b1),
    }


def gru_layout(d):
    import numpy as np
    g = {k[len("L1_attn_"):]: v for k, v in d.items() if k.startswith("L1_attn_")}
    cols = np.concatenate([g["dw_w"][:, 0, :], np.stack([g["dw_b"], g["pw_b"], g["conv_gamma"], g["gru_gamma"], g["ff_gamma"]], 1)], 1)
    heads, hd = g["w_hg"].shape[0], g["w_hg"].shape[1]
    hg = np.zeros((P, 4, 2 * DI), np.float32)
    wo = np.zeros((2 * DI, 2, P), np.float32)
    for h in range(heads):
        pair, col = h // 2, (h % 2) * DI
        hg[h * hd:(h + 1) * hd, pair, col:col + DI] = g["w_hg"][h, :, 0:DI]
        hg[h * hd:(h + 1) * hd, 2 + pair, col:col + DI] = g["w_hg"][h, :, DI:]
        wo[col:col + DI, pair, h * hd:(h + 1) * hd] = g["w_out"][h]
    return {"gru_pwT": g["pw_w"].T, "gru_cols": cols, "gru_hg": hg, "gru_out": wo,
            "gru_w1": np.concatenate([g["w_value"], g["w_gate"]], 1), "gru_w2": g["w_ff_out"], "gru_vec": np.zeros((P, 9), np.float32)}


def build(nc, t, out, stages=("mla", "L0", "gru", "L1")):
    with ExitStack() as ctx:
        m = Machine(nc, ctx)
        norm, ffn, att, mla, gru = Norm(m), Ffn(m), Windowed(m), Mla(m), Gru(m)
        loaded = ctx.enter_context(nc.semaphore("loaded"))
        stored = ctx.enter_context(nc.semaphore("stored"))
        scratch = nc.dram_tensor("parts", (2, 3, P, TOK), BF16, kind="Internal").ap()
        mask_f = m.sb("mask_f", [P, 2 * P])
        zeroed = m.sem("zeroed")

        with nc.Block() as block:
            @block.sync
            def _(sp):
                n = 0
                for dst, src in [(m.ident, 0), (m.center, 1), (m.center_a, 2), (m.center_b, 3), (m.mean, 4)]:
                    sp.dma_start(dst[:, :], t["squares"][:, src * P:(src + 1) * P]).then_inc(loaded, 16)
                sp.dma_start(att.prior_off[:, :], t["flags"][:, 0, :]).then_inc(loaded, 16)
                sp.dma_start(att.keep[:, :], t["flags"][:, 1, :]).then_inc(loaded, 16)
                sp.dma_start(att.prior_cap[:, :], t["flags"][:, 2, :]).then_inc(loaded, 16)
                sp.dma_start(m.onehot[:, :], t["onehot"]).then_inc(loaded, 16)
                sp.dma_start(mask_f[:, 0:2 * P], t["causal"]).then_inc(loaded, 16)
                sp.dma_start(m.xa[:, X0:X0 + TOK], t["xT"]).then_inc(loaded, 16)
                sp.dma_start(m.xres[:, X0:X0 + TOK], t["xT"]).then_inc(loaded, 16)
                sp.wait_ge(loaded, 12 * 16)

            @block.vector
            def _(dve):
                dve.wait_ge(loaded, 12 * 16)
                nc.vector.tensor_copy(m.ident_bf[:, :], m.ident[:, :])
                nc.vector.memset(m.xa[:, 0:X0], 0.0)
                nc.vector.memset(m.xa[:, X0 + TOK:X0 + TOK + PAD], 0.0)
                nc.vector.memset(m.xb[:, 0:X0], 0.0)
                nc.vector.tensor_copy(mla.causal[:, :], mask_f[:, 0:2 * P])
                nc.vector.memset(att.o[:, :], 0.0)
        m.phase_end()

        def family_start(pre):
            with nc.Block() as block:
                @block.sync
                def _(sp):
                    sp.dma_start(att.rope[:, :, :, :], t["rope_" + pre]).then_inc(att.s_load, 16)
                    sp.dma_start(mask_f[:, 0:P + HD], t["masks_" + pre]).then_inc(att.s_load, 16)
                    sp.wait_ge(att.s_load, 32)

                @block.vector
                def _(dve):
                    dve.wait_ge(att.s_load, 32)
                    nc.vector.tensor_copy(att.masks[:, :], mask_f[:, 0:P + HD])
                    nc.vector.memset(att.ep[:, :, :], 0.0)
                    nc.vector.memset(att.v[:, :, :, :], 1.0)
                    nc.vector.memset(m.hn[:, TOK:TOK + HALF], 0.0)

                @block.gpsimd
                def _(pool):
                    nc.gpsimd.memset(att.kt[:, :, :, :, :], 0.0)
            m.phase_end()

        def windowed_family(pre):
            c = LOCAL[pre]
            G, L = c["groups"], c["layers"]
            family_start(pre)
            wqkv, wo = t[pre + "_wqkv"], t[pre + "_wo"].rearrange("l (c p) n -> l p c n", p=P)
            with nc.Fori(0, L) as layer:
                def one(ap):
                    return ap[ds(layer, 1)][0]

                with nc.Block() as block:
                    @block.sync
                    def _(sp):
                        att.load(sp, one(wqkv), one(wo), one(t[pre + "_scale_qk"]), 4 * G)
                m.phase_end()
                att.scale_tables()
                att.phase(G, c["window"], sp_work=lambda sp: ffn.load(sp, one(t[pre + "_w1"]), one(t[pre + "_w2"]), one(t[pre + "_vec"])))
                norm.phase("layer", terms=[(m.center_a, m.xb, False), (m.center_b, m.xb, True)], gain=ffn.vec[:, 0:1],
                           bias=ffn.vec[:, 1:2], out=m.hn)
                ffn.phase(m.xb, m.xa, ACT.Gelu)

        def outer_norm():
            norm.phase("layer", terms=[(m.center, m.xres, False), (m.center, m.xa, False)], out=m.xa, out_at=X0, out2=m.xres)

        if "mla" in stages:
            mla.weights(t)
            with nc.Block() as block:
                @block.vector
                def _(dve):
                    nc.vector.memset(m.hn[:, :], 1.0)
            m.phase_end()
            mla.projections(scratch)
            mla.attention(scratch)
            norm.phase("layer", terms=[(m.center, m.xres, False), (m.center, m.xb, False)], out=m.xa, out_at=X0, out2=m.xres)
        if "L0" in stages:
            windowed_family("L0")
            outer_norm()
        if "gru" in stages:
            gru.setup(t)
            with nc.Block() as block:
                @block.sync
                def _(sp):
                    ffn.load(sp, t["gru_w1"], t["gru_w2"], t["gru_vec"])
            m.phase_end()
            norm.phase("rms", src=m.xa, gain=gru.gain[:, 0:1], out=m.hn)
            gru.conv()
            norm.phase("rms", src=m.xb, gain=gru.gain[:, 1:2], out=m.hn)
            gru.recurrence()
            norm.phase("rms", src=m.xa, gain=gru.gain[:, 2:3], out=m.hn)
            ffn.phase(m.xa, m.xa, ACT.Silu)
            outer_norm()
        if "L1" in stages:
            windowed_family("L1")
            outer_norm()

        with nc.Block() as block:
            @block.sync
            def _(sp):
                sp.dma_start(out, m.xa[:, X0:X0 + TOK]).then_inc(stored, 16)
                sp.wait_ge(stored, 16)


def host_arrays(d):
    import numpy as np
    d = {k: np.asarray(v) for k, v in d.items()}
    a = {"xT": d["L0_attn_x"].reshape(TOK, P).T}
    a.update(local_layout(d, "L0", True))
    a.update(local_layout(d, "L1", False))
    a.update(gru_layout(d))
    a.update({"mla_dq": d["L0_attn_W_dq"], "mla_uqT": d["L0_attn_W_uq"].T, "mla_dkv": d["L0_attn_W_dkv"],
              "mla_uk": d["L0_attn_W_uk"], "mla_uv": d["L0_attn_W_uv"], "mla_oT": d["L0_attn_W_o"].T})
    a.update(shape_constants())
    return {k: np.ascontiguousarray(v) for k, v in a.items()}


def kernel(**inputs):
    import concourse.bacc as bacc
    from concourse.bass_utils import run_bass_kernel_spmd

    nc = bacc.Bacc("TRN2", target_bir_lowering=False, num_devices=1)
    arrays = host_arrays(inputs)
    t = {k: nc.dram_tensor(f"in_{k}", v.shape, mybir.dt.from_np(v.dtype), kind="ExternalInput").ap() for k, v in arrays.items()}
    out = nc.dram_tensor("out_x", (P, TOK), F32, kind="ExternalOutput").ap()
    build(nc, t, out)
    r = run_bass_kernel_spmd(nc, [{f"in_{k}": v for k, v in arrays.items()}], core_ids=[0])
    return r.results[0]["out_x"].T.reshape(SEQS, SEQ, P)
```

```python
from contextlib import ExitStack

import numpy as np
import concourse.bass as bass
from concourse import mybir

F32 = mybir.dt.float32
BF16 = mybir.dt.bfloat16
ALU = mybir.AluOpType
ACT = mybir.ActivationFunctionType
AX_X = mybir.AxisListType.X
ds = bass.ds

P = 128
SEQS, SEQ = 4, 1024
TOK = SEQS * SEQ
TILES = SEQ // P
HALF = 512
X0 = P
PAD = 3 * P
HD = 64
GH = 8
GW = GH * HD
SCRATCH = 10 * 1024
ARENA = 27 * 1024
LEAD = 4
MASKED = -1e30
OFF = -3e38
HID = int(P * 4 * 2 / 3)
HC = [114, 114, 113]
HO = [0, 114, 228]
NORM_EPS = 1e-5
MLA_HEADS, MLA_HD, MLA_LAT = 16, 8, 64
DI = 48
CONV = 4
LOCAL = {"L0": dict(layers=6, groups=2, window=32), "L1": dict(layers=2, groups=1, window=64)}
AHEAD = 3
ROPE_TILES = TILES + AHEAD


def after(n):
    return n + 1 + LEAD


class Machine:

    def __init__(self, nc, ctx):
        self.nc, self.ctx = nc, ctx
        self.sems = []
        self.settled = self.sem("settled")
        sb = self.sb
        self.xa = sb("xa", [P, X0 + TOK + PAD])
        self.xb = sb("xb", [P, X0 + TOK])
        self.xres = sb("xres", [P, X0 + TOK])
        self.hn = sb("hn", [P, TOK + HALF])
        self.ident = sb("ident", [P, P])
        self.center = sb("center", [P, P])
        self.center_a = sb("center_a", [P, P])
        self.center_b = sb("center_b", [P, P])
        self.mean = sb("mean", [P, P])
        self.onehot = sb("onehot", [P, MLA_HEADS])
        self.ident_bf = sb("ident_bf", [P, P], BF16)
        self.arena = sb("arena", [P, ARENA])
        self.psum = ctx.enter_context(nc.psum_tensor("psum", [P, 8, HALF], F32))

    def sb(self, name, shape, dt=F32):
        return self.ctx.enter_context(self.nc.sbuf_tensor(name, shape, dt))

    def carve(self, at, shape):
        size = int(np.prod(shape[1:]))
        assert at + size <= ARENA
        ap = self.arena[0:shape[0], at:at + size]
        if len(shape) > 2:
            names = "abcd"[:len(shape) - 1]
            ap = ap.rearrange(f"p ({' '.join(names)}) -> p {' '.join(names)}", **dict(zip(names, shape[1:])))
        return ap, at + size

    def sem(self, name):
        s = self.ctx.enter_context(self.nc.semaphore(name))
        self.sems.append(s)
        return s

    def settle(self, eng):
        eng.sem_inc(self.settled, 1)

    def phase_end(self):
        nums = sorted(s.num for s in self.sems)
        self.nc.all_engine_barrier(sems_to_clear=range(nums[0], nums[-1] + 1))


class Norm:

    def __init__(self, m):
        self.m = m
        self.sq, at = m.carve(0, [P, 2, HALF])
        self.lnv, at = m.carve(at, [P, 2, HALF])
        self.y0, at = m.carve(at, [P, 2, HALF])
        self.t1, at = m.carve(at, [P, 2, HALF])
        self.t2, at = m.carve(at, [P, 2, HALF])
        self.t3, at = m.carve(at, [P, 2, HALF])
        self.un, at = m.carve(at, [P, 2, HALF])
        self.fl, at = m.carve(at, [P, 2, HALF])
        self.s_cen = m.sem("norm_centred")
        self.s_sq = m.sem("norm_squared")
        self.s_var = m.sem("norm_variance")
        self.s_floor = m.sem("norm_floored")
        self.s_ln = m.sem("norm_ln")
        self.s_y0 = m.sem("norm_guess")
        self.s_t1 = m.sem("norm_newton1")
        self.s_t2 = m.sem("norm_newton2")
        self.s_t3 = m.sem("norm_newton3")
        self.s_un = m.sem("norm_scaled")
        self.s_out = m.sem("norm_written")

    def phase(self, kind, terms=None, src=None, gain=None, bias=None, out=None, out_at=0, out2=None, sp_work=None):
        nc, m, s = self.m.nc, self.m, self
        layer = kind == "layer"
        ln_scale = 2.0 ** 24
        floor = 1e-24 / P
        eps = NORM_EPS if layer else 0.0
        CH = TOK // HALF
        pairs = [(n, n + 1) for n in range(0, CH, 2)]

        def cen(n):
            return m.psum[:, n % 4, :]

        def var(n):
            return m.psum[:, 4 + n % 4, :]

        def chunk(buf, n, at=X0):
            return buf[:, at + n * HALF:at + (n + 1) * HALF]

        with nc.Block() as block:
            if sp_work:
                block.sync(sp_work)

            @block.tensor
            def _(pe):
                pe.sem_inc(s.s_cen, LEAD)
                pe.sem_inc(s.s_var, LEAD)
                for pair in pairs:
                    for n in pair:
                        if not layer:
                            break
                        pe.wait_ge(s.s_un, after(n - 4))
                        for i, (mat, buf, shifted) in enumerate(terms):
                            cut = 1 if shifted and n % 2 == 0 else 0
                            at = X0 + n * HALF + cut - shifted
                            mm = nc.tensor.matmul(cen(n)[:, cut:HALF], mat[:, :], buf[:, at:at + HALF - cut], start=i == 0, stop=True,
                                                  skip_group_check=True)
                        mm.then_inc(s.s_cen, 1)
                    for n in pair:
                        pe.wait_ge(s.s_sq, after(n))
                        pe.wait_ge(s.s_t1, after(n - 4))
                        nc.tensor.matmul(var(n), m.mean[:, :], s.sq[:, n % 2, :], start=True, stop=True, skip_group_check=True).then_inc(s.s_var, 1)

            @block.scalar
            def _(act):
                act.preload_act_table_set("natural_log_exp_and_others")
                for x in (s.s_sq, s.s_ln, s.s_y0, s.s_out):
                    act.sem_inc(x, LEAD)

                def finish(n):
                    act.wait_ge(s.s_un, after(n))
                    if gain is not None:
                        nc.scalar.activation(chunk(out, n, out_at), s.un[:, n % 2, :], ACT.Identity, scale=gain,
                                             bias=bias if bias is not None else 0.0).then_inc(s.s_out, 1)
                    else:
                        nc.scalar.activation(chunk(out, n, out_at), s.un[:, n % 2, :], ACT.Copy).then_inc(s.s_out, 1)

                for pair in pairs:
                    for n in pair:
                        act.wait_ge(s.s_var, after(n - 2))
                        if layer:
                            act.wait_ge(s.s_cen, after(n))
                        nc.scalar.activation(s.sq[:, n % 2, :], cen(n) if layer else chunk(src, n), ACT.Square).then_inc(s.s_sq, 1)
                    for n in pair:
                        if n >= 2:
                            finish(n - 2)
                    for n in pair:
                        act.wait_ge(s.s_var if layer else s.s_floor, after(n))
                        act.wait_ge(s.s_y0, after(n - 2))
                        nc.scalar.activation(s.lnv[:, n % 2, :], var(n) if layer else s.fl[:, n % 2, :], ACT.Ln, scale=ln_scale,
                                             bias=eps * ln_scale).then_inc(s.s_ln, 1)
                    for n in pair:
                        act.wait_ge(s.s_ln, after(n))
                        act.wait_ge(s.s_t3, after(n - 2))
                        nc.scalar.activation(s.y0[:, n % 2, :], s.lnv[:, n % 2, :], ACT.Exp, scale=-0.5,
                                             bias=12 * float(np.log(2.0))).then_inc(s.s_y0, 1)
                for n in pairs[-1]:
                    finish(n)

            @block.vector
            def _(dve):
                for x in (s.s_floor, s.s_t1, s.s_t2, s.s_t3, s.s_un):
                    dve.sem_inc(x, LEAD)

                def floored(pair):
                    for n in pair:
                        dve.wait_ge(s.s_var, after(n))
                        dve.wait_ge(s.s_ln, after(n - 2))
                        nc.vector.tensor_scalar(s.fl[:, n % 2, :], var(n), floor, None, ALU.max).then_inc(s.s_floor, 1)

                if not layer:
                    floored(pairs[0])
                for i, pair in enumerate(pairs):
                    for n in pair:
                        dve.wait_ge(s.s_y0, after(n))
                        dve.wait_ge(s.s_t2, after(n - 2))
                        nc.vector.scalar_tensor_tensor(s.t1[:, n % 2, :], var(n), eps if layer else floor, s.y0[:, n % 2, :],
                                                       ALU.add if layer else ALU.max, ALU.mult).then_inc(s.s_t1, 1)
                    if not layer and i + 1 < len(pairs):
                        floored(pairs[i + 1])
                    for n in pair:
                        dve.wait_ge(s.s_t1, after(n))
                        dve.wait_ge(s.s_t3, after(n - 2))
                        nc.vector.scalar_tensor_tensor(s.t2[:, n % 2, :], s.t1[:, n % 2, :], -0.5, s.y0[:, n % 2, :],
                                                       ALU.mult, ALU.mult).then_inc(s.s_t2, 1)
                    for n in pair:
                        dve.wait_ge(s.s_t2, after(n))
                        dve.wait_ge(s.s_un, after(n - 2))
                        nc.vector.scalar_tensor_tensor(s.t3[:, n % 2, :], s.t2[:, n % 2, :], 1.5, s.y0[:, n % 2, :],
                                                       ALU.add, ALU.mult).then_inc(s.s_t3, 1)
                    for n in pair:
                        dve.wait_ge(s.s_t3, after(n))
                        dve.wait_ge(s.s_out, after(n - 2))
                        nc.vector.tensor_tensor(s.un[:, n % 2, :], cen(n) if layer else chunk(src, n), s.t3[:, n % 2, :],
                                                ALU.mult).then_inc(s.s_un, 1)

            if out2 is not None:
                @block.gpsimd
                def _(pool):
                    for n in range(CH):
                        pool.wait_ge(s.s_out, after(n))
                        nc.gpsimd.tensor_copy(chunk(out2, n, out_at), chunk(out, n, out_at))
        m.phase_end()


class Ffn:

    def __init__(self, m):
        self.m = m
        self.w1 = m.sb("ffn_w1", [P, 2 * HID])
        self.w2 = m.sb("ffn_w2", [HC[0], 3, P])
        self.vec = m.sb("ffn_vec", [P, 9])
        self.gate, at = m.carve(0, [HC[0], 3, HALF])
        self.u, at = m.carve(at, [HC[0], 3, HALF])
        self.s_load = m.sem("ffn_loaded")
        self.s_gp = m.sem("ffn_gate_products")
        self.s_ap = m.sem("ffn_value_products")
        self.s_gate = m.sem("ffn_gates")
        self.s_u = m.sem("ffn_gated")
        self.s_down = m.sem("ffn_down")
        self.s_x = m.sem("ffn_added")

    def load(self, sp, w1, w2, vec):
        sp.dma_start(self.w1[:, :], w1).then_inc(self.s_load, 16)
        sp.dma_start(self.w2[:, 0:2, :], w2[0:HO[2], :].rearrange("(c p) n -> p c n", c=2)).then_inc(self.s_load, 16)
        sp.dma_start(self.w2[0:HC[2], 2, :], w2[HO[2]:HID, :]).then_inc(self.s_load, 16)
        sp.dma_start(self.vec[:, :], vec).then_inc(self.s_load, 16)
        sp.wait_ge(self.s_load, 64)

    def phase(self, src, dst, func, sp_work=None, pool_work=None):
        nc, m, s = self.m.nc, self.m, self
        CH = TOK // HALF
        avals, gates, down = m.psum[:, 0:3, :], m.psum[:, 3:6, :], m.psum[:, 6, :]
        off = dict(a=0, g=HID)
        with nc.Block() as block:
            if sp_work:
                block.sync(sp_work)
            if pool_work:
                block.gpsimd(pool_work)

            @block.tensor
            def _(pe):
                for x in (s.s_gp, s.s_ap, s.s_down):
                    pe.sem_inc(x, LEAD)

                def up(which, bank, n, at):
                    for c in range(3):
                        if which == "g":
                            pe.wait_ge(s.s_gate, after(3 * (n - 1) + c))
                        else:
                            pe.wait_ge(s.s_u, after(3 * (n - 1) + c))
                        nc.tensor.matmul(bank[0:HC[c], c, :], s.w1[:, off[which] + HO[c]:off[which] + HO[c] + HC[c]],
                                         m.hn[:, at], start=True, stop=True, skip_group_check=True).then_inc(s.s_gp if which == "g" else s.s_ap, 1)

                up("g", gates, 0, ds(0, HALF))
                up("a", avals, 0, ds(0, HALF))
                with pe.Fori(0, CH) as n:
                    up("g", gates, n + 1, ds((n + 1) * HALF, HALF))
                    pe.wait_ge(s.s_x, after(n - 1))
                    for c in range(3):
                        pe.wait_ge(s.s_u, after(3 * n + c))
                        mm = nc.tensor.matmul(down, s.w2[0:HC[c], c, :], s.u[0:HC[c], c, :], start=c == 0, stop=True, skip_group_check=True)
                    mm.then_inc(s.s_down, 1)
                    up("a", avals, n + 1, ds((n + 1) * HALF, HALF))

            @block.scalar
            def _(act):
                act.preload_act_table(func)
                act.sem_inc(s.s_gate, LEAD)
                with act.Fori(0, CH) as n:
                    for c in range(3):
                        act.wait_ge(s.s_gp, after(3 * n + c))
                        act.wait_ge(s.s_u, after(3 * (n - 1) + c))
                        nc.scalar.activation(s.gate[0:HC[c], c, :], gates[0:HC[c], c, :], func,
                                             bias=s.vec[0:HC[c], 6 + c:7 + c]).then_inc(s.s_gate, 1)

            @block.vector
            def _(dve):
                dve.sem_inc(s.s_u, LEAD)
                dve.sem_inc(s.s_x, LEAD)
                with dve.Fori(0, CH) as n:
                    for c in range(3):
                        dve.wait_ge(s.s_ap, after(3 * n + c))
                        dve.wait_ge(s.s_gate, after(3 * n + c))
                        dve.wait_ge(s.s_down, after(n - 1))
                        nc.vector.scalar_tensor_tensor(s.u[0:HC[c], c, :], avals[0:HC[c], c, :], s.vec[0:HC[c], 3 + c:4 + c],
                                                       s.gate[0:HC[c], c, :], ALU.add, ALU.mult).then_inc(s.s_u, 1)
                    dve.wait_ge(s.s_down, after(n))
                    here = ds(X0 + n * HALF, HALF)
                    nc.vector.scalar_tensor_tensor(dst[:, here], down, s.vec[:, 2:3], src[:, here],
                                                   ALU.add, ALU.add).then_inc(s.s_x, 1)
        m.phase_end()


class Windowed:

    U = 4

    def __init__(self, m):
        self.m = m
        sb, sem, U = m.sb, m.sem, self.U
        self.wqkv, top = m.carve(SCRATCH, [P, 2 * 3 * GW])
        self.wo, top = m.carve(top, [P, 8, P])
        self.scale_qk = sb("att_scale_qk", [P, 2, HD])
        self.rope, top = m.carve(top, [P, 4, ROPE_TILES, HD])
        self.rope_l, top = m.carve(top, [P, 4, ROPE_TILES, HD])
        self.mask = sb("att_mask", [P, P], BF16)
        self.mask_p = sb("att_mask_prior", [P, ROPE_TILES, HD], BF16)
        self.keep = sb("att_keep", [P, ROPE_TILES])
        self.h, at = m.carve(0, [P, U, P])
        self.sq, at = m.carve(at, [P, 2 * GW])
        self.ssq = sb("att_ssq", [P, 2 * GH])
        self.lnv = sb("att_lnv", [P, 2 * GH])
        self.y0 = sb("att_y0", [P, 2 * GH])
        self.t1 = sb("att_t1", [P, 2 * GH])
        self.t2 = sb("att_t2", [P, 2 * GH])
        self.t3 = sb("att_t3", [P, 2 * GH])
        self.rinv = sb("att_rinv", [P, 2 * GH])
        self.qkn, at = m.carve(at, [P, 2, GW])
        self.qcos, at = m.carve(at, [P, GW])
        self.qsin, at = m.carve(at, [P, GW])
        self.kcos, at = m.carve(at, [P, GW])
        self.ksin, at = m.carve(at, [P, GW])
        self.qr, at = m.carve(at, [P, GW])
        self.kr, at = m.carve(at, [P, GW])
        self.qt, at = m.carve(at, [P, 4, P])
        self.kt, top = m.carve(top, [P, U, 4, 2, P])
        self.v, top = m.carve(top, [P, U, GH, HD])
        self.vc, top = m.carve(top, [P, 2, GH, HD])
        self.mx = sb("att_mx", [P, GH])
        self.e, at = m.carve(at, [P, 2, GH, P])
        self.et, at = m.carve(at, [P, GH, P])
        self.den = sb("att_den", [P, GH])
        self.rden = sb("att_rden", [P, GH])
        self.ot, at = m.carve(at, [P, 4, P])
        assert at <= SCRATCH
        self.s_h = sem("att_tile_staged")
        self.s_qk = sem("att_q_k_projected")
        self.s_vp = sem("att_v_projected")
        self.s_sq = sem("att_squared")
        self.s_ssq = sem("att_squares_summed")
        self.s_clamp = sem("att_sums_clamped")
        self.s_ln = sem("att_sums_ln")
        self.s_y0 = sem("att_norm_guess")
        self.s_t1 = sem("att_newton1")
        self.s_t2 = sem("att_newton2")
        self.s_t3 = sem("att_newton3")
        self.s_rinv = sem("att_norm_inverse")
        self.s_qkn = sem("att_q_k_normalised")
        self.s_qcos = sem("att_q_cos")
        self.s_qsin = sem("att_q_sin")
        self.s_qr = sem("att_q_rotated")
        self.s_kcos = sem("att_k_cos")
        self.s_ksin = sem("att_k_sin")
        self.s_kr = sem("att_k_rotated")
        self.s_qkt = sem("att_q_k_transposed")
        self.s_qt = sem("att_q_copied")
        self.s_kt = sem("att_k_copied")
        self.s_v = sem("att_v_copied")
        self.s_sc = sem("att_scores")
        self.s_mx = sem("att_maxima")
        self.s_sub = sem("att_less_maxima")
        self.s_e = sem("att_exp")
        self.s_pt = sem("att_weights_transposed")
        self.s_et = sem("att_weights_copied")
        self.s_pv = sem("att_values_weighted")
        self.s_den = sem("att_weights_summed")
        self.s_rden = sem("att_reciprocals")
        self.s_en = sem("att_weights_divided")
        self.s_ot = sem("att_output_copied")
        self.s_wo = sem("att_output_projected")
        self.s_x = sem("att_output_added")
        self.s_load = sem("att_loaded")

    def load(self, sp, wqkv, wo, scale_qk):
        for dst, src in [(self.wqkv[:, 0:wqkv.shape[-1]], wqkv), (self.wo[:, 0:wo.shape[1], :], wo), (self.scale_qk[:, :, :], scale_qk)]:
            sp.dma_start(dst, src).then_inc(self.s_load, 16)
        sp.wait_ge(self.s_load, 16 * 3)

    def scale_tables(self, pool):
        H2 = HD // 2
        pool.wait_ge(self.s_load, 16 * 3)
        for i, (side, swap) in enumerate([(0, False), (0, True), (1, False), (1, True)]):
            for a in range(2):
                b = 1 - a if swap else a
                self.m.nc.gpsimd.tensor_tensor(self.rope_l[:, i, :, a * H2:(a + 1) * H2], self.rope[:, i, :, a * H2:(a + 1) * H2],
                                               self.scale_qk[:, side, b * H2:(b + 1) * H2].unsqueeze(1).to_broadcast([P, ROPE_TILES, H2]),
                                               ALU.mult)

    def phase(self, G, W, sp_work=None):
        nc, m, s, U = self.m.nc, self.m, self, self.U
        NT = U // G
        BODIES = TILES // NT
        UNITS = SEQS * BODIES * U
        ps = m.psum
        p_qk, p_v = ps[:, 0:2, :], ps[:, 2, :]
        p_qt, p_kt = ps[:, 3, :], ps[:, 4, :]
        p_s = ps[:, 3:5, :]
        p_et = ps[:, 6:8, :]
        p_ot, p_wo = ps[:, 5, :], ps[:, 5, 0:P]
        H2 = HD // 2

        def heads(ap, d=HD):
            return ap.rearrange("p (h d) -> p h d", d=d)

        def halves(ap):
            return ap.rearrange("p (h two d) -> p h two d", two=2, d=H2)

        def flat(ap):
            return ap.rearrange("p h t -> p (h t)")

        def split(k):
            return k // G, k % G

        def tile_of(j, k):
            return ds(j * NT + split(k)[0], 1)

        def pe_qk(pe, bi, k):
            n = bi * U + k
            tile, g = split(k)
            pe.wait_ge(s.s_h, after(bi * NT + tile))
            pe.wait_ge(s.s_qkn, after(n - 1))
            for side in range(2):
                at = (side * G + g) * GW
                mm = nc.tensor.matmul(ps[:, side, :], s.h[:, tile % NT, :], s.wqkv[:, at:at + GW], start=True, stop=True, skip_group_check=True)
            mm.then_inc(s.s_qk, 1)

        def pe_v(pe, n, k):
            tile, g = split(k)
            pe.wait_ge(s.s_v, after(n - 1))
            at = (2 * G + g) * GW
            nc.tensor.matmul(p_v, s.h[:, tile % NT, :], s.wqkv[:, at:at + GW], start=True, stop=True, skip_group_check=True).then_inc(s.s_vp, 1)

        def pe_transpose(pe, n):
            pe.wait_ge(s.s_qr, after(n))
            pe.wait_ge(s.s_kr, after(n))
            pe.wait_ge(s.s_sub, after(n - 1))
            for src, bank in ((s.qr, p_qt), (s.kr, p_kt)):
                for c in range(4):
                    mm = nc.tensor.transpose(bank[:, c * P:(c + 1) * P], src[:, c * P:(c + 1) * P], m.ident[:, :])
            mm.then_inc(s.s_qkt, 1)

        def pe_scores(pe, n, j, k):
            pe.wait_ge(s.s_qt, after(n))
            pe.wait_ge(s.s_kt, after(n))
            for b in range(2):
                nc.tensor.matmul(p_s[:, b, :], m.ident_bf[:, :], s.mask[:, :].unsqueeze(1).to_broadcast([P, 4, P]),
                                 start=True, stop=True, skip_group_check=True)
                for pair in (2 * b, 2 * b + 1):
                    at = (pair % 2) * 2 * P
                    nc.tensor.matmul(p_s[:, b, at:at + 2 * P], s.qt[:, pair, :], flat(s.kt[:, k % U, pair, :, :]),
                                     start=False, stop=True, skip_group_check=True)
                for pair in (2 * b, 2 * b + 1):
                    at = (pair % 2) * 2 * P
                    place = p_s[0:W, b, at:at + 2 * P].rearrange("p (h t) -> p h t", t=P)[:, :, P - W:P]
                    nc.tensor.matmul(place, s.qt[:, pair, 0:W], s.kt[:, (k - G) % U, pair, :, P - W:P], start=True, stop=True, skip_group_check=True)
                    mm = nc.tensor.matmul(place, m.ident_bf[:, 0:W], s.mask_p[:, tile_of(j, k), 0:W].to_broadcast([P, 2, W]),
                                          start=False, stop=True, skip_group_check=True)
            mm.then_inc(s.s_sc, 1)

        def pe_transpose_weights(pe, n, k):
            pe.wait_ge(s.s_en, after(n))
            for b in range(2):
                pe.wait_ge(s.s_et, after(2 * (n - 1) + b))
                for c in range(4):
                    mm = nc.tensor.transpose(p_et[:, b, c * P:(c + 1) * P], s.e[:, k % 2, 4 * b + c, :], m.ident[:, :])
                mm.then_inc(s.s_pt, 1)

        def pe_values(pe, n, k):
            pe.wait_ge(s.s_v, after(n))
            pe.wait_ge(s.s_x, after(n - 1))
            for h in range(GH):
                if h % 4 == 0:
                    pe.wait_ge(s.s_et, after(2 * n + h // 4))
                rows, at = slice((h % 2) * HD, (h % 2 + 1) * HD), (h // 2) * P
                nc.tensor.matmul(p_ot[rows, at:at + W], s.vc[:, k % 2, h, :], s.et[:, h, 0:W], start=True, stop=True, skip_group_check=True)
                mm = nc.tensor.matmul(p_ot[rows, at + W:at + P], s.v[:, k % U, h, :], s.et[:, h, W:P], start=True, stop=True, skip_group_check=True)
            mm.then_inc(s.s_pv, 1)

        def pe_project_out(pe, n, k):
            pe.wait_ge(s.s_ot, after(n))
            for c in range(4):
                mm = nc.tensor.matmul(p_wo, s.wo[:, 4 * split(k)[1] + c, :], s.ot[:, c, :], start=c == 0, stop=True, skip_group_check=True)
            mm.then_inc(s.s_wo, 1)

        def act_stage(act, bi, j, k):
            tile = split(k)[0]
            slot = tile % NT
            col = X0 + (bi * NT + tile) * P
            act.wait_ge(s.s_vp, after(bi * U + k - U + G - 1))
            m.settle(act)
            nc.scalar.activation(s.h[0:64, slot, :], m.xa[0:64, ds(col, P)], ACT.Copy)
            nc.scalar.activation(s.h[64:P, slot, 1:P], m.xa[64:P, ds(col, P - 1)], ACT.Copy)
            nc.scalar.activation(s.h[64:P, slot, 0:1], m.xa[64:P, ds(col - 1, 1)], ACT.Copy,
                                 scale=s.keep[64:P, tile_of(j, k)]).then_inc(s.s_h, 1)

        def act_squares(act, n):
            act.wait_ge(s.s_qk, after(n))
            act.wait_ge(s.s_ssq, after(n - 1))
            nc.scalar.activation(s.sq[:, :].rearrange("p (a c) -> p a c", a=2), p_qk, ACT.Square).then_inc(s.s_sq, 1)

        def act_guess(act, n):
            act.wait_ge(s.s_clamp, after(n))
            nc.scalar.activation(s.lnv[:, :], s.ssq[:, :], ACT.Ln, scale=2.0 ** 16).then_inc(s.s_ln, 1)
            act.wait_ge(s.s_ln, after(n))
            act.wait_ge(s.s_rinv, after(n - 1))
            nc.scalar.activation(s.y0[:, :], s.lnv[:, :], ACT.Exp, scale=-0.5, bias=8 * float(np.log(2.0))).then_inc(s.s_y0, 1)

        def act_qk(act, n, k):
            act.wait_ge(s.s_qkt, after(n))
            act.wait_ge(s.s_sc, after(n - 1))
            nc.scalar.activation(flat(s.qt[:, :, :]), p_qt, ACT.Copy).then_inc(s.s_qt, 1)
            src = p_kt.rearrange("p (c t) -> p c t", c=4)
            nc.scalar.activation(s.kt[0:HD, k % U, :, 0, :], src[0:HD], ACT.Copy)
            nc.scalar.activation(s.kt[HD:P, k % U, :, 1, :], src[HD:P], ACT.Copy).then_inc(s.s_kt, 1)

        def act_v(act, n, k):
            act.wait_ge(s.s_vp, after(n))
            act.wait_ge(s.s_pv, after(n - 2))
            act.wait_ge(s.s_v, after(n - 1))
            nc.scalar.activation(s.vc[P - W:P, k % 2, :, :], s.v[P - W:P, (k - G) % U, :, :], ACT.Copy)
            nc.scalar.activation(s.vc[0:P - W, k % 2, :, :], heads(p_v)[0:P - W], ACT.Copy)
            nc.scalar.activation(s.v[:, k % U, :, :], heads(p_v), ACT.Copy).then_inc(s.s_v, 1)

        def act_exp(act, n, k):
            act.wait_ge(s.s_sub, after(n))
            nc.scalar.activation(s.e[:, k % 2, :, :], s.e[:, k % 2, :, :], ACT.Exp).then_inc(s.s_e, 1)

        def act_weights(act, n):
            act.wait_ge(s.s_pv, after(n - 1))
            for b in range(2):
                act.wait_ge(s.s_pt, after(2 * n + b))
                nc.scalar.activation(flat(s.et[:, 4 * b:4 * b + 4, :]), p_et[:, b, :], ACT.Copy).then_inc(s.s_et, 1)

        def act_out(act, n):
            act.wait_ge(s.s_pv, after(n))
            act.wait_ge(s.s_wo, after(n - 1))
            nc.scalar.activation(flat(s.ot[:, :, :]), p_ot, ACT.Copy).then_inc(s.s_ot, 1)

        def dve_sums(dve, n):
            dve.wait_ge(s.s_sq, after(n))
            dve.wait_ge(s.s_t1, after(n - 1))
            nc.vector.reduce_sum(s.ssq[:, :], heads(s.sq[:, :]), AX_X).then_inc(s.s_ssq, 1)

        def dve_norm(dve, n):
            dve.wait_ge(s.s_rinv, after(n))
            dve.wait_ge(s.s_qsin, after(n - 1))
            dve.wait_ge(s.s_ksin, after(n - 1))
            nc.vector.tensor_tensor(s.qkn[:, :, :].rearrange("p a (h d) -> p (a h) d", d=HD), p_qk.rearrange("p a (h d) -> p (a h) d", d=HD),
                                    s.rinv[:, :].unsqueeze(2).to_broadcast([P, 2 * GH, HD]), ALU.mult).then_inc(s.s_qkn, 1)

        def cos_sin(eng, j, k, side, cos_b, sin_b, s_cos, s_sin):
            src = s.qkn[:, side, :]
            cos, sin = (s.rope_l[:, 2 * side + i, tile_of(j, k), :] for i in range(2))
            eng.tensor_tensor(heads(cos_b[:, :]), heads(src), cos.to_broadcast([P, GH, HD]), ALU.mult).then_inc(s_cos, 1)
            for a in range(2):
                ins = eng.tensor_tensor(halves(sin_b[:, :])[:, :, a, :], halves(src)[:, :, 1 - a, :],
                                        sin[:, :, a * H2:(a + 1) * H2].to_broadcast([P, GH, H2]), ALU.mult)
            ins.then_inc(s_sin, 1)

        def dve_q(dve, n, j, k):
            dve.wait_ge(s.s_qkn, after(n))
            dve.wait_ge(s.s_qr, after(n - 1))
            cos_sin(nc.vector, j, k, 0, s.qcos, s.qsin, s.s_qcos, s.s_qsin)
            dve.wait_ge(s.s_qsin, after(n))
            dve.wait_ge(s.s_qkt, after(n - 1))
            nc.vector.tensor_tensor(s.qr[:, :], s.qcos[:, :], s.qsin[:, :], ALU.add).then_inc(s.s_qr, 1)

        def dve_maxima(dve, n, k):
            dve.wait_ge(s.s_sc, after(n))
            dve.wait_ge(s.s_sub, after(n - 1))
            scores = p_s.rearrange("p b (h t) -> p (b h) t", t=P)
            nc.vector.reduce_max(s.mx[:, :], scores, AX_X).then_inc(s.s_mx, 1)
            dve.wait_ge(s.s_mx, after(n))
            dve.wait_ge(s.s_pt, after(2 * (n - 2) + 1))
            nc.vector.tensor_tensor(s.e[:, k % 2, :, :], scores, s.mx[:, :].unsqueeze(2).to_broadcast([P, GH, P]), ALU.subtract).then_inc(s.s_sub, 1)

        def dve_weight_sums(dve, n, k):
            dve.wait_ge(s.s_e, after(n))
            dve.wait_ge(s.s_rden, after(n - 1))
            nc.vector.reduce_sum(s.den[:, :], s.e[:, k % 2, :, :], AX_X).then_inc(s.s_den, 1)
            dve.wait_ge(s.s_den, after(n))
            dve.wait_ge(s.s_en, after(n - 1))
            nc.vector.reciprocal(s.rden[:, :], s.den[:, :]).then_inc(s.s_rden, 1)

        def dve_add(dve, n, bi, k):
            tile, g = split(k)
            dve.wait_ge(s.s_wo, after(n))
            here = ds(X0 + (bi * NT + tile) * P, P)
            if g:
                dve.wait_ge(s.s_x, after(n - 1))
            nc.vector.tensor_tensor(m.xb[:, here], p_wo, (m.xb if g else m.xa)[:, here], ALU.add).then_inc(s.s_x, 1)

        def pool_clamp(pool, n):
            pool.wait_ge(s.s_ssq, after(n))
            m.settle(pool)
            nc.gpsimd.tensor_scalar(s.ssq[:, :], s.ssq[:, :], 1e-24, None, ALU.max).then_inc(s.s_clamp, 1)

        def pool_newton(pool, n):
            pool.wait_ge(s.s_y0, after(n))
            pool.wait_ge(s.s_t2, after(n - 1))
            nc.gpsimd.tensor_tensor(s.t1[:, :], s.ssq[:, :], s.y0[:, :], ALU.mult).then_inc(s.s_t1, 1)
            pool.wait_ge(s.s_t1, after(n))
            pool.wait_ge(s.s_rinv, after(n - 1))
            nc.gpsimd.tensor_tensor(s.t2[:, :], s.t1[:, :], s.y0[:, :], ALU.mult).then_inc(s.s_t2, 1)
            pool.wait_ge(s.s_t2, after(n))
            m.settle(pool)
            nc.gpsimd.tensor_scalar(s.t3[:, :], s.t2[:, :], -0.5, 1.5, ALU.mult, ALU.add).then_inc(s.s_t3, 1)
            pool.wait_ge(s.s_t3, after(n))
            pool.wait_ge(s.s_qkn, after(n - 1))
            nc.gpsimd.tensor_tensor(s.rinv[:, :], s.t3[:, :], s.y0[:, :], ALU.mult).then_inc(s.s_rinv, 1)

        def pool_rotate(pool, n, j, k):
            pool.wait_ge(s.s_qkn, after(n))
            pool.wait_ge(s.s_kr, after(n - 1))
            m.settle(pool)
            cos_sin(nc.gpsimd, j, k, 1, s.kcos, s.ksin, s.s_kcos, s.s_ksin)
            pool.wait_ge(s.s_ksin, after(n))
            pool.wait_ge(s.s_qkt, after(n - 1))
            nc.gpsimd.tensor_tensor(s.kr[:, :], s.kcos[:, :], s.ksin[:, :], ALU.add).then_inc(s.s_kr, 1)

        def pool_divide(pool, n, k):
            pool.wait_ge(s.s_rden, after(n))
            nc.gpsimd.tensor_tensor(s.e[:, k % 2, :, :], s.e[:, k % 2, :, :], s.rden[:, :].unsqueeze(2).to_broadcast([P, GH, P]),
                                    ALU.mult).then_inc(s.s_en, 1)

        with nc.Block() as block:
            if sp_work:
                block.sync(sp_work)

            @block.tensor
            def _(pe):
                for x in (s.s_qk, s.s_vp, s.s_qkt, s.s_sc, s.s_pt, s.s_pv):
                    pe.sem_inc(x, LEAD)
                pe.sem_inc(s.s_wo, LEAD - 1)
                pe_qk(pe, 0, 0)
                pe_qk(pe, 0, 1)
                pe_transpose(pe, 0)
                pe_scores(pe, 0, 0, 0)
                pe_qk(pe, 0, 2)
                pe_transpose(pe, 1)
                pe_v(pe, 0, 0)
                with pe.Fori(0, SEQS) as seq:
                    with pe.Fori(0, BODIES) as j:
                        for k in range(U):
                            bi = seq * BODIES + j
                            n = bi * U + k
                            pe_scores(pe, n + 1, j, k + 1)
                            pe_qk(pe, bi, k + 3)
                            pe_project_out(pe, n - 1, k - 1)
                            pe_transpose_weights(pe, n, k)
                            pe_transpose(pe, n + 2)
                            pe_v(pe, n + 1, k + 1)
                            pe_values(pe, n, k)
                pe_project_out(pe, UNITS - 1, U - 1)

            @block.scalar
            def _(act):
                act.preload_act_table_set("natural_log_exp_and_others")
                for x in (s.s_h, s.s_sq, s.s_ln, s.s_y0, s.s_v, s.s_qt, s.s_kt, s.s_e, s.s_et):
                    act.sem_inc(x, LEAD)
                for k in range(0, AHEAD, G):
                    act_stage(act, 0, 0, k)
                act_squares(act, 0)
                act_guess(act, 0)
                act_squares(act, 1)
                act_guess(act, 1)
                act_qk(act, 0, 0)
                act_squares(act, 2)
                act_exp(act, 0, 0)
                act_guess(act, 2)
                act_qk(act, 1, 1)
                act_v(act, 0, 0)
                with act.Fori(0, SEQS) as seq:
                    with act.Fori(0, BODIES) as j:
                        for k in range(U):
                            bi = seq * BODIES + j
                            n = bi * U + k
                            if (k + 3) % G == 0:
                                act_stage(act, bi, j, k + 3)
                            act_squares(act, n + 3)
                            act_exp(act, n + 1, k + 1)
                            act_weights(act, n)
                            act_guess(act, n + 3)
                            act_qk(act, n + 2, k + 2)
                            act_v(act, n + 1, k + 1)
                            act_out(act, n)

            @block.vector
            def _(dve):
                for x in (s.s_ssq, s.s_qkn, s.s_qcos, s.s_qsin, s.s_qr, s.s_mx, s.s_sub, s.s_den, s.s_rden):
                    dve.sem_inc(x, LEAD)
                dve.sem_inc(s.s_x, LEAD - 1)
                dve_sums(dve, 0)
                dve_norm(dve, 0)
                dve_q(dve, 0, 0, 0)
                dve_sums(dve, 1)
                dve_norm(dve, 1)
                dve_maxima(dve, 0, 0)
                dve_q(dve, 1, 0, 1)
                dve_sums(dve, 2)
                dve_weight_sums(dve, 0, 0)
                dve_norm(dve, 2)
                with dve.Fori(0, SEQS) as seq:
                    with dve.Fori(0, BODIES) as j:
                        for k in range(U):
                            bi = seq * BODIES + j
                            n = bi * U + k
                            dve_q(dve, n + 2, j, k + 2)
                            dve_maxima(dve, n + 1, k + 1)
                            dve_add(dve, n - 1, bi, k - 1)
                            dve_sums(dve, n + 3)
                            dve_weight_sums(dve, n + 1, k + 1)
                            dve_norm(dve, n + 3)
                dve_add(dve, UNITS - 1, SEQS * BODIES - 1, U - 1)

            @block.gpsimd
            def _(pool):
                for x in (s.s_clamp, s.s_t1, s.s_t2, s.s_t3, s.s_rinv, s.s_kcos, s.s_ksin, s.s_kr, s.s_en):
                    pool.sem_inc(x, LEAD)
                pool.sem_inc(s.s_ot, LEAD - 1)
                nc.gpsimd.memset(s.ot[:, :, :], 0.0).then_inc(s.s_ot, 1)
                for k in range(2):
                    pool_clamp(pool, k)
                    pool_newton(pool, k)
                    pool_rotate(pool, k, 0, k)
                pool_clamp(pool, 2)
                pool_newton(pool, 2)
                pool_divide(pool, 0, 0)
                with pool.Fori(0, SEQS) as seq:
                    with pool.Fori(0, BODIES) as j:
                        for k in range(U):
                            n = (seq * BODIES + j) * U + k
                            pool_rotate(pool, n + 2, j, k + 2)
                            pool_clamp(pool, n + 3)
                            pool_newton(pool, n + 3)
                            pool_divide(pool, n + 1, k + 1)
        m.phase_end()


class Mla:

    SHIFT, ROWS = 96, 112
    PART_Q, PART_K = [0, 0, 1, 0, 2, 1], [0, 1, 0, 2, 0, 1]
    VW = MLA_HD + 1
    PIECE = HALF // P

    def __init__(self, m):
        self.m = m
        sem = m.sem
        self.qs, at = self.wide(0)
        self.ks, at = self.wide(at)
        self.e, at = m.carve(at, [P, 4, HALF])
        self.mxp, at = m.carve(at, [P, MLA_HEADS, 2])
        self.neg, at = m.carve(at, [P, self.ROWS])
        self.y, at = m.carve(at, [P, P])
        self.rden, at = m.carve(at, [P, MLA_HEADS])
        self.oc, at = m.carve(at, [P, 2, HALF])
        self.vs, at = m.carve(at, [P, 4, self.PIECE, self.VW])
        self.w = {}
        top = 0
        for name, rows in (("dq", 64), ("uqT", 64), ("dkv", 64), ("uk", P), ("uv", P), ("oT", P), ("aT", P), ("a", P),
                           ("keT", 64), ("kw", P), ("ve", 64), ("vw", P)):
            ap, top = m.carve(top, [P, P])
            self.w[name] = ap[0:rows]
        self.part, top = self.bf(top, 2 * 3 * HALF)
        self.rest, top = m.carve(top, [P, 2, HALF])
        self.rest2, top = m.carve(top, [P, 2, HALF])
        self.xt, top = m.carve(top, [P, SEQ])
        self.v = m.hn[:, 0:SEQS * TILES * MLA_HEADS * self.VW].rearrange("p (t h d) -> p t h d", h=MLA_HEADS, d=self.VW)
        self.causal = m.sb("mla_causal", [P, 2 * P], BF16)
        self.s_w = sem("mla_s_w")
        self.s_wc = sem("mla_s_wc")
        self.s_pj = sem("mla_s_pj")
        self.s_p1 = sem("mla_s_p1")
        self.s_r1 = sem("mla_s_r1")
        self.s_p2 = sem("mla_s_p2")
        self.s_r2 = sem("mla_s_r2")
        self.s_p3 = sem("mla_s_p3")
        self.s_scr = sem("mla_s_scr")
        self.s_xt = sem("mla_s_xt")
        self.s_v = sem("mla_s_v")
        self.s_vc = sem("mla_s_vc")
        self.s_load = sem("mla_s_load")
        self.s_one = sem("mla_s_one")
        self.s_a = sem("mla_s_a")
        self.s_max = sem("mla_s_max")
        self.s_neg = sem("mla_s_neg")
        self.s_negt = sem("mla_s_negt")
        self.s_shift = sem("mla_s_shift")
        self.s_st = sem("mla_s_st")
        self.s_e = sem("mla_s_e")
        self.s_pv = sem("mla_s_pv")
        self.s_y = sem("mla_s_y")
        self.s_yt = sem("mla_s_yt")
        self.s_out = sem("mla_s_out")
        self.s_rden = sem("mla_s_rden")
        self.s_heads = [sem(f"mla_heads_loaded{i}") for i in range(4)]
        self.s_vs = sem("mla_s_vs")
        self.s_oc = sem("mla_s_oc")
        self.s_ot = sem("mla_s_ot")
        self.s_negc = sem("mla_s_negc")

    def bf(self, at, cols):
        return self.m.arena[:, at:at + cols // 2].bitcast(BF16), at + cols // 2

    def wide(self, at):
        ap, at = self.bf(at, MLA_HEADS * SEQ)
        return ap.rearrange("p (h t) -> p h t", h=MLA_HEADS), at

    def weights(self, t):
        nc, m, s, w = self.m.nc, self.m, self, self.w
        steps = [("aT", "uqT", "dq"), ("a", "dq", "uqT"), ("ve", "uv", "oT"), ("keT", "uk", "aT"), ("kw", "dkv", "keT"), ("vw", "dkv", "ve")]
        widths = {"uk": MLA_LAT, "uv": MLA_LAT}
        with nc.Block() as block:
            @block.sync
            def _(sp):
                for name in ("dq", "uqT", "dkv", "uk", "uv", "oT"):
                    sp.dma_start(w[name][:, 0:widths.get(name, P)], t["mla_" + name]).then_inc(s.s_load, 16)

            @block.tensor
            def _(pe):
                pe.wait_ge(s.s_load, 6 * 16)
                for i, (_, a, b) in enumerate(steps):
                    if i:
                        pe.wait_ge(s.s_wc, i)
                    cols = widths.get(a, P)
                    nc.tensor.matmul(m.psum[0:cols, 0, 0:P], w[a][:, 0:cols], w[b][:, 0:P], start=True, stop=True).then_inc(s.s_w, 1)

            @block.vector
            def _(dve):
                for i, (name, a, _) in enumerate(steps):
                    dve.wait_ge(s.s_w, i + 1)
                    nc.vector.tensor_copy(w[name], m.psum[0:widths.get(a, P), 0, 0:P]).then_inc(s.s_wc, 1)
        m.phase_end()

    def projections(self, scratch):
        nc, m, s = self.m.nc, self.m, self
        scale = float(MLA_HD) ** -0.5
        part = s.part.rearrange("p (a i t) -> p a i t", a=2, i=3)
        with nc.Block() as block:
            @block.tensor
            def _(pe):
                pe.sem_inc(s.s_pj, LEAD)
                pe.sem_inc(s.s_v, LEAD)
                with pe.Fori(0, SEQS) as seq:
                    for half in range(2):
                        n = 2 * seq + half
                        pe.wait_ge(s.s_r1, after(n - 1))
                        for a, wn in enumerate(("a", "kw")):
                            mm = nc.tensor.matmul(m.psum[:, a, :], s.w[wn], m.xa[:, ds(X0 + seq * SEQ + half * HALF, HALF)], start=True, stop=True)
                        mm.then_inc(s.s_pj, 1)
                    pe.wait_ge(s.s_xt, after(seq))
                    pe.wait_ge(s.s_vc, after(seq - 1))
                    for i in range(TILES):
                        mm = nc.tensor.matmul(m.psum[:, 4 + i // 4, (i % 4) * P:(i % 4 + 1) * P], s.xt[:, i * P:(i + 1) * P], s.w["vw"],
                                              start=True, stop=True)
                    mm.then_inc(s.s_v, 1)

            @block.scalar
            def _(act):
                for x in (s.s_p1, s.s_p2, s.s_p3, s.s_xt, s.s_vc):
                    act.sem_inc(x, LEAD)
                with act.Fori(0, SEQS) as seq:
                    act.wait_ge(s.s_v, after(seq - 1))
                    m.settle(act)
                    nc.scalar.activation(s.xt[:, :], m.xa[:, ds(X0 + seq * SEQ, SEQ)], ACT.Copy).then_inc(s.s_xt, 1)
                    for half in range(2):
                        n = 2 * seq + half
                        act.wait_ge(s.s_pj, after(n))
                        act.wait_ge(s.s_scr, 16 * (2 * n + LEAD))
                        nc.scalar.activation(part[:, 0, 0, :], m.psum[:, 0, :], ACT.Copy, scale=scale)
                        nc.scalar.activation(part[:, 1, 0, :], m.psum[:, 1, :], ACT.Copy).then_inc(s.s_p1, 1)
                        act.wait_ge(s.s_r1, after(n))
                        nc.scalar.activation(part[:, :, 1, :], s.rest[:, :, :], ACT.Copy).then_inc(s.s_p2, 1)
                        act.wait_ge(s.s_r2, after(n))
                        nc.scalar.activation(part[:, :, 2, :], s.rest2[:, :, :], ACT.Copy).then_inc(s.s_p3, 1)
                    act.wait_ge(s.s_v, after(seq))
                    m.settle(act)
                    for i in range(TILES):
                        ins = nc.scalar.activation(s.v[:, ds(seq * TILES + i, 1), :, 0:MLA_HD],
                                                   m.psum[:, 4 + i // 4, (i % 4) * P:(i % 4 + 1) * P].rearrange("p (h d) -> p h d", d=MLA_HD).unsqueeze(1),
                                                   ACT.Copy)
                    ins.then_inc(s.s_vc, 1)

            @block.vector
            def _(dve):
                dve.sem_inc(s.s_r1, LEAD)
                dve.sem_inc(s.s_r2, LEAD)
                with dve.Fori(0, SEQS) as seq:
                    for half in range(2):
                        n = 2 * seq + half
                        dve.wait_ge(s.s_p1, after(n))
                        dve.wait_ge(s.s_p2, after(n - 1))
                        dve.wait_ge(s.s_r2, after(n - 1))
                        nc.vector.scalar_tensor_tensor(s.rest[:, 0, :], m.psum[:, 0, :], scale, part[:, 0, 0, :], ALU.mult, ALU.subtract)
                        nc.vector.scalar_tensor_tensor(s.rest[:, 1, :], m.psum[:, 1, :], 1.0, part[:, 1, 0, :], ALU.mult, ALU.subtract).then_inc(s.s_r1, 1)
                        dve.wait_ge(s.s_p2, after(n))
                        dve.wait_ge(s.s_p3, after(n - 1))
                        nc.vector.tensor_tensor(s.rest2[:, :, :], s.rest[:, :, :], part[:, :, 1, :], ALU.subtract).then_inc(s.s_r2, 1)

            @block.sync
            def _(sp):
                sp.sem_inc(s.s_scr, 16 * LEAD)
                with sp.Fori(0, SEQS) as seq:
                    for half in range(2):
                        n = 2 * seq + half
                        sp.wait_ge(s.s_p3, after(n))
                        m.settle(sp)
                        for a in range(2):
                            sp.dma_start(scratch[a][:, :, ds(seq * SEQ + half * HALF, HALF)].rearrange("i p t -> p i t"),
                                         part[:, a, :, :]).then_inc(s.s_scr, 16)
                sp.wait_ge(s.s_scr, 16 * (4 * SEQS + LEAD))
        m.phase_end()

    def attention(self, scratch):
        nc, m, s = self.m.nc, self.m, self
        H, SH, R, NB, HB = MLA_HEADS, self.SHIFT, self.ROWS, TILES, 4
        BODIES = H // HB
        ps = m.psum
        mask_q, mask_k = s.causal[:, 0:P], s.causal[:, P:2 * P]
        np_ = [i // self.PIECE + 1 for i in range(NB)]
        base = [H * sum(np_[:i]) for i in range(NB)]
        TOTAL = H * sum(np_)

        with nc.Block() as block:
            @block.vector
            def _(dve):
                nc.vector.memset(s.neg[:, :], 0.0)
                nc.vector.tensor_copy(s.ks[SH:R, :, :], m.onehot[SH:R, :].unsqueeze(2).to_broadcast([H, H, SEQ]))
                nc.vector.memset(s.oc[:, :, :], 0.0)
                nc.vector.memset(m.arena[32:64, 0:MLA_HEADS * SEQ], 0.0)

            @block.gpsimd
            def _(pool):
                nc.gpsimd.memset(m.arena[64:SH, 0:MLA_HEADS * SEQ], 0.0)
        m.phase_end()

        def pieces(i):
            return [(hh, range(piece * self.PIECE, min(i + 1, (piece + 1) * self.PIECE))) for hh in range(HB) for piece in range(np_[i])]

        def number(seq, i, hb, g):
            return seq * TOTAL + base[i] + hb * HB * np_[i] + g

        def head(ap, rows, h, a, b):
            return ap[0:rows, ds(h, 1), a * P:b * P].rearrange("p h t -> p (h t)")

        def maxima_scores(pe, seq, i, hb, g):
            hh, bl = pieces(i)[g]
            h = hb * HB + hh
            pe.wait_ge(s.s_max, after(number(seq, i, hb, g) - 2))
            mm = nc.tensor.matmul(ps[:, g % 2, 0:len(bl) * P], head(s.qs, SH, h, i, i + 1), head(s.ks, SH, h, bl[0], bl[-1] + 1), start=True, stop=True)
            if bl[-1] == i:
                mm = nc.tensor.matmul(ps[:, g % 2, (len(bl) - 1) * P:len(bl) * P], m.ident_bf[:, :], mask_q, start=False, stop=True,
                                      skip_group_check=True)
            mm.then_inc(s.s_a, 1)

        def reduce_maxima(dve, seq, i, hb, g):
            hh, bl = pieces(i)[g]
            dve.wait_ge(s.s_a, after(number(seq, i, hb, g)))
            piece = bl[0] // self.PIECE
            nc.vector.reduce_max(s.mxp[:, ds(hb * HB + hh, 1), piece:piece + 1].rearrange("p h o -> p (h o)"),
                                 ps[:, g % 2, 0:len(bl) * P], AX_X).then_inc(s.s_max, 1)

        def finish_maxima(dve, seq, i):
            T = seq * NB + i
            dve.wait_ge(s.s_max, after(number(seq, i, BODIES, -1)))
            dve.wait_ge(s.s_negt, after(T - 1))
            if np_[i] == 2:
                nc.vector.tensor_tensor(s.mxp[:, :, 0], s.mxp[:, :, 0], s.mxp[:, :, 1], ALU.max).then_inc(s.s_negc, 1)
                dve.wait_ge(s.s_negc, after(seq * np_.count(2) + i - np_.index(2)))
            nc.vector.tensor_scalar(s.neg[:, SH:R], s.mxp[:, :, 0], -1.0, None, ALU.mult).then_inc(s.s_neg, 1)

        def transpose_maxima(pe, seq, i):
            T = seq * NB + i
            pe.wait_ge(s.s_neg, after(T))
            pe.wait_ge(s.s_out, after(T - 2 if i else T - 1))
            nc.tensor.matmul(ps[0:R, 7, 0:P], s.neg[:, :], m.ident[:, :], start=True, stop=True).then_inc(s.s_negt, 1)

        def write_shift(act, seq, i, hb):
            act.wait_ge(s.s_negt, after(seq * NB + i))
            m.settle(act)
            nc.scalar.activation(s.qs[SH:R, ds(hb * HB, HB), i * P:(i + 1) * P], ps[SH:R, 7, 0:P].unsqueeze(1).to_broadcast([H, HB, P]),
                                 ACT.Copy).then_inc(s.s_shift, 1)

        def shifted_scores(pe, seq, i, hb, g):
            hh, bl = pieces(i)[g]
            h = hb * HB + hh
            pe.wait_ge(s.s_e, after(number(seq, i, hb, g) - 4))
            for b in bl:
                at = (b - bl[0]) * P
                mm = nc.tensor.matmul(ps[:, 2 + g % 4, at:at + P], head(s.ks, R, h, b, b + 1), head(s.qs, R, h, i, i + 1), start=True, stop=True)
                if b == i:
                    mm = nc.tensor.matmul(ps[:, 2 + g % 4, at:at + P], m.ident_bf[:, :], mask_k, start=False, stop=True,
                                          skip_group_check=True)
            mm.then_inc(s.s_st, 1)

        def weigh(pe, seq, i, hb, g):
            hh, bl = pieces(i)[g]
            pe.wait_ge(s.s_e, after(number(seq, i, hb, g)))
            pe.wait_ge(s.s_vs, after(number(seq, i, hb, g)))
            if bl[0] == 0:
                pe.wait_ge(s.s_oc, after(H * (seq * NB + i) + hb * HB + hh - 4))
            for b in bl:
                c = b - bl[0]
                mm = nc.tensor.matmul(ps[32 * hh:32 * hh + s.VW, 6, 0:P], s.vs[:, g % 4, c, :], s.e[:, g % 4, c * P:(c + 1) * P],
                                      start=b == 0, stop=True, skip_group_check=True)
            mm.then_inc(s.s_pv, 1)

        def body(pe, seq, i, hb, last=False):
            count = len(pieces(i))
            more = len(pieces(i + 1)) if i + 1 < NB else 0
            for g in range(count):
                if g + 4 < count:
                    shifted_scores(pe, seq, i, hb, g + 4)
                elif not last:
                    if g + 4 == count:
                        pe.wait_ge(s.s_shift, after(BODIES * (seq * NB + i) + hb + 1))
                    shifted_scores(pe, seq, i, hb + 1, g + 4 - count)
                for a in range(more * min(g, 4) // 4, more * min(g + 1, 4) // 4):
                    maxima_scores(pe, seq, i + 1, hb, a)
                if last and more and count > 4 and g == count - 1:
                    transpose_maxima(pe, seq, i + 1)
                weigh(pe, seq, i, hb, g)
                if last and i and g == 1:
                    transpose_output(pe, seq * NB + i - 1)
            if last and more and count == 4:
                transpose_maxima(pe, seq, i + 1)

        def transpose_weighed(pe, T, i):
            pe.wait_ge(s.s_oc, after(H * T + H - 1))
            pe.wait_ge(s.s_out, after(T - 1))
            for c in range(BODIES):
                mm = nc.tensor.transpose(ps[:, 7, c * P:(c + 1) * P], s.oc[:, i % 2, c * P:(c + 1) * P], m.ident[:, :])
            mm.then_inc(s.s_ot, 1)

        def transpose_output(pe, T):
            pe.wait_ge(s.s_y, after(T))
            nc.tensor.transpose(ps[:, 7, 0:P], s.y[:, :], m.ident[:, :]).then_inc(s.s_yt, 1)

        def exp_body(act, seq, i, hb):
            for g, (hh, bl) in enumerate(pieces(i)):
                act.wait_ge(s.s_st, after(number(seq, i, hb, g)))
                act.wait_ge(s.s_pv, after(number(seq, i, hb, g) - 4))
                nc.scalar.activation(s.e[:, g % 4, 0:len(bl) * P], ps[:, 2 + g % 4, 0:len(bl) * P], ACT.Exp).then_inc(s.s_e, 1)

        def copy_weighed(dve, seq, i, hb, hh):
            T = seq * NB + i
            dve.wait_ge(s.s_pv, after(number(seq, i, hb, (hh + 1) * np_[i] - 1)))
            dve.wait_ge(s.s_ot, after(T - 2))
            rows = slice(32 * hh, 32 * hh + s.VW)
            nc.vector.tensor_copy(s.oc[rows, i % 2, ds(hb * P, P)], ps[rows, 6, 0:P]).then_inc(s.s_oc, 1)

        def dve_body(dve, seq, i, hb, last=False):
            more = len(pieces(i + 1)) if i + 1 < NB else 0
            for g, (hh, bl) in enumerate(pieces(i)):
                for a in range(more * min(g, 4) // 4, more * min(g + 1, 4) // 4):
                    reduce_maxima(dve, seq, i + 1, hb, a)
                if last and more and g == len(pieces(i)) - 1:
                    finish_maxima(dve, seq, i + 1)
                if bl[-1] == i:
                    copy_weighed(dve, seq, i, hb, hh)

        def copy_output(act, T):
            act.wait_ge(s.s_yt, after(T))
            m.settle(act)
            nc.scalar.activation(m.xb[:, ds(X0 + T * P, P)], ps[:, 7, 0:P], ACT.Copy).then_inc(s.s_out, 1)

        def divide(dve, T):
            dve.wait_ge(s.s_ot, after(T))
            ov = ps[:, 7, :].rearrange("p (h d) -> p h d", h=H)
            nc.vector.reciprocal(s.rden[:, :], ov[:, :, MLA_HD]).then_inc(s.s_rden, 1)
            dve.wait_ge(s.s_rden, after(T))
            dve.wait_ge(s.s_yt, after(T - 1))
            nc.vector.tensor_tensor(s.y[:, :].rearrange("p (h d) -> p h d", d=MLA_HD), ov[:, :, 0:MLA_HD],
                                    s.rden[:, :].unsqueeze(2).to_broadcast([P, H, MLA_HD]), ALU.mult).then_inc(s.s_y, 1)

        with nc.Block() as block:
            @block.sync
            def _(sp):
                def load(seq, hb):
                    heads = slice(hb * HB * MLA_HD, (hb + 1) * HB * MLA_HD)
                    for dst, a, parts in ((s.qs, 0, s.PART_Q), (s.ks, 1, s.PART_K)):
                        for slot, i in enumerate(parts):
                            sp.dma_start(dst[slot * MLA_HD:(slot + 1) * MLA_HD, hb * HB:(hb + 1) * HB, :],
                                         scratch[a][i, heads, ds(seq * SEQ, SEQ)].rearrange("(h d) t -> d h t", d=MLA_HD)).then_inc(s.s_heads[hb], 16)

                for hb in range(BODIES):
                    load(0, hb)
                with sp.Fori(1, SEQS) as seq:
                    for hb in range(BODIES):
                        sp.wait_ge(s.s_st, after(number(seq - 1, NB - 1, hb + 1, -1)))
                        m.settle(sp)
                        load(seq, hb)

            @block.gpsimd
            def _(pool):
                pool.sem_inc(s.s_vs, LEAD)
                with pool.Fori(0, SEQS) as seq:
                    for i in range(NB):
                        for hb in range(BODIES):
                            for g, (hh, bl) in enumerate(pieces(i)):
                                pool.wait_ge(s.s_pv, after(number(seq, i, hb, g) - 4))
                                m.settle(pool)
                                nc.gpsimd.tensor_copy(s.vs[:, g % 4, 0:len(bl), :],
                                                      s.v[:, ds(seq * TILES + bl[0], len(bl)), ds(hb * HB + hh, 1), :]
                                                      .rearrange("p t h d -> p t (h d)")).then_inc(s.s_vs, 1)

            @block.tensor
            def _(pe):
                for x in (s.s_a, s.s_negt, s.s_st, s.s_pv, s.s_ot, s.s_yt):
                    pe.sem_inc(x, LEAD)
                with pe.Fori(0, SEQS) as seq:
                    for hb in range(BODIES):
                        pe.wait_ge(s.s_heads[hb], 16 * 12 * (seq + 1))
                        for g in range(HB):
                            maxima_scores(pe, seq, 0, hb, g)
                    transpose_maxima(pe, seq, 0)
                    for i in range(NB):
                        T = seq * NB + i
                        pe.wait_ge(s.s_shift, after(BODIES * T))
                        for g in range(4):
                            shifted_scores(pe, seq, i, 0, g)
                        m.settle(pe)
                        for hb in range(BODIES - 1):
                            body(pe, seq, i, hb)
                        if i:
                            pe.wait_ge(s.s_shift, after(BODIES * T + BODIES - 1))
                            transpose_weighed(pe, T - 1, i - 1)
                        body(pe, seq, i, BODIES - 1, last=True)
                    transpose_weighed(pe, seq * NB + NB - 1, NB - 1)
                    transpose_output(pe, seq * NB + NB - 1)

            @block.scalar
            def _(act):
                act.preload_act_table(ACT.Exp)
                for x in (s.s_shift, s.s_e, s.s_out):
                    act.sem_inc(x, LEAD)
                with act.Fori(0, SEQS) as seq:
                    for i in range(NB):
                        write_shift(act, seq, i, 0)
                        for hb in range(BODIES - 1):
                            write_shift(act, seq, i, hb + 1)
                            exp_body(act, seq, i, hb)
                        exp_body(act, seq, i, BODIES - 1)
                        if i:
                            copy_output(act, seq * NB + i - 1)
                    copy_output(act, seq * NB + NB - 1)

            @block.vector
            def _(dve):
                for x in (s.s_max, s.s_negc, s.s_neg, s.s_oc, s.s_rden, s.s_y):
                    dve.sem_inc(x, LEAD)
                with dve.Fori(0, SEQS) as seq:
                    with dve.Fori(0, BODIES) as hb:
                        for g in range(HB):
                            reduce_maxima(dve, seq, 0, hb, g)
                    finish_maxima(dve, seq, 0)
                    for i in range(NB):
                        T = seq * NB + i
                        dve.wait_ge(s.s_neg, after(T))
                        m.settle(dve)
                        for hb in range(BODIES - 1):
                            dve_body(dve, seq, i, hb)
                        if i:
                            divide(dve, T - 1)
                        dve_body(dve, seq, i, BODIES - 1, last=True)
                    divide(dve, seq * NB + NB - 1)
        m.phase_end()


class Gru:

    ROWS = 2 * DI

    def __init__(self, m):
        self.m = m
        sb, sem = m.sb, m.sem
        self.taps, top = m.carve(SCRATCH, [P, CONV, P])
        self.pwt, top = m.carve(top, [P, P])
        self.cols, top = m.carve(top, [P, 16])
        self.gain, top = m.carve(top, [P, 4])
        self.cbias, top = m.carve(top, [P, 1])
        self.w_hg, top = m.carve(top, [P, 4, self.ROWS])
        self.w_out, top = m.carve(top, [self.ROWS, 2, P])
        R = self.ROWS
        self.sg, at = m.carve(0, [R, 2, HALF])
        self.a, at = m.carve(at, [R, 2, HALF])
        self.sh, at = m.carve(at, [R, 2, HALF])
        self.g, at = m.carve(at, [R, 2, HALF])
        self.v, at = m.carve(at, [R, 2, HALF])
        self.h, at = m.carve(at, [R, 2, 2, HALF])
        self.s_load = sem("gru_s_load")
        self.s_taps = sem("gru_s_taps")
        self.s_cb = sem("gru_s_cb")
        self.s_cbc = sem("gru_s_cbc")
        self.s_conv = sem("gru_s_conv")
        self.s_x = sem("gru_s_x")
        self.s_up = sem("gru_s_up")
        self.s_sg = sem("gru_s_sg")
        self.s_a = sem("gru_s_a")
        self.s_sh = sem("gru_s_sh")
        self.s_m = sem("gru_s_m")
        self.s_g = sem("gru_s_g")
        self.s_v = sem("gru_s_v")
        self.s_h = sem("gru_s_h")
        self.s_out = sem("gru_s_out")

    def setup(self, t):
        nc, m, s = self.m.nc, self.m, self
        with nc.Block() as block:
            @block.sync
            def _(sp):
                for dst, name in ((s.pwt, "gru_pwT"), (s.cols[:, 0:9], "gru_cols"), (s.w_hg, "gru_hg"), (s.w_out, "gru_out")):
                    sp.dma_start(dst, t[name]).then_inc(s.s_load, 16)

            @block.vector
            def _(dve):
                dve.wait_ge(s.s_load, 64)
                for j in range(CONV):
                    nc.vector.tensor_scalar(s.taps[:, j, :], s.pwt[:, :], s.cols[:, j:j + 1], None, ALU.mult)
                nc.vector.tensor_scalar(s.gain[:, 0:3], s.cols[:, 6:9], 1.0, None, ALU.add)
                nc.vector.memset(m.hn[:, TOK:TOK + HALF], 0.0)
                dve.wait_ge(s.s_cb, 1)
                nc.vector.tensor_tensor(s.cbias[:, :], m.psum[:, 0, 0:1], s.cols[:, 5:6], ALU.add)

            @block.tensor
            def _(pe):
                pe.wait_ge(s.s_load, 64)
                nc.tensor.matmul(m.psum[:, 0, 0:1], s.pwt[:, :], s.cols[:, 4:5], start=True, stop=True).then_inc(s.s_cb, 1)
        m.phase_end()

    def conv(self):
        nc, m, s = self.m.nc, self.m, self
        with nc.Block() as block:
            @block.tensor
            def _(pe):
                pe.sem_inc(s.s_conv, LEAD)
                with pe.Fori(0, SEQS) as seq:
                    for half in range(2):
                        n = 2 * seq + half
                        pe.wait_ge(s.s_x, after(n - 2))
                        for j in range(CONV - 1, -1, -1):
                            lag = CONV - 1 - j
                            at = seq * SEQ + half * HALF - lag
                            cut = lag if half == 0 else 0
                            mm = nc.tensor.matmul(m.psum[:, half, cut:HALF], s.taps[:, j, :], m.hn[:, ds(at + cut, HALF - cut)],
                                                  start=lag == 0, stop=True, skip_group_check=True)
                        mm.then_inc(s.s_conv, 1)

            @block.vector
            def _(dve):
                dve.sem_inc(s.s_x, LEAD)
                with dve.Fori(0, SEQS) as seq:
                    for half in range(2):
                        n = 2 * seq + half
                        here = ds(X0 + seq * SEQ + half * HALF, HALF)
                        dve.wait_ge(s.s_conv, after(n))
                        nc.vector.scalar_tensor_tensor(m.xb[:, here], m.psum[:, half, :], s.cbias[:, 0:1], m.xa[:, here],
                                                       ALU.add, ALU.add).then_inc(s.s_x, 1)
        m.phase_end()

    def recurrence(self):
        nc, m, s, R = self.m.nc, self.m, self, self.ROWS
        hid, gate, down = m.psum[0:R, 0:2, :], m.psum[0:R, 2:4, :], m.psum[:, 4:6, :]
        with nc.Block() as block:
            @block.tensor
            def _(pe):
                pe.sem_inc(s.s_up, LEAD)
                pe.sem_inc(s.s_out, LEAD)

                def up(n, at):
                    pe.wait_ge(s.s_a, after(n - 1))
                    for c in range(2):
                        nc.tensor.matmul(gate[:, c, :], s.w_hg[:, 2 + c, :], m.hn[:, at], start=True, stop=True)
                    pe.wait_ge(s.s_g, after(n - 1))
                    for c in range(2):
                        mm = nc.tensor.matmul(hid[:, c, :], s.w_hg[:, c, :], m.hn[:, at], start=True, stop=True)
                    mm.then_inc(s.s_up, 1)

                up(0, ds(0, HALF))
                with pe.Fori(0, SEQS) as seq:
                    for half in range(2):
                        n = 2 * seq + half
                        up(n + 1, ds((n + 1) * HALF, HALF))
                        pe.wait_ge(s.s_h, after(n))
                        pe.wait_ge(s.s_x, after(n - 2))
                        for c in range(2):
                            mm = nc.tensor.matmul(down[:, half, :], s.w_out[:, c, :], s.h[:, half, c, :], start=c == 0, stop=True, skip_group_check=True)
                        mm.then_inc(s.s_out, 1)

            @block.scalar
            def _(act):
                act.preload_act_table(ACT.Sigmoid)
                for x in (s.s_sg, s.s_a, s.s_sh):
                    act.sem_inc(x, LEAD)
                with act.Fori(0, SEQS * 2) as n:
                    act.wait_ge(s.s_up, after(n))
                    act.wait_ge(s.s_m, after(n - 1))
                    nc.scalar.activation(s.sh[:, :, :], hid, ACT.Sigmoid).then_inc(s.s_sh, 1)
                    act.wait_ge(s.s_v, after(n - 1))
                    nc.scalar.activation(s.sg[:, :, :], gate, ACT.Sigmoid).then_inc(s.s_sg, 1)
                    act.wait_ge(s.s_h, after(n - 1))
                    nc.scalar.activation(s.a[:, :, :], gate, ACT.Sigmoid, scale=-1.0).then_inc(s.s_a, 1)

            @block.vector
            def _(dve):
                for x in (s.s_m, s.s_g, s.s_v, s.s_h, s.s_x):
                    dve.sem_inc(x, LEAD)

                def add(n, half):
                    dve.wait_ge(s.s_out, after(n))
                    here = ds(X0 + n * HALF, HALF)
                    nc.vector.tensor_tensor(m.xa[:, here], down[:, half, :], m.xb[:, here], ALU.add).then_inc(s.s_x, 1)

                with dve.Fori(0, SEQS) as seq:
                    for half in range(2):
                        n = 2 * seq + half
                        dve.wait_ge(s.s_sh, after(n))
                        dve.wait_ge(s.s_v, after(n - 1))
                        nc.vector.tensor_scalar(s.g[:, :, :], s.sh[:, :, :], 0.5, None, ALU.min).then_inc(s.s_m, 1)
                        dve.wait_ge(s.s_m, after(n))
                        nc.vector.scalar_tensor_tensor(s.v[:, :, :], hid, 0.0, s.g[:, :, :], ALU.max, ALU.add).then_inc(s.s_g, 1)
                        dve.wait_ge(s.s_g, after(n))
                        dve.wait_ge(s.s_sg, after(n))
                        nc.vector.tensor_tensor(s.g[:, :, :], s.v[:, :, :], s.sg[:, :, :], ALU.mult).then_inc(s.s_v, 1)
                        dve.wait_ge(s.s_v, after(n))
                        dve.wait_ge(s.s_a, after(n))
                        dve.wait_ge(s.s_out, after(n - 2))
                        dve.wait_ge(s.s_h, after(n - 1))
                        for c in range(2):
                            ins = nc.vector.tensor_tensor_scan(s.h[:, half, c, :], s.a[:, c, :], s.g[:, c, :],
                                                               0.0 if half == 0 else s.h[:, 0, c, HALF - 1:HALF], ALU.mult, ALU.add)
                        ins.then_inc(s.s_h, 1)
                        add(n, half)
        m.phase_end()


def shape_constants():
    f = np.float32
    eye = np.eye(P, dtype=f)
    center = eye - f(1.0 / P)
    upper = (np.arange(P) >= HD)[:, None]
    parts = [eye, center, np.where(upper, f(0), center), np.where(upper, center, f(0)), np.full((P, P), 1.0 / P, f)]
    out = {"squares": np.concatenate(parts, 1).astype(f)}
    i = np.arange(P)
    for name, c in LOCAL.items():
        W = c["window"]
        lag = i[:, None] - i[None, :]
        own = np.where((lag >= 0) & (lag <= W), 0, MASKED)
        prior = np.full((P, ROPE_TILES, HD), OFF)
        prior[0:W, :, 0:W] = np.where(i[:W, None] <= i[None, :W], 0, MASKED)[:, None, :]
        prior[:, [0, TILES]] = OFF
        out["masks_" + name] = np.concatenate([own, prior.reshape(P, -1)], 1).astype(f)
        half = np.arange(0, HD, 2, dtype=f)
        inv_freq = (f(1.0) / f(10000.0) ** (half / f(HD))).astype(f)
        t = np.arange(SEQ, dtype=f)
        freqs = t[:, None] * inv_freq[None, :]
        base = ((half + f(0.4 * HD)) / f(1.4 * HD)).astype(f)
        power = ((t - f(SEQ // 2)) / f(W // 2)).astype(f)
        scale = (base[None, :] ** power[:, None]).astype(f)
        cos, sin = np.cos(freqs).astype(f), np.sin(freqs).astype(f)
        tabs = []
        for s in (scale * f(8.0), f(1.0) / scale):
            tabs += [np.concatenate([cos * s, cos * s], 1), np.concatenate([-sin * s, sin * s], 1)]
        tab = np.stack(tabs).astype(f).reshape(4, TILES, P, HD).transpose(2, 0, 1, 3)
        out["rope_" + name] = np.ascontiguousarray(np.concatenate([tab, tab[:, :, 0:AHEAD]], 2))
    keep = np.ones((P, ROPE_TILES), f)
    keep[:, [0, TILES]] = 0
    out["keep"] = keep
    one = np.zeros((P, MLA_HEADS), f)
    one[Mla.SHIFT:Mla.SHIFT + MLA_HEADS] = np.eye(MLA_HEADS, dtype=f)
    out["onehot"] = one
    causal = np.where(i[:, None] >= i[None, :], 0, MASKED).astype(f)
    out["causal"] = np.concatenate([causal, causal.T], 1)
    return out


def ffn_vectors(gain, bias, b2, b1):
    import numpy as np
    L = gain.shape[0]
    v = np.zeros((L, P, 9), np.float32)
    v[:, :, 0], v[:, :, 1], v[:, :, 2] = gain, bias, b2
    for c in range(3):
        v[:, 0:HC[c], 3 + c] = b1[:, HO[c]:HO[c] + HC[c]]
        v[:, 0:HC[c], 6 + c] = b1[:, HID + HO[c]:HID + HO[c] + HC[c]]
    return v


def local_layout(d, pre, up):
    import numpy as np
    qk = np.stack([d[f"{pre}_ffn_q_scale"], d[f"{pre}_ffn_k_scale"]], 1)
    names = ("Wqkv", "Wo", "W1", "b1", "W2", "b2") if up else ("wqkv", "wo", "w1", "b1", "w2", "b2")
    wqkv, wo, w1, b1, w2, b2 = (d[f"{pre}_ffn_{n}"] for n in names)

    def again(w):
        return np.concatenate([w, w[:1]])

    return {
        f"{pre}_wqkv": again(wqkv), f"{pre}_wo": again(wo), f"{pre}_w1": w1, f"{pre}_w2": w2,
        f"{pre}_scale_qk": again(np.broadcast_to(qk[:, None], (len(qk), P, 2, HD))),
        f"{pre}_vec": ffn_vectors(d[f"{pre}_ffn_ln_g"], d[f"{pre}_ffn_ln_b"], b2, b1),
    }


def gru_layout(d):
    import numpy as np
    g = {k[len("L1_attn_"):]: v for k, v in d.items() if k.startswith("L1_attn_")}
    cols = np.concatenate([g["dw_w"][:, 0, :], np.stack([g["dw_b"], g["pw_b"], g["conv_gamma"], g["gru_gamma"], g["ff_gamma"]], 1)], 1)
    heads, hd = g["w_hg"].shape[0], g["w_hg"].shape[1]
    hg = np.zeros((P, 4, 2 * DI), np.float32)
    wo = np.zeros((2 * DI, 2, P), np.float32)
    for h in range(heads):
        pair, col = h // 2, (h % 2) * DI
        hg[h * hd:(h + 1) * hd, pair, col:col + DI] = g["w_hg"][h, :, 0:DI]
        hg[h * hd:(h + 1) * hd, 2 + pair, col:col + DI] = g["w_hg"][h, :, DI:]
        wo[col:col + DI, pair, h * hd:(h + 1) * hd] = g["w_out"][h]
    return {"gru_pwT": g["pw_w"].T, "gru_cols": cols, "gru_hg": hg, "gru_out": wo,
            "gru_w1": np.concatenate([g["w_value"], g["w_gate"]], 1), "gru_w2": g["w_ff_out"], "gru_vec": np.zeros((P, 9), np.float32)}


def build(nc, t, out, stages=("mla", "L0", "gru", "L1")):
    with ExitStack() as ctx:
        m = Machine(nc, ctx)
        norm, ffn, att, mla, gru = Norm(m), Ffn(m), Windowed(m), Mla(m), Gru(m)
        loaded = ctx.enter_context(nc.semaphore("loaded"))
        stored = ctx.enter_context(nc.semaphore("stored"))
        scratch = nc.dram_tensor("parts", (2, 3, P, TOK), BF16, kind="Internal").ap()
        mask_f = m.sb("mask_f", [P, 2 * P])
        zeroed = m.sem("zeroed")

        with nc.Block() as block:
            @block.sync
            def _(sp):
                n = 0
                for dst, src in [(m.ident, 0), (m.center, 1), (m.center_a, 2), (m.center_b, 3), (m.mean, 4)]:
                    sp.dma_start(dst[:, :], t["squares"][:, src * P:(src + 1) * P]).then_inc(loaded, 16)
                sp.dma_start(att.keep[:, :], t["keep"]).then_inc(loaded, 16)
                sp.dma_start(m.onehot[:, :], t["onehot"]).then_inc(loaded, 16)
                sp.dma_start(mask_f[:, 0:2 * P], t["causal"]).then_inc(loaded, 16)
                sp.dma_start(m.xa[:, X0:X0 + TOK], t["xT"]).then_inc(loaded, 16)
                sp.dma_start(m.xres[:, X0:X0 + TOK], t["xT"]).then_inc(loaded, 16)
                sp.wait_ge(loaded, 10 * 16)

            @block.vector
            def _(dve):
                dve.wait_ge(loaded, 10 * 16)
                nc.vector.tensor_copy(m.ident_bf[:, :], m.ident[:, :])
                nc.vector.memset(m.xa[:, 0:X0], 0.0)
                nc.vector.memset(m.xa[:, X0 + TOK:X0 + TOK + PAD], 0.0)
                nc.vector.memset(m.xb[:, 0:X0], 0.0)
                nc.vector.tensor_copy(mla.causal[:, :], mask_f[:, 0:2 * P])
        m.phase_end()

        def family_start(pre):
            masks = P + ROPE_TILES * HD
            with nc.Block() as block:
                @block.sync
                def _(sp):
                    sp.dma_start(att.rope[:, :, :, :], t["rope_" + pre]).then_inc(att.s_load, 16)
                    sp.dma_start(m.arena[:, 0:masks], t["masks_" + pre]).then_inc(att.s_load, 16)
                    sp.wait_ge(att.s_load, 32)

                @block.vector
                def _(dve):
                    dve.wait_ge(att.s_load, 32)
                    nc.vector.tensor_copy(att.mask[:, :], m.arena[:, 0:P])
                    nc.vector.tensor_copy(att.mask_p[:, :, :], m.arena[:, P:masks].rearrange("p (t d) -> p t d", d=HD))
                    nc.vector.memset(att.v[:, :, :, :], 0.0)
                    nc.vector.memset(m.hn[:, TOK:TOK + HALF], 0.0)

                @block.gpsimd
                def _(pool):
                    nc.gpsimd.memset(att.kt[:, :, :, :, :], 0.0)
            m.phase_end()

        def windowed_family(pre):
            c = LOCAL[pre]
            G, L = c["groups"], c["layers"]
            family_start(pre)
            wqkv, wo = t[pre + "_wqkv"], t[pre + "_wo"].rearrange("l (c p) n -> l p c n", p=P)

            def load(layer):
                return lambda sp: att.load(sp, *(ap[ds(layer, 1)][0] for ap in (wqkv, wo, t[pre + "_scale_qk"])))

            with nc.Block() as block:
                block.sync(load(0))
                block.gpsimd(att.scale_tables)
            m.phase_end()
            with nc.Fori(0, L) as layer:
                att.phase(G, c["window"], sp_work=lambda sp: ffn.load(sp, *(t[pre + "_" + n][ds(layer, 1)][0] for n in ("w1", "w2", "vec"))))
                norm.phase("layer", terms=[(m.center_a, m.xb, False), (m.center_b, m.xb, True)], gain=ffn.vec[:, 0:1],
                           bias=ffn.vec[:, 1:2], out=m.hn)
                ffn.phase(m.xb, m.xa, ACT.Gelu, sp_work=load(layer + 1), pool_work=att.scale_tables)

        def outer_norm():
            norm.phase("layer", terms=[(m.center, m.xres, False), (m.center, m.xa, False)], out=m.xa, out_at=X0, out2=m.xres)

        if "mla" in stages:
            mla.weights(t)
            with nc.Block() as block:
                @block.vector
                def _(dve):
                    nc.vector.memset(m.hn[:, :], 1.0)
            m.phase_end()
            mla.projections(scratch)
            mla.attention(scratch)
            norm.phase("layer", terms=[(m.center, m.xres, False), (m.center, m.xb, False)], out=m.xa, out_at=X0, out2=m.xres)
        if "L0" in stages:
            windowed_family("L0")
            outer_norm()
        if "gru" in stages:
            gru.setup(t)
            with nc.Block() as block:
                @block.sync
                def _(sp):
                    ffn.load(sp, t["gru_w1"], t["gru_w2"], t["gru_vec"])
            m.phase_end()
            norm.phase("rms", src=m.xa, gain=gru.gain[:, 0:1], out=m.hn)
            gru.conv()
            norm.phase("rms", src=m.xb, gain=gru.gain[:, 1:2], out=m.hn)
            gru.recurrence()
            norm.phase("rms", src=m.xa, gain=gru.gain[:, 2:3], out=m.hn)
            ffn.phase(m.xa, m.xa, ACT.Silu)
            outer_norm()
        if "L1" in stages:
            windowed_family("L1")
            outer_norm()

        with nc.Block() as block:
            @block.sync
            def _(sp):
                sp.dma_start(out, m.xa[:, X0:X0 + TOK]).then_inc(stored, 16)
                sp.wait_ge(stored, 16)


def host_arrays(d):
    import numpy as np
    d = {k: np.asarray(v) for k, v in d.items()}
    a = {"xT": d["L0_attn_x"].reshape(TOK, P).T}
    a.update(local_layout(d, "L0", True))
    a.update(local_layout(d, "L1", False))
    a.update(gru_layout(d))
    a.update({"mla_dq": d["L0_attn_W_dq"], "mla_uqT": d["L0_attn_W_uq"].T, "mla_dkv": d["L0_attn_W_dkv"],
              "mla_uk": d["L0_attn_W_uk"], "mla_uv": d["L0_attn_W_uv"], "mla_oT": d["L0_attn_W_o"].T})
    a.update(shape_constants())
    return {k: np.ascontiguousarray(v) for k, v in a.items()}


def kernel(**inputs):
    import concourse.bacc as bacc
    from concourse.bass_utils import run_bass_kernel_spmd

    nc = bacc.Bacc("TRN2", target_bir_lowering=False, num_devices=1)
    arrays = host_arrays(inputs)
    t = {k: nc.dram_tensor(f"in_{k}", v.shape, mybir.dt.from_np(v.dtype), kind="ExternalInput").ap() for k, v in arrays.items()}
    out = nc.dram_tensor("out_x", (P, TOK), F32, kind="ExternalOutput").ap()
    build(nc, t, out)
    r = run_bass_kernel_spmd(nc, [{f"in_{k}": v for k, v in arrays.items()}], core_ids=[0])
    return r.results[0]["out_x"].T.reshape(SEQS, SEQ, P)
```

```python
from contextlib import ExitStack

import numpy as np
import concourse.bass as bass
from concourse import mybir

F32 = mybir.dt.float32
BF16 = mybir.dt.bfloat16
ALU = mybir.AluOpType
ACT = mybir.ActivationFunctionType
AX_X = mybir.AxisListType.X
ds = bass.ds

P = 128
SEQS, SEQ = 4, 1024
TOK = SEQS * SEQ
TILES = SEQ // P
HALF = 512
X0 = P
PAD = 3 * P
HD = 64
GH = 8
GW = GH * HD
SCRATCH = 10 * 1024
ARENA = 27 * 1024
LEAD = 4
MASKED = -1e30
OFF = -3e38
HID = int(P * 4 * 2 / 3)
HC = [114, 114, 113]
HO = [0, 114, 228]
NORM_EPS = 1e-5
MLA_HEADS, MLA_HD, MLA_LAT = 16, 8, 64
DI = 48
CONV = 4
LOCAL = {"L0": dict(layers=6, groups=2, window=32), "L1": dict(layers=2, groups=1, window=64)}
AHEAD = 3
ROPE_TILES = TILES + AHEAD


def after(n):
    return n + 1 + LEAD


class Machine:

    def __init__(self, nc, ctx):
        self.nc, self.ctx = nc, ctx
        self.sems = []
        self.settled = self.sem("settled")
        sb = self.sb
        self.xa = sb("xa", [P, X0 + TOK + PAD])
        self.xb = sb("xb", [P, X0 + TOK])
        self.xres = sb("xres", [P, X0 + TOK])
        self.hn = sb("hn", [P, TOK + HALF])
        self.ident = sb("ident", [P, P])
        self.center = sb("center", [P, P])
        self.center_a = sb("center_a", [P, P])
        self.center_b = sb("center_b", [P, P])
        self.mean = sb("mean", [P, P])
        self.onehot = sb("onehot", [P, MLA_HEADS])
        self.ident_bf = sb("ident_bf", [P, P], BF16)
        self.arena = sb("arena", [P, ARENA])
        self.psum = ctx.enter_context(nc.psum_tensor("psum", [P, 8, HALF], F32))

    def sb(self, name, shape, dt=F32):
        return self.ctx.enter_context(self.nc.sbuf_tensor(name, shape, dt))

    def carve(self, at, shape):
        size = int(np.prod(shape[1:]))
        assert at + size <= ARENA
        ap = self.arena[0:shape[0], at:at + size]
        if len(shape) > 2:
            names = "abcd"[:len(shape) - 1]
            ap = ap.rearrange(f"p ({' '.join(names)}) -> p {' '.join(names)}", **dict(zip(names, shape[1:])))
        return ap, at + size

    def sem(self, name):
        s = self.ctx.enter_context(self.nc.semaphore(name))
        self.sems.append(s)
        return s

    def settle(self, eng):
        eng.sem_inc(self.settled, 1)

    def phase_end(self):
        nums = sorted(s.num for s in self.sems)
        self.nc.all_engine_barrier(sems_to_clear=range(nums[0], nums[-1] + 1))


class Norm:

    def __init__(self, m):
        self.m = m
        self.sq, at = m.carve(0, [P, 2, HALF])
        self.lnv, at = m.carve(at, [P, 2, HALF])
        self.y0, at = m.carve(at, [P, 2, HALF])
        self.t1, at = m.carve(at, [P, 2, HALF])
        self.t2, at = m.carve(at, [P, 2, HALF])
        self.t3, at = m.carve(at, [P, 2, HALF])
        self.un, at = m.carve(at, [P, 2, HALF])
        self.fl, at = m.carve(at, [P, 2, HALF])
        self.s_cen = m.sem("norm_centred")
        self.s_sq = m.sem("norm_squared")
        self.s_var = m.sem("norm_variance")
        self.s_floor = m.sem("norm_floored")
        self.s_ln = m.sem("norm_ln")
        self.s_y0 = m.sem("norm_guess")
        self.s_t1 = m.sem("norm_newton1")
        self.s_t2 = m.sem("norm_newton2")
        self.s_t3 = m.sem("norm_newton3")
        self.s_un = m.sem("norm_scaled")
        self.s_out = m.sem("norm_written")

    def phase(self, kind, terms=None, src=None, gain=None, bias=None, out=None, out_at=0, out2=None, sp_work=None):
        nc, m, s = self.m.nc, self.m, self
        layer = kind == "layer"
        ln_scale = 2.0 ** 24
        floor = 1e-24 / P
        eps = NORM_EPS if layer else 0.0
        CH = TOK // HALF
        pairs = [(n, n + 1) for n in range(0, CH, 2)]

        def cen(n):
            return m.psum[:, n % 4, :]

        def var(n):
            return m.psum[:, 4 + n % 4, :]

        def chunk(buf, n, at=X0):
            return buf[:, at + n * HALF:at + (n + 1) * HALF]

        with nc.Block() as block:
            if sp_work:
                block.sync(sp_work)

            @block.tensor
            def _(pe):
                pe.sem_inc(s.s_cen, LEAD)
                pe.sem_inc(s.s_var, LEAD)
                for pair in pairs:
                    for n in pair:
                        if not layer:
                            break
                        pe.wait_ge(s.s_un, after(n - 4))
                        for i, (mat, buf, shifted) in enumerate(terms):
                            cut = 1 if shifted and n % 2 == 0 else 0
                            at = X0 + n * HALF + cut - shifted
                            mm = nc.tensor.matmul(cen(n)[:, cut:HALF], mat[:, :], buf[:, at:at + HALF - cut], start=i == 0, stop=True,
                                                  skip_group_check=True)
                        mm.then_inc(s.s_cen, 1)
                    for n in pair:
                        pe.wait_ge(s.s_sq, after(n))
                        pe.wait_ge(s.s_t1, after(n - 4))
                        nc.tensor.matmul(var(n), m.mean[:, :], s.sq[:, n % 2, :], start=True, stop=True, skip_group_check=True).then_inc(s.s_var, 1)

            @block.scalar
            def _(act):
                act.preload_act_table_set("natural_log_exp_and_others")
                for x in (s.s_sq, s.s_ln, s.s_y0, s.s_out):
                    act.sem_inc(x, LEAD)

                def finish(n):
                    act.wait_ge(s.s_un, after(n))
                    if gain is not None:
                        nc.scalar.activation(chunk(out, n, out_at), s.un[:, n % 2, :], ACT.Identity, scale=gain,
                                             bias=bias if bias is not None else 0.0).then_inc(s.s_out, 1)
                    else:
                        nc.scalar.activation(chunk(out, n, out_at), s.un[:, n % 2, :], ACT.Copy).then_inc(s.s_out, 1)

                for pair in pairs:
                    for n in pair:
                        act.wait_ge(s.s_var, after(n - 2))
                        if layer:
                            act.wait_ge(s.s_cen, after(n))
                        nc.scalar.activation(s.sq[:, n % 2, :], cen(n) if layer else chunk(src, n), ACT.Square).then_inc(s.s_sq, 1)
                    for n in pair:
                        if n >= 2:
                            finish(n - 2)
                    for n in pair:
                        act.wait_ge(s.s_var if layer else s.s_floor, after(n))
                        act.wait_ge(s.s_y0, after(n - 2))
                        nc.scalar.activation(s.lnv[:, n % 2, :], var(n) if layer else s.fl[:, n % 2, :], ACT.Ln, scale=ln_scale,
                                             bias=eps * ln_scale).then_inc(s.s_ln, 1)
                    for n in pair:
                        act.wait_ge(s.s_ln, after(n))
                        act.wait_ge(s.s_t3, after(n - 2))
                        nc.scalar.activation(s.y0[:, n % 2, :], s.lnv[:, n % 2, :], ACT.Exp, scale=-0.5,
                                             bias=12 * float(np.log(2.0))).then_inc(s.s_y0, 1)
                for n in pairs[-1]:
                    finish(n)

            @block.vector
            def _(dve):
                for x in (s.s_floor, s.s_t1, s.s_t2, s.s_t3, s.s_un):
                    dve.sem_inc(x, LEAD)

                def floored(pair):
                    for n in pair:
                        dve.wait_ge(s.s_var, after(n))
                        dve.wait_ge(s.s_ln, after(n - 2))
                        nc.vector.tensor_scalar(s.fl[:, n % 2, :], var(n), floor, None, ALU.max).then_inc(s.s_floor, 1)

                if not layer:
                    floored(pairs[0])
                for i, pair in enumerate(pairs):
                    for n in pair:
                        dve.wait_ge(s.s_y0, after(n))
                        dve.wait_ge(s.s_t2, after(n - 2))
                        nc.vector.scalar_tensor_tensor(s.t1[:, n % 2, :], var(n), eps if layer else floor, s.y0[:, n % 2, :],
                                                       ALU.add if layer else ALU.max, ALU.mult).then_inc(s.s_t1, 1)
                    if not layer and i + 1 < len(pairs):
                        floored(pairs[i + 1])
                    for n in pair:
                        dve.wait_ge(s.s_t1, after(n))
                        dve.wait_ge(s.s_t3, after(n - 2))
                        nc.vector.scalar_tensor_tensor(s.t2[:, n % 2, :], s.t1[:, n % 2, :], -0.5, s.y0[:, n % 2, :],
                                                       ALU.mult, ALU.mult).then_inc(s.s_t2, 1)
                    for n in pair:
                        dve.wait_ge(s.s_t2, after(n))
                        dve.wait_ge(s.s_un, after(n - 2))
                        nc.vector.scalar_tensor_tensor(s.t3[:, n % 2, :], s.t2[:, n % 2, :], 1.5, s.y0[:, n % 2, :],
                                                       ALU.add, ALU.mult).then_inc(s.s_t3, 1)
                    for n in pair:
                        dve.wait_ge(s.s_t3, after(n))
                        dve.wait_ge(s.s_out, after(n - 2))
                        nc.vector.tensor_tensor(s.un[:, n % 2, :], cen(n) if layer else chunk(src, n), s.t3[:, n % 2, :],
                                                ALU.mult).then_inc(s.s_un, 1)

            if out2 is not None:
                @block.gpsimd
                def _(pool):
                    for n in range(CH):
                        pool.wait_ge(s.s_out, after(n))
                        nc.gpsimd.tensor_copy(chunk(out2, n, out_at), chunk(out, n, out_at))
        m.phase_end()


class Ffn:

    def __init__(self, m):
        self.m = m
        self.w1 = m.sb("ffn_w1", [P, 2 * HID])
        self.w2 = m.sb("ffn_w2", [HC[0], 3, P])
        self.vec = m.sb("ffn_vec", [P, 9])
        self.gate, at = m.carve(0, [HC[0], 3, HALF])
        self.u, at = m.carve(at, [HC[0], 3, HALF])
        self.s_load = m.sem("ffn_loaded")
        self.s_gp = m.sem("ffn_gate_products")
        self.s_ap = m.sem("ffn_value_products")
        self.s_gate = m.sem("ffn_gates")
        self.s_u = m.sem("ffn_gated")
        self.s_down = m.sem("ffn_down")
        self.s_x = m.sem("ffn_added")

    def load(self, sp, w1, w2, vec):
        sp.dma_start(self.w1[:, :], w1).then_inc(self.s_load, 16)
        sp.dma_start(self.w2[:, 0:2, :], w2[0:HO[2], :].rearrange("(c p) n -> p c n", c=2)).then_inc(self.s_load, 16)
        sp.dma_start(self.w2[0:HC[2], 2, :], w2[HO[2]:HID, :]).then_inc(self.s_load, 16)
        sp.dma_start(self.vec[:, :], vec).then_inc(self.s_load, 16)
        sp.wait_ge(self.s_load, 64)

    def phase(self, src, dst, func, sp_work=None, pool_work=None):
        nc, m, s = self.m.nc, self.m, self
        CH = TOK // HALF
        avals, gates, down = m.psum[:, 0:3, :], m.psum[:, 3:6, :], m.psum[:, 6, :]
        off = dict(a=0, g=HID)
        with nc.Block() as block:
            if sp_work:
                block.sync(sp_work)
            if pool_work:
                block.gpsimd(pool_work)

            @block.tensor
            def _(pe):
                for x in (s.s_gp, s.s_ap, s.s_down):
                    pe.sem_inc(x, LEAD)

                def up(which, bank, n, at):
                    for c in range(3):
                        if which == "g":
                            pe.wait_ge(s.s_gate, after(3 * (n - 1) + c))
                        else:
                            pe.wait_ge(s.s_u, after(3 * (n - 1) + c))
                        nc.tensor.matmul(bank[0:HC[c], c, :], s.w1[:, off[which] + HO[c]:off[which] + HO[c] + HC[c]],
                                         m.hn[:, at], start=True, stop=True, skip_group_check=True).then_inc(s.s_gp if which == "g" else s.s_ap, 1)

                up("g", gates, 0, ds(0, HALF))
                up("a", avals, 0, ds(0, HALF))
                with pe.Fori(0, CH) as n:
                    up("g", gates, n + 1, ds((n + 1) * HALF, HALF))
                    pe.wait_ge(s.s_x, after(n - 1))
                    for c in range(3):
                        pe.wait_ge(s.s_u, after(3 * n + c))
                        mm = nc.tensor.matmul(down, s.w2[0:HC[c], c, :], s.u[0:HC[c], c, :], start=c == 0, stop=True, skip_group_check=True)
                    mm.then_inc(s.s_down, 1)
                    up("a", avals, n + 1, ds((n + 1) * HALF, HALF))

            @block.scalar
            def _(act):
                act.preload_act_table(func)
                act.sem_inc(s.s_gate, LEAD)
                with act.Fori(0, CH) as n:
                    for c in range(3):
                        act.wait_ge(s.s_gp, after(3 * n + c))
                        act.wait_ge(s.s_u, after(3 * (n - 1) + c))
                        nc.scalar.activation(s.gate[0:HC[c], c, :], gates[0:HC[c], c, :], func,
                                             bias=s.vec[0:HC[c], 6 + c:7 + c]).then_inc(s.s_gate, 1)

            @block.vector
            def _(dve):
                dve.sem_inc(s.s_u, LEAD)
                dve.sem_inc(s.s_x, LEAD)
                with dve.Fori(0, CH) as n:
                    for c in range(3):
                        dve.wait_ge(s.s_ap, after(3 * n + c))
                        dve.wait_ge(s.s_gate, after(3 * n + c))
                        dve.wait_ge(s.s_down, after(n - 1))
                        nc.vector.scalar_tensor_tensor(s.u[0:HC[c], c, :], avals[0:HC[c], c, :], s.vec[0:HC[c], 3 + c:4 + c],
                                                       s.gate[0:HC[c], c, :], ALU.add, ALU.mult).then_inc(s.s_u, 1)
                    dve.wait_ge(s.s_down, after(n))
                    here = ds(X0 + n * HALF, HALF)
                    nc.vector.scalar_tensor_tensor(dst[:, here], down, s.vec[:, 2:3], src[:, here],
                                                   ALU.add, ALU.add).then_inc(s.s_x, 1)
        m.phase_end()


class Windowed:

    U = 4

    def __init__(self, m):
        self.m = m
        sb, sem, U = m.sb, m.sem, self.U
        self.wqkv, top = m.carve(SCRATCH, [P, 2 * 3 * GW])
        self.wo, top = m.carve(top, [P, 8, P])
        self.scale_qk = sb("att_scale_qk", [P, 2, HD])
        self.rope, top = m.carve(top, [P, 4, ROPE_TILES, HD])
        self.rope_l, top = m.carve(top, [P, 4, ROPE_TILES, HD])
        self.mask = sb("att_mask", [P, P], BF16)
        self.mask_p = sb("att_mask_prior", [P, ROPE_TILES, HD], BF16)
        self.keep = sb("att_keep", [P, ROPE_TILES])
        self.h, at = m.carve(0, [P, U, P])
        self.sq, at = m.carve(at, [P, 2 * GW])
        self.ssq = sb("att_ssq", [P, 2 * GH])
        self.lnv = sb("att_lnv", [P, 2 * GH])
        self.y0 = sb("att_y0", [P, 2 * GH])
        self.t1 = sb("att_t1", [P, 2 * GH])
        self.t2 = sb("att_t2", [P, 2 * GH])
        self.t3 = sb("att_t3", [P, 2 * GH])
        self.rinv = sb("att_rinv", [P, 2 * GH])
        self.qkn, at = m.carve(at, [P, 2, GW])
        self.qcos, at = m.carve(at, [P, GW])
        self.qsin, at = m.carve(at, [P, GW])
        self.kcos, at = m.carve(at, [P, GW])
        self.ksin, at = m.carve(at, [P, GW])
        self.qr, at = m.carve(at, [P, GW])
        self.kr, at = m.carve(at, [P, GW])
        self.qt, at = m.carve(at, [P, 4, P])
        self.kt, top = m.carve(top, [P, U, 4, 2, P])
        self.v, top = m.carve(top, [P, U, GH, HD])
        self.vc, top = m.carve(top, [P, 2, GH, HD])
        self.mx = sb("att_mx", [P, GH])
        self.e, at = m.carve(at, [P, 2, GH, P])
        self.et, at = m.carve(at, [P, GH, P])
        self.den = sb("att_den", [P, GH])
        self.rden = sb("att_rden", [P, GH])
        self.ot, at = m.carve(at, [P, 4, P])
        assert at <= SCRATCH
        self.s_tile_staged = sem("att_tile_staged")
        self.s_q_k_projected = sem("att_q_k_projected")
        self.s_v_projected = sem("att_v_projected")
        self.s_squared = sem("att_squared")
        self.s_squares_summed = sem("att_squares_summed")
        self.s_sums_clamped = sem("att_sums_clamped")
        self.s_sums_ln = sem("att_sums_ln")
        self.s_norm_guess = sem("att_norm_guess")
        self.s_newton1 = sem("att_newton1")
        self.s_newton2 = sem("att_newton2")
        self.s_newton3 = sem("att_newton3")
        self.s_norm_inverse = sem("att_norm_inverse")
        self.s_q_k_normalised = sem("att_q_k_normalised")
        self.s_q_cos = sem("att_q_cos")
        self.s_q_sin = sem("att_q_sin")
        self.s_q_rotated = sem("att_q_rotated")
        self.s_k_cos = sem("att_k_cos")
        self.s_k_sin = sem("att_k_sin")
        self.s_k_rotated = sem("att_k_rotated")
        self.s_q_k_transposed = sem("att_q_k_transposed")
        self.s_q_copied = sem("att_q_copied")
        self.s_k_copied = sem("att_k_copied")
        self.s_v_copied = sem("att_v_copied")
        self.s_scores = sem("att_scores")
        self.s_maxima = sem("att_maxima")
        self.s_less_maxima = sem("att_less_maxima")
        self.s_exp = sem("att_exp")
        self.s_weights_transposed = sem("att_weights_transposed")
        self.s_weights_copied = sem("att_weights_copied")
        self.s_values_weighted = sem("att_values_weighted")
        self.s_weights_summed = sem("att_weights_summed")
        self.s_reciprocals = sem("att_reciprocals")
        self.s_weights_divided = sem("att_weights_divided")
        self.s_output_copied = sem("att_output_copied")
        self.s_output_projected = sem("att_output_projected")
        self.s_output_added = sem("att_output_added")
        self.s_loaded = sem("att_loaded")
        self.s_tables_loaded = sem("att_tables_loaded")

    def load(self, sp, wqkv, wo, scale_qk):
        for dst, src in [(self.wqkv[:, 0:wqkv.shape[-1]], wqkv), (self.wo[:, 0:wo.shape[1], :], wo), (self.scale_qk[:, :, :], scale_qk)]:
            sp.dma_start(dst, src).then_inc(self.s_loaded, 16)
        sp.wait_ge(self.s_loaded, 16 * 3)

    def scale_tables(self, pool, loading=False):
        H2 = HD // 2
        if loading:
            pool.wait_ge(self.s_loaded, 16 * 3)
        for i, (side, swap) in enumerate([(0, False), (0, True), (1, False), (1, True)]):
            for a in range(2):
                b = 1 - a if swap else a
                self.m.nc.gpsimd.tensor_tensor(self.rope_l[:, i, :, a * H2:(a + 1) * H2], self.rope[:, i, :, a * H2:(a + 1) * H2],
                                               self.scale_qk[:, side, b * H2:(b + 1) * H2].unsqueeze(1).to_broadcast([P, ROPE_TILES, H2]),
                                               ALU.mult)

    def phase(self, G, W, sp_work=None):
        nc, m, s, U = self.m.nc, self.m, self, self.U
        NT = U // G
        BODIES = TILES // NT
        UNITS = SEQS * BODIES * U
        ps = m.psum
        p_qk, p_v = ps[:, 0:2, :], ps[:, 2, :]
        p_qt, p_kt = ps[:, 3, :], ps[:, 4, :]
        p_s = ps[:, 3:5, :]
        p_et = ps[:, 6:8, :]
        p_ot, p_wo = ps[:, 5, :], ps[:, 5, 0:P]
        H2 = HD // 2

        def heads(ap, d=HD):
            return ap.rearrange("p (h d) -> p h d", d=d)

        def halves(ap):
            return ap.rearrange("p (h two d) -> p h two d", two=2, d=H2)

        def flat(ap):
            return ap.rearrange("p h t -> p (h t)")

        def split(k):
            return k // G, k % G

        def tile_of(j, k):
            return ds(j * NT + split(k)[0], 1)

        def pe_qk(pe, bi, k):
            n = bi * U + k
            tile, g = split(k)
            pe.wait_ge(s.s_tile_staged, after(bi * NT + tile))
            pe.wait_ge(s.s_q_k_normalised, after(n - 1))
            for side in range(2):
                at = (side * G + g) * GW
                mm = nc.tensor.matmul(ps[:, side, :], s.h[:, tile % NT, :], s.wqkv[:, at:at + GW], start=True, stop=True, skip_group_check=True)
            mm.then_inc(s.s_q_k_projected, 1)

        def pe_v(pe, n, k):
            tile, g = split(k)
            pe.wait_ge(s.s_v_copied, after(n - 1))
            at = (2 * G + g) * GW
            nc.tensor.matmul(p_v, s.h[:, tile % NT, :], s.wqkv[:, at:at + GW], start=True, stop=True, skip_group_check=True).then_inc(s.s_v_projected, 1)

        def pe_transpose(pe, n):
            pe.wait_ge(s.s_q_rotated, after(n))
            pe.wait_ge(s.s_k_rotated, after(n))
            pe.wait_ge(s.s_less_maxima, after(n - 1))
            for src, bank in ((s.qr, p_qt), (s.kr, p_kt)):
                for c in range(4):
                    mm = nc.tensor.transpose(bank[:, c * P:(c + 1) * P], src[:, c * P:(c + 1) * P], m.ident[:, :])
            mm.then_inc(s.s_q_k_transposed, 1)

        def pe_scores(pe, n, j, k):
            pe.wait_ge(s.s_q_copied, after(n))
            pe.wait_ge(s.s_k_copied, after(n))
            for b in range(2):
                nc.tensor.matmul(p_s[:, b, :], m.ident_bf[:, :], s.mask[:, :].unsqueeze(1).to_broadcast([P, 4, P]),
                                 start=True, stop=True, skip_group_check=True)
                for pair in (2 * b, 2 * b + 1):
                    at = (pair % 2) * 2 * P
                    nc.tensor.matmul(p_s[:, b, at:at + 2 * P], s.qt[:, pair, :], flat(s.kt[:, k % U, pair, :, :]),
                                     start=False, stop=True, skip_group_check=True)
                for pair in (2 * b, 2 * b + 1):
                    at = (pair % 2) * 2 * P
                    place = p_s[0:W, b, at:at + 2 * P].rearrange("p (h t) -> p h t", t=P)[:, :, P - W:P]
                    nc.tensor.matmul(place, s.qt[:, pair, 0:W], s.kt[:, (k - G) % U, pair, :, P - W:P], start=True, stop=True, skip_group_check=True)
                    mm = nc.tensor.matmul(place, m.ident_bf[:, 0:W], s.mask_p[:, tile_of(j, k), 0:W].to_broadcast([P, 2, W]),
                                          start=False, stop=True, skip_group_check=True)
            mm.then_inc(s.s_scores, 1)

        def pe_transpose_weights(pe, n, k):
            pe.wait_ge(s.s_weights_divided, after(n))
            for b in range(2):
                pe.wait_ge(s.s_weights_copied, after(2 * (n - 1) + b))
                for c in range(4):
                    mm = nc.tensor.transpose(p_et[:, b, c * P:(c + 1) * P], s.e[:, k % 2, 4 * b + c, :], m.ident[:, :])
                mm.then_inc(s.s_weights_transposed, 1)

        def pe_values(pe, n, k):
            pe.wait_ge(s.s_v_copied, after(n))
            pe.wait_ge(s.s_output_added, after(n - 1))
            for h in range(GH):
                if h % 4 == 0:
                    pe.wait_ge(s.s_weights_copied, after(2 * n + h // 4))
                rows, at = slice((h % 2) * HD, (h % 2 + 1) * HD), (h // 2) * P
                nc.tensor.matmul(p_ot[rows, at:at + W], s.vc[:, k % 2, h, :], s.et[:, h, 0:W], start=True, stop=True, skip_group_check=True)
                mm = nc.tensor.matmul(p_ot[rows, at + W:at + P], s.v[:, k % U, h, :], s.et[:, h, W:P], start=True, stop=True, skip_group_check=True)
            mm.then_inc(s.s_values_weighted, 1)

        def pe_project_out(pe, n, k):
            pe.wait_ge(s.s_output_copied, after(n))
            for c in range(4):
                mm = nc.tensor.matmul(p_wo, s.wo[:, 4 * split(k)[1] + c, :], s.ot[:, c, :], start=c == 0, stop=True, skip_group_check=True)
            mm.then_inc(s.s_output_projected, 1)

        def act_stage(act, bi, j, k):
            tile = split(k)[0]
            slot = tile % NT
            col = X0 + (bi * NT + tile) * P
            act.wait_ge(s.s_v_projected, after(bi * U + k - U + G - 1))
            m.settle(act)
            nc.scalar.activation(s.h[0:64, slot, :], m.xa[0:64, ds(col, P)], ACT.Copy)
            nc.scalar.activation(s.h[64:P, slot, 1:P], m.xa[64:P, ds(col, P - 1)], ACT.Copy)
            nc.scalar.activation(s.h[64:P, slot, 0:1], m.xa[64:P, ds(col - 1, 1)], ACT.Copy,
                                 scale=s.keep[64:P, tile_of(j, k)]).then_inc(s.s_tile_staged, 1)

        def act_squares(act, n):
            act.wait_ge(s.s_q_k_projected, after(n))
            act.wait_ge(s.s_squares_summed, after(n - 1))
            nc.scalar.activation(s.sq[:, :].rearrange("p (a c) -> p a c", a=2), p_qk, ACT.Square).then_inc(s.s_squared, 1)

        def act_guess(act, n):
            act.wait_ge(s.s_sums_clamped, after(n))
            nc.scalar.activation(s.lnv[:, :], s.ssq[:, :], ACT.Ln, scale=2.0 ** 16).then_inc(s.s_sums_ln, 1)
            act.wait_ge(s.s_sums_ln, after(n))
            act.wait_ge(s.s_norm_inverse, after(n - 1))
            nc.scalar.activation(s.y0[:, :], s.lnv[:, :], ACT.Exp, scale=-0.5, bias=8 * float(np.log(2.0))).then_inc(s.s_norm_guess, 1)

        def act_qk(act, n, k):
            act.wait_ge(s.s_q_k_transposed, after(n))
            act.wait_ge(s.s_scores, after(n - 1))
            nc.scalar.activation(flat(s.qt[:, :, :]), p_qt, ACT.Copy).then_inc(s.s_q_copied, 1)
            src = p_kt.rearrange("p (c t) -> p c t", c=4)
            nc.scalar.activation(s.kt[0:HD, k % U, :, 0, :], src[0:HD], ACT.Copy)
            nc.scalar.activation(s.kt[HD:P, k % U, :, 1, :], src[HD:P], ACT.Copy).then_inc(s.s_k_copied, 1)

        def act_v(act, n, k):
            act.wait_ge(s.s_v_projected, after(n))
            act.wait_ge(s.s_values_weighted, after(n - 2))
            act.wait_ge(s.s_v_copied, after(n - 1))
            nc.scalar.activation(s.vc[P - W:P, k % 2, :, :], s.v[P - W:P, (k - G) % U, :, :], ACT.Copy)
            nc.scalar.activation(s.vc[0:P - W, k % 2, :, :], heads(p_v)[0:P - W], ACT.Copy)
            nc.scalar.activation(s.v[:, k % U, :, :], heads(p_v), ACT.Copy).then_inc(s.s_v_copied, 1)

        def act_exp(act, n, k):
            act.wait_ge(s.s_less_maxima, after(n))
            nc.scalar.activation(s.e[:, k % 2, :, :], s.e[:, k % 2, :, :], ACT.Exp).then_inc(s.s_exp, 1)

        def act_weights(act, n):
            act.wait_ge(s.s_values_weighted, after(n - 1))
            for b in range(2):
                act.wait_ge(s.s_weights_transposed, after(2 * n + b))
                nc.scalar.activation(flat(s.et[:, 4 * b:4 * b + 4, :]), p_et[:, b, :], ACT.Copy).then_inc(s.s_weights_copied, 1)

        def act_out(act, n):
            act.wait_ge(s.s_values_weighted, after(n))
            act.wait_ge(s.s_output_projected, after(n - 1))
            nc.scalar.activation(flat(s.ot[:, :, :]), p_ot, ACT.Copy).then_inc(s.s_output_copied, 1)

        def dve_sums(dve, n):
            dve.wait_ge(s.s_squared, after(n))
            dve.wait_ge(s.s_newton1, after(n - 1))
            nc.vector.reduce_sum(s.ssq[:, :], heads(s.sq[:, :]), AX_X).then_inc(s.s_squares_summed, 1)

        def dve_norm(dve, n):
            dve.wait_ge(s.s_norm_inverse, after(n))
            dve.wait_ge(s.s_q_sin, after(n - 1))
            dve.wait_ge(s.s_k_sin, after(n - 1))
            nc.vector.tensor_tensor(s.qkn[:, :, :].rearrange("p a (h d) -> p (a h) d", d=HD), p_qk.rearrange("p a (h d) -> p (a h) d", d=HD),
                                    s.rinv[:, :].unsqueeze(2).to_broadcast([P, 2 * GH, HD]), ALU.mult).then_inc(s.s_q_k_normalised, 1)

        def cos_sin(eng, j, k, side, cos_b, sin_b, s_cos, s_sin):
            src = s.qkn[:, side, :]
            cos, sin = (s.rope_l[:, 2 * side + i, tile_of(j, k), :] for i in range(2))
            eng.tensor_tensor(heads(cos_b[:, :]), heads(src), cos.to_broadcast([P, GH, HD]), ALU.mult).then_inc(s_cos, 1)
            for a in range(2):
                ins = eng.tensor_tensor(halves(sin_b[:, :])[:, :, a, :], halves(src)[:, :, 1 - a, :],
                                        sin[:, :, a * H2:(a + 1) * H2].to_broadcast([P, GH, H2]), ALU.mult)
            ins.then_inc(s_sin, 1)

        def dve_q(dve, n, j, k):
            dve.wait_ge(s.s_q_k_normalised, after(n))
            dve.wait_ge(s.s_q_rotated, after(n - 1))
            cos_sin(nc.vector, j, k, 0, s.qcos, s.qsin, s.s_q_cos, s.s_q_sin)
            dve.wait_ge(s.s_q_sin, after(n))
            dve.wait_ge(s.s_q_k_transposed, after(n - 1))
            nc.vector.tensor_tensor(s.qr[:, :], s.qcos[:, :], s.qsin[:, :], ALU.add).then_inc(s.s_q_rotated, 1)

        def dve_maxima(dve, n, k):
            dve.wait_ge(s.s_scores, after(n))
            dve.wait_ge(s.s_less_maxima, after(n - 1))
            scores = p_s.rearrange("p b (h t) -> p (b h) t", t=P)
            nc.vector.reduce_max(s.mx[:, :], scores, AX_X).then_inc(s.s_maxima, 1)
            dve.wait_ge(s.s_maxima, after(n))
            dve.wait_ge(s.s_weights_transposed, after(2 * (n - 2) + 1))
            nc.vector.tensor_tensor(s.e[:, k % 2, :, :], scores, s.mx[:, :].unsqueeze(2).to_broadcast([P, GH, P]), ALU.subtract).then_inc(s.s_less_maxima, 1)

        def dve_weight_sums(dve, n, k):
            dve.wait_ge(s.s_exp, after(n))
            dve.wait_ge(s.s_reciprocals, after(n - 1))
            nc.vector.reduce_sum(s.den[:, :], s.e[:, k % 2, :, :], AX_X).then_inc(s.s_weights_summed, 1)
            dve.wait_ge(s.s_weights_summed, after(n))
            dve.wait_ge(s.s_weights_divided, after(n - 1))
            nc.vector.reciprocal(s.rden[:, :], s.den[:, :]).then_inc(s.s_reciprocals, 1)

        def dve_add(dve, n, bi, k):
            tile, g = split(k)
            dve.wait_ge(s.s_output_projected, after(n))
            here = ds(X0 + (bi * NT + tile) * P, P)
            if g:
                dve.wait_ge(s.s_output_added, after(n - 1))
            nc.vector.tensor_tensor(m.xb[:, here], p_wo, (m.xb if g else m.xa)[:, here], ALU.add).then_inc(s.s_output_added, 1)

        def pool_clamp(pool, n):
            pool.wait_ge(s.s_squares_summed, after(n))
            m.settle(pool)
            nc.gpsimd.tensor_scalar(s.ssq[:, :], s.ssq[:, :], 1e-24, None, ALU.max).then_inc(s.s_sums_clamped, 1)

        def pool_newton(pool, n):
            pool.wait_ge(s.s_norm_guess, after(n))
            pool.wait_ge(s.s_newton2, after(n - 1))
            nc.gpsimd.tensor_tensor(s.t1[:, :], s.ssq[:, :], s.y0[:, :], ALU.mult).then_inc(s.s_newton1, 1)
            pool.wait_ge(s.s_newton1, after(n))
            pool.wait_ge(s.s_norm_inverse, after(n - 1))
            nc.gpsimd.tensor_tensor(s.t2[:, :], s.t1[:, :], s.y0[:, :], ALU.mult).then_inc(s.s_newton2, 1)
            pool.wait_ge(s.s_newton2, after(n))
            m.settle(pool)
            nc.gpsimd.tensor_scalar(s.t3[:, :], s.t2[:, :], -0.5, 1.5, ALU.mult, ALU.add).then_inc(s.s_newton3, 1)
            pool.wait_ge(s.s_newton3, after(n))
            pool.wait_ge(s.s_q_k_normalised, after(n - 1))
            nc.gpsimd.tensor_tensor(s.rinv[:, :], s.t3[:, :], s.y0[:, :], ALU.mult).then_inc(s.s_norm_inverse, 1)

        def pool_rotate(pool, n, j, k):
            pool.wait_ge(s.s_q_k_normalised, after(n))
            pool.wait_ge(s.s_k_rotated, after(n - 1))
            m.settle(pool)
            cos_sin(nc.gpsimd, j, k, 1, s.kcos, s.ksin, s.s_k_cos, s.s_k_sin)
            pool.wait_ge(s.s_k_sin, after(n))
            pool.wait_ge(s.s_q_k_transposed, after(n - 1))
            nc.gpsimd.tensor_tensor(s.kr[:, :], s.kcos[:, :], s.ksin[:, :], ALU.add).then_inc(s.s_k_rotated, 1)

        def pool_divide(pool, n, k):
            pool.wait_ge(s.s_reciprocals, after(n))
            nc.gpsimd.tensor_tensor(s.e[:, k % 2, :, :], s.e[:, k % 2, :, :], s.rden[:, :].unsqueeze(2).to_broadcast([P, GH, P]),
                                    ALU.mult).then_inc(s.s_weights_divided, 1)

        with nc.Block() as block:
            if sp_work:
                block.sync(sp_work)

            @block.tensor
            def _(pe):
                for x in (s.s_q_k_projected, s.s_v_projected, s.s_q_k_transposed, s.s_scores, s.s_weights_transposed, s.s_values_weighted):
                    pe.sem_inc(x, LEAD)
                pe.sem_inc(s.s_output_projected, LEAD - 1)
                pe_qk(pe, 0, 0)
                pe_qk(pe, 0, 1)
                pe_transpose(pe, 0)
                pe_scores(pe, 0, 0, 0)
                pe_qk(pe, 0, 2)
                pe_transpose(pe, 1)
                pe_v(pe, 0, 0)
                with pe.Fori(0, SEQS) as seq:
                    with pe.Fori(0, BODIES) as j:
                        for k in range(U):
                            bi = seq * BODIES + j
                            n = bi * U + k
                            pe_scores(pe, n + 1, j, k + 1)
                            pe_qk(pe, bi, k + 3)
                            pe_project_out(pe, n - 1, k - 1)
                            pe_transpose_weights(pe, n, k)
                            pe_transpose(pe, n + 2)
                            pe_v(pe, n + 1, k + 1)
                            pe_values(pe, n, k)
                pe_project_out(pe, UNITS - 1, U - 1)

            @block.scalar
            def _(act):
                for x in (s.s_tile_staged, s.s_squared, s.s_sums_ln, s.s_norm_guess, s.s_v_copied, s.s_q_copied, s.s_k_copied, s.s_exp, s.s_weights_copied):
                    act.sem_inc(x, LEAD)
                for k in range(0, AHEAD, G):
                    act_stage(act, 0, 0, k)
                act.preload_act_table_set("natural_log_exp_and_others")
                act_squares(act, 0)
                act_guess(act, 0)
                act_squares(act, 1)
                act_guess(act, 1)
                act_qk(act, 0, 0)
                act_squares(act, 2)
                act_exp(act, 0, 0)
                act_guess(act, 2)
                act_qk(act, 1, 1)
                act_v(act, 0, 0)
                with act.Fori(0, SEQS) as seq:
                    with act.Fori(0, BODIES) as j:
                        for k in range(U):
                            bi = seq * BODIES + j
                            n = bi * U + k
                            if (k + 3) % G == 0:
                                act_stage(act, bi, j, k + 3)
                            act_squares(act, n + 3)
                            act_exp(act, n + 1, k + 1)
                            act_weights(act, n)
                            act_guess(act, n + 3)
                            act_qk(act, n + 2, k + 2)
                            act_v(act, n + 1, k + 1)
                            act_out(act, n)

            @block.vector
            def _(dve):
                for x in (s.s_squares_summed, s.s_q_k_normalised, s.s_q_cos, s.s_q_sin, s.s_q_rotated, s.s_maxima, s.s_less_maxima, s.s_weights_summed, s.s_reciprocals):
                    dve.sem_inc(x, LEAD)
                dve.sem_inc(s.s_output_added, LEAD - 1)
                dve_sums(dve, 0)
                dve_norm(dve, 0)
                dve_q(dve, 0, 0, 0)
                dve_sums(dve, 1)
                dve_norm(dve, 1)
                dve_maxima(dve, 0, 0)
                dve_q(dve, 1, 0, 1)
                dve_sums(dve, 2)
                dve_weight_sums(dve, 0, 0)
                dve_norm(dve, 2)
                with dve.Fori(0, SEQS) as seq:
                    with dve.Fori(0, BODIES) as j:
                        for k in range(U):
                            bi = seq * BODIES + j
                            n = bi * U + k
                            dve_q(dve, n + 2, j, k + 2)
                            dve_maxima(dve, n + 1, k + 1)
                            dve_add(dve, n - 1, bi, k - 1)
                            dve_sums(dve, n + 3)
                            dve_weight_sums(dve, n + 1, k + 1)
                            dve_norm(dve, n + 3)
                dve_add(dve, UNITS - 1, SEQS * BODIES - 1, U - 1)

            @block.gpsimd
            def _(pool):
                for x in (s.s_sums_clamped, s.s_newton1, s.s_newton2, s.s_newton3, s.s_norm_inverse, s.s_k_cos, s.s_k_sin, s.s_k_rotated, s.s_weights_divided):
                    pool.sem_inc(x, LEAD)
                pool.sem_inc(s.s_output_copied, LEAD - 1)
                nc.gpsimd.memset(s.ot[:, :, :], 0.0).then_inc(s.s_output_copied, 1)
                for k in range(2):
                    pool_clamp(pool, k)
                    pool_newton(pool, k)
                    pool_rotate(pool, k, 0, k)
                pool_clamp(pool, 2)
                pool_newton(pool, 2)
                pool_divide(pool, 0, 0)
                with pool.Fori(0, SEQS) as seq:
                    with pool.Fori(0, BODIES) as j:
                        for k in range(U):
                            n = (seq * BODIES + j) * U + k
                            pool_rotate(pool, n + 2, j, k + 2)
                            pool_clamp(pool, n + 3)
                            pool_newton(pool, n + 3)
                            pool_divide(pool, n + 1, k + 1)
        m.phase_end()


class Mla:

    SHIFT, ROWS = 96, 112
    PART_Q, PART_K = [0, 0, 1, 0, 2, 1], [0, 1, 0, 2, 0, 1]
    VW = MLA_HD + 1
    PIECE = HALF // P

    def __init__(self, m):
        self.m = m
        sem = m.sem
        self.qs, at = self.wide(0)
        self.ks, at = self.wide(at)
        self.e, at = m.carve(at, [P, 4, HALF])
        self.mxp, at = m.carve(at, [P, MLA_HEADS, 2])
        self.neg, at = m.carve(at, [P, self.ROWS])
        self.y, at = m.carve(at, [P, P])
        self.rden, at = m.carve(at, [P, MLA_HEADS])
        self.oc, at = m.carve(at, [P, 2, HALF])
        self.vs, at = m.carve(at, [P, 4, self.PIECE, self.VW])
        self.w = {}
        top = 0
        for name, rows in (("dq", 64), ("uqT", 64), ("dkv", 64), ("uk", P), ("uv", P), ("oT", P), ("aT", P), ("a", P),
                           ("keT", 64), ("kw", P), ("ve", 64), ("vw", P)):
            ap, top = m.carve(top, [P, P])
            self.w[name] = ap[0:rows]
        self.part, top = self.bf(top, 2 * 3 * HALF)
        self.rest, top = m.carve(top, [P, 2, HALF])
        self.rest2, top = m.carve(top, [P, 2, HALF])
        self.xt, top = m.carve(top, [P, SEQ])
        self.v = m.hn[:, 0:SEQS * TILES * MLA_HEADS * self.VW].rearrange("p (t h d) -> p t h d", h=MLA_HEADS, d=self.VW)
        self.causal = m.sb("mla_causal", [P, 2 * P], BF16)
        self.s_weights_multiplied = sem("mla_weights_multiplied")
        self.s_weights_copied = sem("mla_weights_copied")
        self.s_q_k_projected = sem("mla_q_k_projected")
        self.s_part1 = sem("mla_part1")
        self.s_rest1 = sem("mla_rest1")
        self.s_part2 = sem("mla_part2")
        self.s_rest2 = sem("mla_rest2")
        self.s_part3 = sem("mla_part3")
        self.s_parts_stored = sem("mla_parts_stored")
        self.s_tokens_staged = sem("mla_tokens_staged")
        self.s_values_projected = sem("mla_values_projected")
        self.s_values_copied = sem("mla_values_copied")
        self.s_weights_loaded = sem("mla_weights_loaded")
        self.s_maxima_scores = sem("mla_maxima_scores")
        self.s_piece_maxima = sem("mla_piece_maxima")
        self.s_maxima_negated = sem("mla_maxima_negated")
        self.s_maxima_transposed = sem("mla_maxima_transposed")
        self.s_maxima_in_queries = sem("mla_maxima_in_queries")
        self.s_scores = sem("mla_scores")
        self.s_exp = sem("mla_exp")
        self.s_values_weighted = sem("mla_values_weighted")
        self.s_output_divided = sem("mla_output_divided")
        self.s_output_transposed = sem("mla_output_transposed")
        self.s_output_copied = sem("mla_output_copied")
        self.s_reciprocals = sem("mla_reciprocals")
        self.s_heads_loaded = [sem(f"mla_heads_loaded{i}") for i in range(4)]
        self.s_values_staged = sem("mla_values_staged")
        self.s_weighed_copied = sem("mla_weighed_copied")
        self.s_weighed_transposed = sem("mla_weighed_transposed")
        self.s_maxima_joined = sem("mla_maxima_joined")

    def bf(self, at, cols):
        return self.m.arena[:, at:at + cols // 2].bitcast(BF16), at + cols // 2

    def wide(self, at):
        ap, at = self.bf(at, MLA_HEADS * SEQ)
        return ap.rearrange("p (h t) -> p h t", h=MLA_HEADS), at

    def weights(self, t):
        nc, m, s, w = self.m.nc, self.m, self, self.w
        steps = [("aT", "uqT", "dq"), ("a", "dq", "uqT"), ("ve", "uv", "oT"), ("keT", "uk", "aT"), ("kw", "dkv", "keT"), ("vw", "dkv", "ve")]
        widths = {"uk": MLA_LAT, "uv": MLA_LAT}
        with nc.Block() as block:
            @block.sync
            def _(sp):
                for name in ("dq", "uqT", "dkv", "uk", "uv", "oT"):
                    sp.dma_start(w[name][:, 0:widths.get(name, P)], t["mla_" + name]).then_inc(s.s_weights_loaded, 16)

            @block.tensor
            def _(pe):
                pe.wait_ge(s.s_weights_loaded, 6 * 16)
                for i, (_, a, b) in enumerate(steps):
                    if i:
                        pe.wait_ge(s.s_weights_copied, i)
                    cols = widths.get(a, P)
                    nc.tensor.matmul(m.psum[0:cols, 0, 0:P], w[a][:, 0:cols], w[b][:, 0:P], start=True, stop=True).then_inc(s.s_weights_multiplied, 1)

            @block.vector
            def _(dve):
                for i, (name, a, _) in enumerate(steps):
                    dve.wait_ge(s.s_weights_multiplied, i + 1)
                    nc.vector.tensor_copy(w[name], m.psum[0:widths.get(a, P), 0, 0:P]).then_inc(s.s_weights_copied, 1)
        m.phase_end()

    def projections(self, scratch):
        nc, m, s = self.m.nc, self.m, self
        scale = float(MLA_HD) ** -0.5
        part = s.part.rearrange("p (a i t) -> p a i t", a=2, i=3)
        with nc.Block() as block:
            @block.tensor
            def _(pe):
                pe.sem_inc(s.s_q_k_projected, LEAD)
                pe.sem_inc(s.s_values_projected, LEAD)
                with pe.Fori(0, SEQS) as seq:
                    for half in range(2):
                        n = 2 * seq + half
                        pe.wait_ge(s.s_rest1, after(n - 1))
                        for a, wn in enumerate(("a", "kw")):
                            mm = nc.tensor.matmul(m.psum[:, a, :], s.w[wn], m.xa[:, ds(X0 + seq * SEQ + half * HALF, HALF)], start=True, stop=True)
                        mm.then_inc(s.s_q_k_projected, 1)
                    pe.wait_ge(s.s_tokens_staged, after(seq))
                    pe.wait_ge(s.s_values_copied, after(seq - 1))
                    for i in range(TILES):
                        mm = nc.tensor.matmul(m.psum[:, 4 + i // 4, (i % 4) * P:(i % 4 + 1) * P], s.xt[:, i * P:(i + 1) * P], s.w["vw"],
                                              start=True, stop=True)
                    mm.then_inc(s.s_values_projected, 1)

            @block.scalar
            def _(act):
                for x in (s.s_part1, s.s_part2, s.s_part3, s.s_tokens_staged, s.s_values_copied):
                    act.sem_inc(x, LEAD)
                with act.Fori(0, SEQS) as seq:
                    act.wait_ge(s.s_values_projected, after(seq - 1))
                    m.settle(act)
                    nc.scalar.activation(s.xt[:, :], m.xa[:, ds(X0 + seq * SEQ, SEQ)], ACT.Copy).then_inc(s.s_tokens_staged, 1)
                    for half in range(2):
                        n = 2 * seq + half
                        act.wait_ge(s.s_q_k_projected, after(n))
                        act.wait_ge(s.s_parts_stored, 16 * (2 * n + LEAD))
                        nc.scalar.activation(part[:, 0, 0, :], m.psum[:, 0, :], ACT.Copy, scale=scale)
                        nc.scalar.activation(part[:, 1, 0, :], m.psum[:, 1, :], ACT.Copy).then_inc(s.s_part1, 1)
                        act.wait_ge(s.s_rest1, after(n))
                        nc.scalar.activation(part[:, :, 1, :], s.rest[:, :, :], ACT.Copy).then_inc(s.s_part2, 1)
                        act.wait_ge(s.s_rest2, after(n))
                        nc.scalar.activation(part[:, :, 2, :], s.rest2[:, :, :], ACT.Copy).then_inc(s.s_part3, 1)
                    act.wait_ge(s.s_values_projected, after(seq))
                    m.settle(act)
                    for i in range(TILES):
                        ins = nc.scalar.activation(s.v[:, ds(seq * TILES + i, 1), :, 0:MLA_HD],
                                                   m.psum[:, 4 + i // 4, (i % 4) * P:(i % 4 + 1) * P].rearrange("p (h d) -> p h d", d=MLA_HD).unsqueeze(1),
                                                   ACT.Copy)
                    ins.then_inc(s.s_values_copied, 1)

            @block.vector
            def _(dve):
                dve.sem_inc(s.s_rest1, LEAD)
                dve.sem_inc(s.s_rest2, LEAD)
                with dve.Fori(0, SEQS) as seq:
                    for half in range(2):
                        n = 2 * seq + half
                        dve.wait_ge(s.s_part1, after(n))
                        dve.wait_ge(s.s_part2, after(n - 1))
                        dve.wait_ge(s.s_rest2, after(n - 1))
                        nc.vector.scalar_tensor_tensor(s.rest[:, 0, :], m.psum[:, 0, :], scale, part[:, 0, 0, :], ALU.mult, ALU.subtract)
                        nc.vector.scalar_tensor_tensor(s.rest[:, 1, :], m.psum[:, 1, :], 1.0, part[:, 1, 0, :], ALU.mult, ALU.subtract).then_inc(s.s_rest1, 1)
                        dve.wait_ge(s.s_part2, after(n))
                        dve.wait_ge(s.s_part3, after(n - 1))
                        nc.vector.tensor_tensor(s.rest2[:, :, :], s.rest[:, :, :], part[:, :, 1, :], ALU.subtract).then_inc(s.s_rest2, 1)

            @block.sync
            def _(sp):
                sp.sem_inc(s.s_parts_stored, 16 * LEAD)
                with sp.Fori(0, SEQS) as seq:
                    for half in range(2):
                        n = 2 * seq + half
                        sp.wait_ge(s.s_part3, after(n))
                        m.settle(sp)
                        for a in range(2):
                            sp.dma_start(scratch[a][:, :, ds(seq * SEQ + half * HALF, HALF)].rearrange("i p t -> p i t"),
                                         part[:, a, :, :]).then_inc(s.s_parts_stored, 16)
                sp.wait_ge(s.s_parts_stored, 16 * (4 * SEQS + LEAD))
        m.phase_end()

    def attention(self, scratch):
        nc, m, s = self.m.nc, self.m, self
        H, SH, R, NB, HB = MLA_HEADS, self.SHIFT, self.ROWS, TILES, 4
        BODIES = H // HB
        ps = m.psum
        mask_q, mask_k = s.causal[:, 0:P], s.causal[:, P:2 * P]
        np_ = [i // self.PIECE + 1 for i in range(NB)]
        base = [H * sum(np_[:i]) for i in range(NB)]
        TOTAL = H * sum(np_)

        with nc.Block() as block:
            @block.vector
            def _(dve):
                nc.vector.memset(s.neg[:, :], 0.0)
                nc.vector.memset(s.oc[:, :, :], 0.0)
                nc.vector.memset(m.arena[32:64, 0:MLA_HEADS * SEQ], 0.0)

            @block.scalar
            def _(act):
                nc.scalar.activation(s.ks[SH:R, :, :], m.onehot[SH:R, :].unsqueeze(2).to_broadcast([H, H, SEQ]), ACT.Copy)

            @block.gpsimd
            def _(pool):
                nc.gpsimd.memset(m.arena[64:SH, 0:MLA_HEADS * SEQ], 0.0)
        m.phase_end()

        def pieces(i):
            return [(hh, range(piece * self.PIECE, min(i + 1, (piece + 1) * self.PIECE))) for hh in range(HB) for piece in range(np_[i])]

        def number(seq, i, hb, g):
            return seq * TOTAL + base[i] + hb * HB * np_[i] + g

        def head(ap, rows, h, a, b):
            return ap[0:rows, ds(h, 1), a * P:b * P].rearrange("p h t -> p (h t)")

        def maxima_scores(pe, seq, i, hb, g):
            hh, bl = pieces(i)[g]
            h = hb * HB + hh
            pe.wait_ge(s.s_piece_maxima, after(number(seq, i, hb, g) - 2))
            mm = nc.tensor.matmul(ps[:, g % 2, 0:len(bl) * P], head(s.qs, SH, h, i, i + 1), head(s.ks, SH, h, bl[0], bl[-1] + 1), start=True, stop=True)
            if bl[-1] == i:
                mm = nc.tensor.matmul(ps[:, g % 2, (len(bl) - 1) * P:len(bl) * P], m.ident_bf[:, :], mask_q, start=False, stop=True,
                                      skip_group_check=True)
            mm.then_inc(s.s_maxima_scores, 1)

        def reduce_maxima(dve, seq, i, hb, g):
            hh, bl = pieces(i)[g]
            dve.wait_ge(s.s_maxima_scores, after(number(seq, i, hb, g)))
            piece = bl[0] // self.PIECE
            nc.vector.reduce_max(s.mxp[:, ds(hb * HB + hh, 1), piece:piece + 1].rearrange("p h o -> p (h o)"),
                                 ps[:, g % 2, 0:len(bl) * P], AX_X).then_inc(s.s_piece_maxima, 1)

        def finish_maxima(dve, seq, i):
            T = seq * NB + i
            dve.wait_ge(s.s_piece_maxima, after(number(seq, i, BODIES, -1)))
            dve.wait_ge(s.s_maxima_transposed, after(T - 1))
            if np_[i] == 2:
                nc.vector.tensor_tensor(s.mxp[:, :, 0], s.mxp[:, :, 0], s.mxp[:, :, 1], ALU.max).then_inc(s.s_maxima_joined, 1)
                dve.wait_ge(s.s_maxima_joined, after(seq * np_.count(2) + i - np_.index(2)))
            nc.vector.tensor_scalar(s.neg[:, SH:R], s.mxp[:, :, 0], -1.0, None, ALU.mult).then_inc(s.s_maxima_negated, 1)

        def transpose_maxima(pe, seq, i):
            T = seq * NB + i
            pe.wait_ge(s.s_maxima_negated, after(T))
            pe.wait_ge(s.s_output_copied, after(T - 2 if i else T - 1))
            nc.tensor.matmul(ps[0:R, 7, 0:P], s.neg[:, :], m.ident[:, :], start=True, stop=True).then_inc(s.s_maxima_transposed, 1)

        def write_shift(act, seq, i, hb):
            act.wait_ge(s.s_maxima_transposed, after(seq * NB + i))
            m.settle(act)
            nc.scalar.activation(s.qs[SH:R, ds(hb * HB, HB), i * P:(i + 1) * P], ps[SH:R, 7, 0:P].unsqueeze(1).to_broadcast([H, HB, P]),
                                 ACT.Copy).then_inc(s.s_maxima_in_queries, 1)

        def shifted_scores(pe, seq, i, hb, g):
            hh, bl = pieces(i)[g]
            h = hb * HB + hh
            pe.wait_ge(s.s_exp, after(number(seq, i, hb, g) - 4))
            for b in bl:
                at = (b - bl[0]) * P
                mm = nc.tensor.matmul(ps[:, 2 + g % 4, at:at + P], head(s.ks, R, h, b, b + 1), head(s.qs, R, h, i, i + 1), start=True, stop=True)
                if b == i:
                    mm = nc.tensor.matmul(ps[:, 2 + g % 4, at:at + P], m.ident_bf[:, :], mask_k, start=False, stop=True,
                                          skip_group_check=True)
            mm.then_inc(s.s_scores, 1)

        def weigh(pe, seq, i, hb, g):
            hh, bl = pieces(i)[g]
            pe.wait_ge(s.s_exp, after(number(seq, i, hb, g)))
            pe.wait_ge(s.s_values_staged, after(number(seq, i, hb, g)))
            if bl[0] == 0:
                pe.wait_ge(s.s_weighed_copied, after(H * (seq * NB + i) + hb * HB + hh - 4))
            for b in bl:
                c = b - bl[0]
                mm = nc.tensor.matmul(ps[32 * hh:32 * hh + s.VW, 6, 0:P], s.vs[:, g % 4, c, :], s.e[:, g % 4, c * P:(c + 1) * P],
                                      start=b == 0, stop=True, skip_group_check=True)
            mm.then_inc(s.s_values_weighted, 1)

        def body(pe, seq, i, hb, last=False):
            count = len(pieces(i))
            more = len(pieces(i + 1)) if i + 1 < NB else 0
            for g in range(count):
                if g + 4 < count:
                    shifted_scores(pe, seq, i, hb, g + 4)
                elif not last:
                    if g + 4 == count:
                        pe.wait_ge(s.s_maxima_in_queries, after(BODIES * (seq * NB + i) + hb + 1))
                    shifted_scores(pe, seq, i, hb + 1, g + 4 - count)
                for a in range(more * min(g, 4) // 4, more * min(g + 1, 4) // 4):
                    maxima_scores(pe, seq, i + 1, hb, a)
                if last and more and count > 4 and g == count - 1:
                    transpose_maxima(pe, seq, i + 1)
                weigh(pe, seq, i, hb, g)
                if last and i and g == 1:
                    transpose_output(pe, seq * NB + i - 1)
            if last and more and count == 4:
                transpose_maxima(pe, seq, i + 1)

        def transpose_weighed(pe, T, i):
            pe.wait_ge(s.s_weighed_copied, after(H * T + H - 1))
            pe.wait_ge(s.s_output_copied, after(T - 1))
            for c in range(BODIES):
                mm = nc.tensor.transpose(ps[:, 7, c * P:(c + 1) * P], s.oc[:, i % 2, c * P:(c + 1) * P], m.ident[:, :])
            mm.then_inc(s.s_weighed_transposed, 1)

        def transpose_output(pe, T):
            pe.wait_ge(s.s_output_divided, after(T))
            nc.tensor.transpose(ps[:, 7, 0:P], s.y[:, :], m.ident[:, :]).then_inc(s.s_output_transposed, 1)

        def exp_body(act, seq, i, hb):
            for g, (hh, bl) in enumerate(pieces(i)):
                act.wait_ge(s.s_scores, after(number(seq, i, hb, g)))
                act.wait_ge(s.s_values_weighted, after(number(seq, i, hb, g) - 4))
                nc.scalar.activation(s.e[:, g % 4, 0:len(bl) * P], ps[:, 2 + g % 4, 0:len(bl) * P], ACT.Exp).then_inc(s.s_exp, 1)

        def copy_weighed(dve, seq, i, hb, hh):
            T = seq * NB + i
            dve.wait_ge(s.s_values_weighted, after(number(seq, i, hb, (hh + 1) * np_[i] - 1)))
            dve.wait_ge(s.s_weighed_transposed, after(T - 2))
            rows = slice(32 * hh, 32 * hh + s.VW)
            nc.vector.tensor_copy(s.oc[rows, i % 2, ds(hb * P, P)], ps[rows, 6, 0:P]).then_inc(s.s_weighed_copied, 1)

        def dve_body(dve, seq, i, hb, last=False):
            more = len(pieces(i + 1)) if i + 1 < NB else 0
            for g, (hh, bl) in enumerate(pieces(i)):
                for a in range(more * min(g, 4) // 4, more * min(g + 1, 4) // 4):
                    reduce_maxima(dve, seq, i + 1, hb, a)
                if last and more and g == len(pieces(i)) - 1:
                    finish_maxima(dve, seq, i + 1)
                if bl[-1] == i:
                    copy_weighed(dve, seq, i, hb, hh)

        def copy_output(act, T):
            act.wait_ge(s.s_output_transposed, after(T))
            m.settle(act)
            nc.scalar.activation(m.xb[:, ds(X0 + T * P, P)], ps[:, 7, 0:P], ACT.Copy).then_inc(s.s_output_copied, 1)

        def divide(dve, T):
            dve.wait_ge(s.s_weighed_transposed, after(T))
            ov = ps[:, 7, :].rearrange("p (h d) -> p h d", h=H)
            nc.vector.reciprocal(s.rden[:, :], ov[:, :, MLA_HD]).then_inc(s.s_reciprocals, 1)
            dve.wait_ge(s.s_reciprocals, after(T))
            dve.wait_ge(s.s_output_transposed, after(T - 1))
            nc.vector.tensor_tensor(s.y[:, :].rearrange("p (h d) -> p h d", d=MLA_HD), ov[:, :, 0:MLA_HD],
                                    s.rden[:, :].unsqueeze(2).to_broadcast([P, H, MLA_HD]), ALU.mult).then_inc(s.s_output_divided, 1)

        with nc.Block() as block:
            @block.sync
            def _(sp):
                def load(seq, hb):
                    heads = slice(hb * HB * MLA_HD, (hb + 1) * HB * MLA_HD)
                    for dst, a, parts in ((s.qs, 0, s.PART_Q), (s.ks, 1, s.PART_K)):
                        for slot, i in enumerate(parts):
                            sp.dma_start(dst[slot * MLA_HD:(slot + 1) * MLA_HD, hb * HB:(hb + 1) * HB, :],
                                         scratch[a][i, heads, ds(seq * SEQ, SEQ)].rearrange("(h d) t -> d h t", d=MLA_HD)).then_inc(s.s_heads_loaded[hb], 16)

                for hb in range(BODIES):
                    load(0, hb)
                with sp.Fori(1, SEQS) as seq:
                    for hb in range(BODIES):
                        sp.wait_ge(s.s_scores, after(number(seq - 1, NB - 1, hb + 1, -1)))
                        m.settle(sp)
                        load(seq, hb)

            @block.gpsimd
            def _(pool):
                pool.sem_inc(s.s_values_staged, LEAD)
                with pool.Fori(0, SEQS) as seq:
                    for i in range(NB):
                        for hb in range(BODIES):
                            for g, (hh, bl) in enumerate(pieces(i)):
                                pool.wait_ge(s.s_values_weighted, after(number(seq, i, hb, g) - 4))
                                m.settle(pool)
                                nc.gpsimd.tensor_copy(s.vs[:, g % 4, 0:len(bl), :],
                                                      s.v[:, ds(seq * TILES + bl[0], len(bl)), ds(hb * HB + hh, 1), :]
                                                      .rearrange("p t h d -> p t (h d)")).then_inc(s.s_values_staged, 1)

            @block.tensor
            def _(pe):
                for x in (s.s_maxima_scores, s.s_maxima_transposed, s.s_scores, s.s_values_weighted, s.s_weighed_transposed, s.s_output_transposed):
                    pe.sem_inc(x, LEAD)
                with pe.Fori(0, SEQS) as seq:
                    for hb in range(BODIES):
                        pe.wait_ge(s.s_heads_loaded[hb], 16 * 12 * (seq + 1))
                        for g in range(HB):
                            maxima_scores(pe, seq, 0, hb, g)
                    transpose_maxima(pe, seq, 0)
                    for i in range(NB):
                        T = seq * NB + i
                        pe.wait_ge(s.s_maxima_in_queries, after(BODIES * T))
                        for g in range(4):
                            shifted_scores(pe, seq, i, 0, g)
                        m.settle(pe)
                        for hb in range(BODIES - 1):
                            body(pe, seq, i, hb)
                        if i:
                            pe.wait_ge(s.s_maxima_in_queries, after(BODIES * T + BODIES - 1))
                            transpose_weighed(pe, T - 1, i - 1)
                        body(pe, seq, i, BODIES - 1, last=True)
                    transpose_weighed(pe, seq * NB + NB - 1, NB - 1)
                    transpose_output(pe, seq * NB + NB - 1)

            @block.scalar
            def _(act):
                act.preload_act_table(ACT.Exp)
                for x in (s.s_maxima_in_queries, s.s_exp, s.s_output_copied):
                    act.sem_inc(x, LEAD)
                with act.Fori(0, SEQS) as seq:
                    for i in range(NB):
                        write_shift(act, seq, i, 0)
                        for hb in range(BODIES - 1):
                            write_shift(act, seq, i, hb + 1)
                            exp_body(act, seq, i, hb)
                        exp_body(act, seq, i, BODIES - 1)
                        if i:
                            copy_output(act, seq * NB + i - 1)
                    copy_output(act, seq * NB + NB - 1)

            @block.vector
            def _(dve):
                for x in (s.s_piece_maxima, s.s_maxima_joined, s.s_maxima_negated, s.s_weighed_copied, s.s_reciprocals, s.s_output_divided):
                    dve.sem_inc(x, LEAD)
                with dve.Fori(0, SEQS) as seq:
                    with dve.Fori(0, BODIES) as hb:
                        for g in range(HB):
                            reduce_maxima(dve, seq, 0, hb, g)
                    finish_maxima(dve, seq, 0)
                    for i in range(NB):
                        T = seq * NB + i
                        dve.wait_ge(s.s_maxima_negated, after(T))
                        m.settle(dve)
                        for hb in range(BODIES - 1):
                            dve_body(dve, seq, i, hb)
                        if i:
                            divide(dve, T - 1)
                        dve_body(dve, seq, i, BODIES - 1, last=True)
                    divide(dve, seq * NB + NB - 1)
        m.phase_end()


class Gru:

    ROWS = 2 * DI

    def __init__(self, m):
        self.m = m
        sb, sem = m.sb, m.sem
        self.taps, top = m.carve(SCRATCH, [P, CONV, P])
        self.pwt, top = m.carve(top, [P, P])
        self.cols, top = m.carve(top, [P, 16])
        self.gain, top = m.carve(top, [P, 4])
        self.cbias, top = m.carve(top, [P, 1])
        self.w_hg, top = m.carve(top, [P, 4, self.ROWS])
        self.w_out, top = m.carve(top, [self.ROWS, 2, P])
        R = self.ROWS
        self.sg, at = m.carve(0, [R, 2, HALF])
        self.a, at = m.carve(at, [R, 2, HALF])
        self.sh, at = m.carve(at, [R, 2, HALF])
        self.g, at = m.carve(at, [R, 2, HALF])
        self.v, at = m.carve(at, [R, 2, HALF])
        self.h, at = m.carve(at, [R, 2, 2, HALF])
        self.s_loaded = sem("gru_loaded")
        self.s_bias_product = sem("gru_bias_product")
        self.s_convolved = sem("gru_convolved")
        self.s_added = sem("gru_added")
        self.s_gates_projected = sem("gru_gates_projected")
        self.s_sigmoid_gate = sem("gru_sigmoid_gate")
        self.s_coefficients = sem("gru_coefficients")
        self.s_sigmoid_hidden = sem("gru_sigmoid_hidden")
        self.s_hidden_floor = sem("gru_hidden_floor")
        self.s_hidden_value = sem("gru_hidden_value")
        self.s_values = sem("gru_values")
        self.s_states = sem("gru_states")
        self.s_states_projected = sem("gru_states_projected")

    def setup(self, t):
        nc, m, s = self.m.nc, self.m, self
        with nc.Block() as block:
            @block.sync
            def _(sp):
                for dst, name in ((s.pwt, "gru_pwT"), (s.cols[:, 0:9], "gru_cols"), (s.w_hg, "gru_hg"), (s.w_out, "gru_out")):
                    sp.dma_start(dst, t[name]).then_inc(s.s_loaded, 16)

            @block.vector
            def _(dve):
                dve.wait_ge(s.s_loaded, 64)
                for j in range(CONV):
                    nc.vector.tensor_scalar(s.taps[:, j, :], s.pwt[:, :], s.cols[:, j:j + 1], None, ALU.mult)
                nc.vector.tensor_scalar(s.gain[:, 0:3], s.cols[:, 6:9], 1.0, None, ALU.add)
                nc.vector.memset(m.hn[:, TOK:TOK + HALF], 0.0)
                dve.wait_ge(s.s_bias_product, 1)
                nc.vector.tensor_tensor(s.cbias[:, :], m.psum[:, 0, 0:1], s.cols[:, 5:6], ALU.add)

            @block.tensor
            def _(pe):
                pe.wait_ge(s.s_loaded, 64)
                nc.tensor.matmul(m.psum[:, 0, 0:1], s.pwt[:, :], s.cols[:, 4:5], start=True, stop=True).then_inc(s.s_bias_product, 1)
        m.phase_end()

    def conv(self):
        nc, m, s = self.m.nc, self.m, self
        with nc.Block() as block:
            @block.tensor
            def _(pe):
                pe.sem_inc(s.s_convolved, LEAD)
                with pe.Fori(0, SEQS) as seq:
                    for half in range(2):
                        n = 2 * seq + half
                        pe.wait_ge(s.s_added, after(n - 2))
                        for j in range(CONV - 1, -1, -1):
                            lag = CONV - 1 - j
                            at = seq * SEQ + half * HALF - lag
                            cut = lag if half == 0 else 0
                            mm = nc.tensor.matmul(m.psum[:, half, cut:HALF], s.taps[:, j, :], m.hn[:, ds(at + cut, HALF - cut)],
                                                  start=lag == 0, stop=True, skip_group_check=True)
                        mm.then_inc(s.s_convolved, 1)

            @block.vector
            def _(dve):
                dve.sem_inc(s.s_added, LEAD)
                with dve.Fori(0, SEQS) as seq:
                    for half in range(2):
                        n = 2 * seq + half
                        here = ds(X0 + seq * SEQ + half * HALF, HALF)
                        dve.wait_ge(s.s_convolved, after(n))
                        nc.vector.scalar_tensor_tensor(m.xb[:, here], m.psum[:, half, :], s.cbias[:, 0:1], m.xa[:, here],
                                                       ALU.add, ALU.add).then_inc(s.s_added, 1)
        m.phase_end()

    def recurrence(self):
        nc, m, s, R = self.m.nc, self.m, self, self.ROWS
        hid, gate, down = m.psum[0:R, 0:2, :], m.psum[0:R, 2:4, :], m.psum[:, 4:6, :]
        with nc.Block() as block:
            @block.tensor
            def _(pe):
                pe.sem_inc(s.s_gates_projected, LEAD)
                pe.sem_inc(s.s_states_projected, LEAD)

                def up(n, at):
                    pe.wait_ge(s.s_coefficients, after(n - 1))
                    for c in range(2):
                        nc.tensor.matmul(gate[:, c, :], s.w_hg[:, 2 + c, :], m.hn[:, at], start=True, stop=True)
                    pe.wait_ge(s.s_hidden_value, after(n - 1))
                    for c in range(2):
                        mm = nc.tensor.matmul(hid[:, c, :], s.w_hg[:, c, :], m.hn[:, at], start=True, stop=True)
                    mm.then_inc(s.s_gates_projected, 1)

                up(0, ds(0, HALF))
                with pe.Fori(0, SEQS) as seq:
                    for half in range(2):
                        n = 2 * seq + half
                        up(n + 1, ds((n + 1) * HALF, HALF))
                        pe.wait_ge(s.s_states, after(n))
                        pe.wait_ge(s.s_added, after(n - 2))
                        for c in range(2):
                            mm = nc.tensor.matmul(down[:, half, :], s.w_out[:, c, :], s.h[:, half, c, :], start=c == 0, stop=True, skip_group_check=True)
                        mm.then_inc(s.s_states_projected, 1)

            @block.scalar
            def _(act):
                act.preload_act_table(ACT.Sigmoid)
                for x in (s.s_sigmoid_gate, s.s_coefficients, s.s_sigmoid_hidden):
                    act.sem_inc(x, LEAD)
                with act.Fori(0, SEQS * 2) as n:
                    act.wait_ge(s.s_gates_projected, after(n))
                    act.wait_ge(s.s_hidden_floor, after(n - 1))
                    nc.scalar.activation(s.sh[:, :, :], hid, ACT.Sigmoid).then_inc(s.s_sigmoid_hidden, 1)
                    act.wait_ge(s.s_values, after(n - 1))
                    nc.scalar.activation(s.sg[:, :, :], gate, ACT.Sigmoid).then_inc(s.s_sigmoid_gate, 1)
                    act.wait_ge(s.s_states, after(n - 1))
                    nc.scalar.activation(s.a[:, :, :], gate, ACT.Sigmoid, scale=-1.0).then_inc(s.s_coefficients, 1)

            @block.vector
            def _(dve):
                for x in (s.s_hidden_floor, s.s_hidden_value, s.s_values, s.s_states, s.s_added):
                    dve.sem_inc(x, LEAD)

                def add(n, half):
                    dve.wait_ge(s.s_states_projected, after(n))
                    here = ds(X0 + n * HALF, HALF)
                    nc.vector.tensor_tensor(m.xa[:, here], down[:, half, :], m.xb[:, here], ALU.add).then_inc(s.s_added, 1)

                with dve.Fori(0, SEQS) as seq:
                    for half in range(2):
                        n = 2 * seq + half
                        dve.wait_ge(s.s_sigmoid_hidden, after(n))
                        dve.wait_ge(s.s_values, after(n - 1))
                        nc.vector.tensor_scalar(s.g[:, :, :], s.sh[:, :, :], 0.5, None, ALU.min).then_inc(s.s_hidden_floor, 1)
                        dve.wait_ge(s.s_hidden_floor, after(n))
                        nc.vector.scalar_tensor_tensor(s.v[:, :, :], hid, 0.0, s.g[:, :, :], ALU.max, ALU.add).then_inc(s.s_hidden_value, 1)
                        dve.wait_ge(s.s_hidden_value, after(n))
                        dve.wait_ge(s.s_sigmoid_gate, after(n))
                        nc.vector.tensor_tensor(s.g[:, :, :], s.v[:, :, :], s.sg[:, :, :], ALU.mult).then_inc(s.s_values, 1)
                        dve.wait_ge(s.s_values, after(n))
                        dve.wait_ge(s.s_coefficients, after(n))
                        dve.wait_ge(s.s_states_projected, after(n - 2))
                        dve.wait_ge(s.s_states, after(n - 1))
                        for c in range(2):
                            ins = nc.vector.tensor_tensor_scan(s.h[:, half, c, :], s.a[:, c, :], s.g[:, c, :],
                                                               0.0 if half == 0 else s.h[:, 0, c, HALF - 1:HALF], ALU.mult, ALU.add)
                        ins.then_inc(s.s_states, 1)
                        add(n, half)
        m.phase_end()


def shape_constants():
    f = np.float32
    eye = np.eye(P, dtype=f)
    center = eye - f(1.0 / P)
    upper = (np.arange(P) >= HD)[:, None]
    parts = [eye, center, np.where(upper, f(0), center), np.where(upper, center, f(0)), np.full((P, P), 1.0 / P, f)]
    out = {"squares": np.concatenate(parts, 1).astype(f)}
    i = np.arange(P)
    for name, c in LOCAL.items():
        W = c["window"]
        lag = i[:, None] - i[None, :]
        own = np.where((lag >= 0) & (lag <= W), 0, MASKED)
        prior = np.full((P, ROPE_TILES, HD), OFF)
        prior[0:W, :, 0:W] = np.where(i[:W, None] <= i[None, :W], 0, MASKED)[:, None, :]
        prior[:, [0, TILES]] = OFF
        out["masks_" + name] = np.concatenate([own, prior.reshape(P, -1)], 1).astype(f)
        half = np.arange(0, HD, 2, dtype=f)
        inv_freq = (f(1.0) / f(10000.0) ** (half / f(HD))).astype(f)
        t = np.arange(SEQ, dtype=f)
        freqs = t[:, None] * inv_freq[None, :]
        base = ((half + f(0.4 * HD)) / f(1.4 * HD)).astype(f)
        power = ((t - f(SEQ // 2)) / f(W // 2)).astype(f)
        scale = (base[None, :] ** power[:, None]).astype(f)
        cos, sin = np.cos(freqs).astype(f), np.sin(freqs).astype(f)
        tabs = []
        for s in (scale * f(8.0), f(1.0) / scale):
            tabs += [np.concatenate([cos * s, cos * s], 1), np.concatenate([-sin * s, sin * s], 1)]
        tab = np.stack(tabs).astype(f).reshape(4, TILES, P, HD).transpose(2, 0, 1, 3)
        out["rope_" + name] = np.ascontiguousarray(np.concatenate([tab, tab[:, :, 0:AHEAD]], 2))
    keep = np.ones((P, ROPE_TILES), f)
    keep[:, [0, TILES]] = 0
    out["keep"] = keep
    one = np.zeros((P, MLA_HEADS), f)
    one[Mla.SHIFT:Mla.SHIFT + MLA_HEADS] = np.eye(MLA_HEADS, dtype=f)
    out["onehot"] = one
    causal = np.where(i[:, None] >= i[None, :], 0, MASKED).astype(f)
    out["causal"] = np.concatenate([causal, causal.T], 1)
    return out


def ffn_vectors(gain, bias, b2, b1):
    import numpy as np
    L = gain.shape[0]
    v = np.zeros((L, P, 9), np.float32)
    v[:, :, 0], v[:, :, 1], v[:, :, 2] = gain, bias, b2
    for c in range(3):
        v[:, 0:HC[c], 3 + c] = b1[:, HO[c]:HO[c] + HC[c]]
        v[:, 0:HC[c], 6 + c] = b1[:, HID + HO[c]:HID + HO[c] + HC[c]]
    return v


def local_layout(d, pre, up):
    import numpy as np
    qk = np.stack([d[f"{pre}_ffn_q_scale"], d[f"{pre}_ffn_k_scale"]], 1)
    names = ("Wqkv", "Wo", "W1", "b1", "W2", "b2") if up else ("wqkv", "wo", "w1", "b1", "w2", "b2")
    wqkv, wo, w1, b1, w2, b2 = (d[f"{pre}_ffn_{n}"] for n in names)

    def again(w):
        return np.concatenate([w, w[:1]])

    return {
        f"{pre}_wqkv": again(wqkv), f"{pre}_wo": again(wo), f"{pre}_w1": w1, f"{pre}_w2": w2,
        f"{pre}_scale_qk": again(np.broadcast_to(qk[:, None], (len(qk), P, 2, HD))),
        f"{pre}_vec": ffn_vectors(d[f"{pre}_ffn_ln_g"], d[f"{pre}_ffn_ln_b"], b2, b1),
    }


def gru_layout(d):
    import numpy as np
    g = {k[len("L1_attn_"):]: v for k, v in d.items() if k.startswith("L1_attn_")}
    cols = np.concatenate([g["dw_w"][:, 0, :], np.stack([g["dw_b"], g["pw_b"], g["conv_gamma"], g["gru_gamma"], g["ff_gamma"]], 1)], 1)
    heads, hd = g["w_hg"].shape[0], g["w_hg"].shape[1]
    hg = np.zeros((P, 4, 2 * DI), np.float32)
    wo = np.zeros((2 * DI, 2, P), np.float32)
    for h in range(heads):
        pair, col = h // 2, (h % 2) * DI
        hg[h * hd:(h + 1) * hd, pair, col:col + DI] = g["w_hg"][h, :, 0:DI]
        hg[h * hd:(h + 1) * hd, 2 + pair, col:col + DI] = g["w_hg"][h, :, DI:]
        wo[col:col + DI, pair, h * hd:(h + 1) * hd] = g["w_out"][h]
    return {"gru_pwT": g["pw_w"].T, "gru_cols": cols, "gru_hg": hg, "gru_out": wo,
            "gru_w1": np.concatenate([g["w_value"], g["w_gate"]], 1), "gru_w2": g["w_ff_out"], "gru_vec": np.zeros((P, 9), np.float32)}


def build(nc, t, out, stages=("mla", "L0", "gru", "L1")):
    with ExitStack() as ctx:
        m = Machine(nc, ctx)
        norm, ffn, att, mla, gru = Norm(m), Ffn(m), Windowed(m), Mla(m), Gru(m)
        loaded = ctx.enter_context(nc.semaphore("loaded"))
        stored = ctx.enter_context(nc.semaphore("stored"))
        scratch = nc.dram_tensor("parts", (2, 3, P, TOK), BF16, kind="Internal").ap()
        mask_f = m.sb("mask_f", [P, 2 * P])
        zeroed = m.sem("zeroed")

        with nc.Block() as block:
            @block.sync
            def _(sp):
                n = 0
                for dst, src in [(m.ident, 0), (m.center, 1), (m.center_a, 2), (m.center_b, 3), (m.mean, 4)]:
                    sp.dma_start(dst[:, :], t["squares"][:, src * P:(src + 1) * P]).then_inc(loaded, 16)
                sp.dma_start(att.keep[:, :], t["keep"]).then_inc(loaded, 16)
                sp.dma_start(m.onehot[:, :], t["onehot"]).then_inc(loaded, 16)
                sp.dma_start(mask_f[:, 0:2 * P], t["causal"]).then_inc(loaded, 16)
                sp.dma_start(m.xa[:, X0:X0 + TOK], t["xT"]).then_inc(loaded, 16)
                sp.dma_start(m.xres[:, X0:X0 + TOK], t["xT"]).then_inc(loaded, 16)
                sp.wait_ge(loaded, 10 * 16)

            @block.vector
            def _(dve):
                nc.vector.memset(m.hn[:, :], 1.0)
                dve.wait_ge(loaded, 10 * 16)
                nc.vector.tensor_copy(m.ident_bf[:, :], m.ident[:, :])
                nc.vector.memset(m.xa[:, 0:X0], 0.0)
                nc.vector.memset(m.xa[:, X0 + TOK:X0 + TOK + PAD], 0.0)
                nc.vector.memset(m.xb[:, 0:X0], 0.0)
                nc.vector.tensor_copy(mla.causal[:, :], mask_f[:, 0:2 * P])
        m.phase_end()

        masks = P + ROPE_TILES * HD

        def family_arrays(pre):
            return t[pre + "_wqkv"], t[pre + "_wo"].rearrange("l (c p) n -> l p c n", p=P), t[pre + "_scale_qk"]

        def family_load(pre):
            def load(sp):
                sp.dma_start(att.rope[:, :, :, :], t["rope_" + pre]).then_inc(att.s_tables_loaded, 16)
                sp.dma_start(m.hn[:, 0:masks], t["masks_" + pre]).then_inc(att.s_tables_loaded, 16)
                att.load(sp, *(ap[0] for ap in family_arrays(pre)))
                sp.wait_ge(att.s_tables_loaded, 32)
            return load

        def windowed_family(pre):
            c = LOCAL[pre]
            G, L = c["groups"], c["layers"]

            def load(layer):
                return lambda sp: att.load(sp, *(ap[ds(layer, 1)][0] for ap in family_arrays(pre)))

            with nc.Block() as block:
                @block.scalar
                def _(act):
                    nc.scalar.activation(att.mask[:, :], m.hn[:, 0:P], ACT.Copy)
                    nc.scalar.activation(att.mask_p[:, :, :], m.hn[:, P:masks].rearrange("p (t d) -> p t d", d=HD), ACT.Copy)

                @block.vector
                def _(dve):
                    nc.vector.memset(att.kt[:, :, :, :, :], 0.0)
                    nc.vector.memset(att.v[:, :, :, :], 0.0)
                    nc.vector.memset(m.hn[:, TOK:TOK + HALF], 0.0)

                @block.gpsimd
                def _(pool):
                    att.scale_tables(pool)
            m.phase_end()
            with nc.Fori(0, L) as layer:
                att.phase(G, c["window"], sp_work=lambda sp: ffn.load(sp, *(t[pre + "_" + n][ds(layer, 1)][0] for n in ("w1", "w2", "vec"))))
                norm.phase("layer", terms=[(m.center_a, m.xb, False), (m.center_b, m.xb, True)], gain=ffn.vec[:, 0:1],
                           bias=ffn.vec[:, 1:2], out=m.hn)
                ffn.phase(m.xb, m.xa, ACT.Gelu, sp_work=load(layer + 1), pool_work=lambda pool: att.scale_tables(pool, loading=True))

        def outer_norm(sp_work=None):
            norm.phase("layer", terms=[(m.center, m.xres, False), (m.center, m.xa, False)], out=m.xa, out_at=X0, out2=m.xres, sp_work=sp_work)

        if "mla" in stages:
            mla.weights(t)
            mla.projections(scratch)
            mla.attention(scratch)
            norm.phase("layer", terms=[(m.center, m.xres, False), (m.center, m.xb, False)], out=m.xa, out_at=X0, out2=m.xres,
                       sp_work=family_load("L0"))
        if stages[0] in LOCAL:
            with nc.Block() as block:
                block.sync(family_load(stages[0]))
            m.phase_end()
        if "L0" in stages:
            windowed_family("L0")
            outer_norm()
        if "gru" in stages:
            gru.setup(t)
            with nc.Block() as block:
                @block.sync
                def _(sp):
                    ffn.load(sp, t["gru_w1"], t["gru_w2"], t["gru_vec"])
            m.phase_end()
            norm.phase("rms", src=m.xa, gain=gru.gain[:, 0:1], out=m.hn)
            gru.conv()
            norm.phase("rms", src=m.xb, gain=gru.gain[:, 1:2], out=m.hn)
            gru.recurrence()
            norm.phase("rms", src=m.xa, gain=gru.gain[:, 2:3], out=m.hn)
            ffn.phase(m.xa, m.xa, ACT.Silu)
            outer_norm(sp_work=family_load("L1"))
        if "L1" in stages:
            windowed_family("L1")
            outer_norm()

        with nc.Block() as block:
            @block.sync
            def _(sp):
                sp.dma_start(out, m.xa[:, X0:X0 + TOK]).then_inc(stored, 16)
                sp.wait_ge(stored, 16)


def host_arrays(d):
    import numpy as np
    d = {k: np.asarray(v) for k, v in d.items()}
    a = {"xT": d["L0_attn_x"].reshape(TOK, P).T}
    a.update(local_layout(d, "L0", True))
    a.update(local_layout(d, "L1", False))
    a.update(gru_layout(d))
    a.update({"mla_dq": d["L0_attn_W_dq"], "mla_uqT": d["L0_attn_W_uq"].T, "mla_dkv": d["L0_attn_W_dkv"],
              "mla_uk": d["L0_attn_W_uk"], "mla_uv": d["L0_attn_W_uv"], "mla_oT": d["L0_attn_W_o"].T})
    a.update(shape_constants())
    return {k: np.ascontiguousarray(v) for k, v in a.items()}


def kernel(**inputs):
    import concourse.bacc as bacc
    from concourse.bass_utils import run_bass_kernel_spmd

    nc = bacc.Bacc("TRN2", target_bir_lowering=False, num_devices=1)
    arrays = host_arrays(inputs)
    t = {k: nc.dram_tensor(f"in_{k}", v.shape, mybir.dt.from_np(v.dtype), kind="ExternalInput").ap() for k, v in arrays.items()}
    out = nc.dram_tensor("out_x", (P, TOK), F32, kind="ExternalOutput").ap()
    build(nc, t, out)
    r = run_bass_kernel_spmd(nc, [{f"in_{k}": v for k, v in arrays.items()}], core_ids=[0])
    return r.results[0]["out_x"].T.reshape(SEQS, SEQ, P)
```
